# Optimizing a Trainium2 kernel written in Bass

```python
import numpy as np
import jax
import jax.numpy as jnp

def _softmax(x, axis=-1):
    return jax.nn.softmax(x, axis=axis)

def _gelu(x):
    return jax.nn.gelu(x, approximate=True)

def _silu(x):
    return jax.nn.silu(x)

def _sigmoid(x):
    return jax.nn.sigmoid(x)

def _layernorm(x, axis=-1, eps=1e-05):
    m = jnp.mean(x, axis=axis, keepdims=True)
    v = jnp.var(x, axis=axis, keepdims=True)
    return (x - m) / jnp.sqrt(v + eps)

def _scatter_add(tgt, idx, src, axis=0):
    return tgt.at[idx].add(src)

def _segment_sum(src, seg, n):
    return jax.ops.segment_sum(src, seg, n)
kernel_name = 'mk_hybrid_d2_jaxref_r4_56f1ab'

def setup_inputs(seed: int=0):
    np.random.seed(seed)
    _w = jnp.asarray

    def _L0_attn_a_setup():
        import jax, jax.numpy as jnp
        import numpy as np
        D_MODEL = 256
        NUM_HEADS = 16
        HEAD_DIM = D_MODEL // NUM_HEADS
        ROPE_THETA = 10000.0

        def apply_rope(x):
            S, d_k = (x.shape[-2], x.shape[-1])
            inv_freq = ROPE_THETA ** (jnp.arange(0, d_k, 2, dtype=jnp.float32) / d_k)
            ang = jnp.arange(S, dtype=jnp.float32)[:, None] / inv_freq[None, :]
            cos, sin = (jnp.cos(ang), jnp.sin(ang))
            xp = x.reshape(x.shape[:-1] + (d_k // 2, 2))
            x0, x1 = (xp[..., 0], xp[..., 1])
            out = jnp.stack([x0 * cos - x1 * sin, x0 * sin + x1 * cos], axis=-1)
            return out.reshape(x.shape)
        key = jax.random.key(seed)
        k1, k2, k3 = jax.random.split(key, 3)
        B, S = (2, 512)
        std = 2.0 / (D_MODEL + 3 * D_MODEL)
        std_o = 2.0 / (D_MODEL + D_MODEL)
        return {'x': jax.random.normal(k1, (B, S, D_MODEL), dtype=jnp.float32), 'W_qkv': jax.random.normal(k2, (3 * D_MODEL, D_MODEL), dtype=jnp.float32) * std, 'W_o': jax.random.normal(k3, (D_MODEL, D_MODEL), dtype=jnp.float32) * std_o}
    _L0_attn_a_in = _L0_attn_a_setup()

    def _L0_attn_b_setup():
        import jax, jax.numpy as jnp
        import numpy as np
        D_MODEL = 256
        NUM_HEADS = 16
        B, S = (1, 1024)
        key = jax.random.key(seed)
        kx, kq, kk, kv, ko = jax.random.split(key, 5)
        std = (1.0 / D_MODEL) ** 0.5

        def trunc(k):
            return std * jax.random.truncated_normal(k, -3.0, 3.0, (D_MODEL, D_MODEL), dtype=jnp.float32)
        return {'x': jax.random.normal(kx, (B, S, D_MODEL), dtype=jnp.float32), 'W_Q': trunc(kq), 'W_K': trunc(kk), 'W_V': trunc(kv), 'W_O': trunc(ko)}
    _L0_attn_b_in = _L0_attn_b_setup()

    def _L0_ffn_setup():
        import jax, jax.numpy as jnp
        import numpy as np
        D_MODEL = 256
        EXPANSION = 4
        D_HIDDEN = D_MODEL * EXPANSION
        NUM_STAGES = int(np.log2(D_HIDDEN))

        def butterfly(y, weights, dim):
            lead = y.shape[:-1]
            for stage in range(weights.shape[0]):
                s = 2 ** stage
                nb = dim // (2 * s)
                yr = y.reshape(*lead, nb, 2, s)
                a = yr[..., 0, :]
                b = yr[..., 1, :]
                w = weights[stage].reshape(nb, s, 2, 2)
                na = w[..., 0, 0] * a + w[..., 0, 1] * b
                nb2 = w[..., 1, 0] * a + w[..., 1, 1] * b
                y = jnp.stack([na, nb2], axis=-2).reshape(*lead, dim)
            return y
        key = jax.random.key(seed)
        ks = jax.random.split(key, 6)
        B, S = (4, 512)
        x = jax.random.normal(ks[0], (B, S, D_MODEL), jnp.float32)
        W_exp = jax.random.normal(ks[1], (D_MODEL, D_HIDDEN), jnp.float32) * 0.02
        b_exp = jnp.zeros((D_HIDDEN,), jnp.float32)
        up_weights = jax.random.normal(ks[2], (NUM_STAGES, D_HIDDEN // 2, 2, 2), jnp.float32) * 0.02
        up_bias = jnp.zeros((D_HIDDEN,), jnp.float32)
        down_weights = jax.random.normal(ks[3], (NUM_STAGES, D_HIDDEN // 2, 2, 2), jnp.float32) * 0.02
        W_con = jax.random.normal(ks[4], (D_HIDDEN, D_MODEL), jnp.float32) * 0.02
        b_con = jnp.zeros((D_MODEL,), jnp.float32)
        down_bias = jnp.zeros((D_MODEL,), jnp.float32)
        return dict(x=x, W_exp=W_exp, b_exp=b_exp, up_weights=up_weights, up_bias=up_bias, down_weights=down_weights, W_con=W_con, b_con=b_con, down_bias=down_bias)
    _L0_ffn_in = _L0_ffn_setup()

    def _L1_attn_a_setup():
        import jax, jax.numpy as jnp
        import numpy as np
        B, N, D = (4, 1024, 256)
        H, DH = (16, 64)
        EPS = 1e-06
        key = jax.random.key(seed)
        ks = jax.random.split(key, 6)
        s = 1.0 / np.sqrt(D)
        return {'x': jax.random.normal(ks[0], (B, N, D), dtype=jnp.float32), 'Wq': jax.random.normal(ks[1], (D, H * DH), dtype=jnp.float32) * s, 'Wk': jax.random.normal(ks[2], (D, H * DH), dtype=jnp.float32) * s, 'Wv': jax.random.normal(ks[3], (D, H * DH), dtype=jnp.float32) * s, 'Wo': jax.random.normal(ks[4], (H * DH, D), dtype=jnp.float32) * s, 'bo': jnp.zeros((D,), dtype=jnp.float32)}
    _L1_attn_a_in = _L1_attn_a_setup()

    def _L1_attn_b_setup():
        import jax, jax.numpy as jnp
        import numpy as np
        D_MODEL = 256
        N_HEADS = 16
        D_LATENT = 64
        HEAD_DIM = D_MODEL // N_HEADS

        def apply_rope(x):
            B, T, H, D = x.shape
            inv_freq = 1.0 / 10000.0 ** (jnp.arange(0, D, 2, dtype=jnp.float32) / D)
            t = jnp.arange(T, dtype=jnp.float32)
            freqs = t[:, None] * inv_freq[None, :]
            sin_f = jnp.sin(freqs)[None, :, None, :]
            cos_f = jnp.cos(freqs)[None, :, None, :]
            x1, x2 = jnp.split(x, 2, axis=-1)
            return jnp.concatenate([x1 * cos_f - x2 * sin_f, x1 * sin_f + x2 * cos_f], axis=-1)
        key = jax.random.key(seed)
        ks = jax.random.split(key, 10)
        B, T = (4, 1024)
        s = lambda fan_in: 1.0 / np.sqrt(fan_in)
        return {'x': jax.random.normal(ks[0], (B, T, D_MODEL), dtype=jnp.float32), 'Wq': jax.random.normal(ks[1], (D_MODEL, D_MODEL), dtype=jnp.float32) * s(D_MODEL), 'bq': jnp.zeros((D_MODEL,), jnp.float32), 'Wdown': jax.random.normal(ks[2], (D_MODEL, D_LATENT), dtype=jnp.float32) * s(D_MODEL), 'bdown': jnp.zeros((D_LATENT,), jnp.float32), 'Wup': jax.random.normal(ks[3], (D_LATENT, 2 * D_MODEL), dtype=jnp.float32) * s(D_LATENT), 'bup': jnp.zeros((2 * D_MODEL,), jnp.float32), 'Wout': jax.random.normal(ks[4], (D_MODEL, D_MODEL), dtype=jnp.float32) * s(D_MODEL), 'bout': jnp.zeros((D_MODEL,), jnp.float32)}
    _L1_attn_b_in = _L1_attn_b_setup()

    def _L1_ffn_setup():
        import jax, jax.numpy as jnp
        import numpy as np
        DIM = 256
        HIDDEN = 768
        SCALE = 1.0 / 127.0

        def _dequant(w_int, dtype):
            return w_int.astype(dtype) * jnp.asarray(SCALE, dtype)
        key = jax.random.key(seed)
        k_x, k_g, k_u, k_d = jax.random.split(key, 4)
        x = jax.random.normal(k_x, (4, 512, DIM), dtype=jnp.float32)
        w_gate = jax.random.randint(k_g, (HIDDEN, DIM), -127, 128, dtype=jnp.int32)
        w_up = jax.random.randint(k_u, (HIDDEN, DIM), -127, 128, dtype=jnp.int32)
        w_down = jax.random.randint(k_d, (DIM, HIDDEN), -127, 128, dtype=jnp.int32)
        return {'x': x, 'w_gate': w_gate, 'w_up': w_up, 'w_down': w_down}
    _L1_ffn_in = _L1_ffn_setup()
    _d = {'L0_attn_a_x': _L0_attn_a_in['x'], 'L0_attn_a_W_qkv': _L0_attn_a_in['W_qkv'], 'L0_attn_a_W_o': _L0_attn_a_in['W_o'], 'L0_attn_b_W_Q': _L0_attn_b_in['W_Q'], 'L0_attn_b_W_K': _L0_attn_b_in['W_K'], 'L0_attn_b_W_V': _L0_attn_b_in['W_V'], 'L0_attn_b_W_O': _L0_attn_b_in['W_O'], 'L0_ffn_W_exp': _L0_ffn_in['W_exp'], 'L0_ffn_b_exp': _L0_ffn_in['b_exp'], 'L0_ffn_up_weights': _L0_ffn_in['up_weights'], 'L0_ffn_up_bias': _L0_ffn_in['up_bias'], 'L0_ffn_down_weights': _L0_ffn_in['down_weights'], 'L0_ffn_W_con': _L0_ffn_in['W_con'], 'L0_ffn_b_con': _L0_ffn_in['b_con'], 'L0_ffn_down_bias': _L0_ffn_in['down_bias'], 'L1_attn_a_Wq': _L1_attn_a_in['Wq'], 'L1_attn_a_Wk': _L1_attn_a_in['Wk'], 'L1_attn_a_Wv': _L1_attn_a_in['Wv'], 'L1_attn_a_Wo': _L1_attn_a_in['Wo'], 'L1_attn_a_bo': _L1_attn_a_in['bo'], 'L1_attn_b_Wq': _L1_attn_b_in['Wq'], 'L1_attn_b_bq': _L1_attn_b_in['bq'], 'L1_attn_b_Wdown': _L1_attn_b_in['Wdown'], 'L1_attn_b_bdown': _L1_attn_b_in['bdown'], 'L1_attn_b_Wup': _L1_attn_b_in['Wup'], 'L1_attn_b_bup': _L1_attn_b_in['bup'], 'L1_attn_b_Wout': _L1_attn_b_in['Wout'], 'L1_attn_b_bout': _L1_attn_b_in['bout'], 'L1_ffn_w_gate': _L1_ffn_in['w_gate'], 'L1_ffn_w_up': _L1_ffn_in['w_up'], 'L1_ffn_w_down': _L1_ffn_in['w_down']}
    _x0 = _d['L0_attn_a_x']
    _d['L0_attn_a_x'] = jax.random.normal(jax.random.fold_in(jax.random.key(seed), 1), (1, 4096, 256), dtype=_x0.dtype)
    del _x0
    return _d

def reference(L0_attn_a_x, L0_attn_a_W_qkv, L0_attn_a_W_o, L0_attn_b_W_Q, L0_attn_b_W_K, L0_attn_b_W_V, L0_attn_b_W_O, L0_ffn_W_exp, L0_ffn_b_exp, L0_ffn_up_weights, L0_ffn_up_bias, L0_ffn_down_weights, L0_ffn_W_con, L0_ffn_b_con, L0_ffn_down_bias, L1_attn_a_Wq, L1_attn_a_Wk, L1_attn_a_Wv, L1_attn_a_Wo, L1_attn_a_bo, L1_attn_b_Wq, L1_attn_b_bq, L1_attn_b_Wdown, L1_attn_b_bdown, L1_attn_b_Wup, L1_attn_b_bup, L1_attn_b_Wout, L1_attn_b_bout, L1_ffn_w_gate, L1_ffn_w_up, L1_ffn_w_down):

    def _L0_attn_a_ref(x, W_qkv, W_o):
        import jax, jax.numpy as jnp
        import numpy as np
        D_MODEL = 256
        NUM_HEADS = 16
        HEAD_DIM = D_MODEL // NUM_HEADS
        ROPE_THETA = 10000.0

        def apply_rope(x):
            S, d_k = (x.shape[-2], x.shape[-1])
            inv_freq = ROPE_THETA ** (jnp.arange(0, d_k, 2, dtype=jnp.float32) / d_k)
            ang = jnp.arange(S, dtype=jnp.float32)[:, None] / inv_freq[None, :]
            cos, sin = (jnp.cos(ang), jnp.sin(ang))
            xp = x.reshape(x.shape[:-1] + (d_k // 2, 2))
            x0, x1 = (xp[..., 0], xp[..., 1])
            out = jnp.stack([x0 * cos - x1 * sin, x0 * sin + x1 * cos], axis=-1)
            return out.reshape(x.shape)
        B, S, d_model = x.shape
        H, d_k = (NUM_HEADS, HEAD_DIM)
        qkv = jnp.einsum('bsi,oi->bso', x, W_qkv)
        Q, K, V = jnp.split(qkv, 3, axis=-1)

        def to_heads(t):
            return t.reshape(B, S, H, d_k).transpose(0, 2, 1, 3)
        Q, K, V = (to_heads(Q), to_heads(K), to_heads(V))
        Q, K = (apply_rope(Q), apply_rope(K))
        scores = jnp.einsum('bhqd,bhkd->bhqk', Q, K) / jnp.sqrt(jnp.float32(d_k))
        causal = jnp.tril(jnp.ones((S, S), dtype=bool))
        scores = jnp.where(causal, scores, -jnp.inf)
        attn = jax.nn.softmax(scores, axis=-1)
        out = jnp.einsum('bhqk,bhkd->bhqd', attn, V)
        out = out.transpose(0, 2, 1, 3).reshape(B, S, d_model)
        return jnp.einsum('bsi,oi->bso', out, W_o)

    def _L0_attn_b_ref(x, W_Q, W_K, W_V, W_O):
        import jax, jax.numpy as jnp
        import numpy as np
        D_MODEL = 256
        NUM_HEADS = 16
        B, S = (1, 1024)
        Bx, Sx, Dm = x.shape
        H = NUM_HEADS
        d_attn = Dm // H
        Q = x @ W_Q.T
        K = x @ W_K.T
        V = x @ W_V.T
        Q = Q.reshape(Bx, Sx, H, d_attn).transpose(0, 2, 1, 3)
        K = K.reshape(Bx, Sx, H, d_attn).transpose(0, 2, 1, 3)
        V = V.reshape(Bx, Sx, H, d_attn).transpose(0, 2, 1, 3)
        scale = 1.0 / jnp.sqrt(jnp.asarray(d_attn, dtype=x.dtype))
        attn = jnp.einsum('bhqd,bhkd->bhqk', Q, K) * scale
        causal = jnp.tril(jnp.ones((Sx, Sx), dtype=bool))
        attn = jnp.where(causal, attn, jnp.asarray(-jnp.inf, dtype=attn.dtype))
        probs = jax.nn.softmax(attn, axis=-1)
        y = jnp.einsum('bhqk,bhkd->bhqd', probs, V)
        y = y.transpose(0, 2, 1, 3).reshape(Bx, Sx, Dm)
        return y @ W_O.T

    def _L0_ffn_ref(x, W_exp, b_exp, up_weights, up_bias, down_weights, W_con, b_con, down_bias):
        import jax, jax.numpy as jnp
        import numpy as np
        D_MODEL = 256
        EXPANSION = 4
        D_HIDDEN = D_MODEL * EXPANSION
        NUM_STAGES = int(np.log2(D_HIDDEN))

        def butterfly(y, weights, dim):
            lead = y.shape[:-1]
            for stage in range(weights.shape[0]):
                s = 2 ** stage
                nb = dim // (2 * s)
                yr = y.reshape(*lead, nb, 2, s)
                a = yr[..., 0, :]
                b = yr[..., 1, :]
                w = weights[stage].reshape(nb, s, 2, 2)
                na = w[..., 0, 0] * a + w[..., 0, 1] * b
                nb2 = w[..., 1, 0] * a + w[..., 1, 1] * b
                y = jnp.stack([na, nb2], axis=-2).reshape(*lead, dim)
            return y
        h = jnp.einsum('bsd,dh->bsh', x, W_exp) + b_exp
        h = butterfly(h, up_weights, D_HIDDEN)
        h = jax.nn.gelu(h + up_bias, approximate=False)
        h = butterfly(h, down_weights, D_HIDDEN)
        y = jnp.einsum('bsh,hd->bsd', h, W_con) + b_con
        return y + down_bias

    def _L1_attn_a_ref(x, Wq, Wk, Wv, Wo, bo):
        import jax, jax.numpy as jnp
        import numpy as np
        B, N, D = (4, 1024, 256)
        H, DH = (16, 64)
        EPS = 1e-06

        def split_heads(t):
            b, n, _ = t.shape
            return t.reshape(b, n, H, DH).transpose(0, 2, 1, 3)
        q = split_heads(x @ Wq)
        k = split_heads(x @ Wk)
        v = split_heads(x @ Wv)
        q = jax.nn.elu(q) + 1.0
        k = jax.nn.elu(k) + 1.0
        k_sum = k.sum(axis=2)
        z = jnp.einsum('bhnd,bhd->bhn', q, k_sum)[..., None] + EPS
        kv = jnp.einsum('bhnd,bhne->bhde', k, v)
        out = jnp.einsum('bhnd,bhde->bhne', q, kv) / z
        out = out.transpose(0, 2, 1, 3).reshape(x.shape[0], x.shape[1], H * DH)
        return out @ Wo + bo

    def _L1_attn_b_ref(x, Wq, bq, Wdown, bdown, Wup, bup, Wout, bout):
        import jax, jax.numpy as jnp
        import numpy as np
        D_MODEL = 256
        N_HEADS = 16
        D_LATENT = 64
        HEAD_DIM = D_MODEL // N_HEADS

        def apply_rope(x):
            B, T, H, D = x.shape
            inv_freq = 1.0 / 10000.0 ** (jnp.arange(0, D, 2, dtype=jnp.float32) / D)
            t = jnp.arange(T, dtype=jnp.float32)
            freqs = t[:, None] * inv_freq[None, :]
            sin_f = jnp.sin(freqs)[None, :, None, :]
            cos_f = jnp.cos(freqs)[None, :, None, :]
            x1, x2 = jnp.split(x, 2, axis=-1)
            return jnp.concatenate([x1 * cos_f - x2 * sin_f, x1 * sin_f + x2 * cos_f], axis=-1)
        B, T, D = x.shape
        H, Dh = (N_HEADS, HEAD_DIM)
        q = x @ Wq + bq
        kv_latent = x @ Wdown + bdown
        kv = kv_latent @ Wup + bup
        q = q.reshape(B, T, H, Dh)
        kv = kv.reshape(B, T, H, 2 * Dh)
        k, v = jnp.split(kv, 2, axis=-1)
        q = apply_rope(q)
        k = apply_rope(k)
        att = jnp.einsum('bthd,btgd->bthg', q, k) / jnp.sqrt(jnp.float32(Dh))
        att = jax.nn.softmax(att, axis=-1)
        out = jnp.einsum('bthg,btgd->bthd', att, v)
        out = out.reshape(B, T, D)
        return out @ Wout + bout

    def _L1_ffn_ref(x, w_gate, w_up, w_down):
        import jax, jax.numpy as jnp
        import numpy as np
        DIM = 256
        HIDDEN = 768
        SCALE = 1.0 / 127.0

        def _dequant(w_int, dtype):
            return w_int.astype(dtype) * jnp.asarray(SCALE, dtype)
        wg = _dequant(w_gate, x.dtype)
        wu = _dequant(w_up, x.dtype)
        wd = _dequant(w_down, x.dtype)
        gate = jnp.einsum('bsd,hd->bsh', x, wg)
        up = jnp.einsum('bsd,hd->bsh', x, wu)
        h = jax.nn.silu(gate) * up
        return jnp.einsum('bsh,dh->bsd', h, wd)
    x = L0_attn_a_x
    x = x + _L0_attn_a_ref(_layernorm(x, axis=-1), L0_attn_a_W_qkv, L0_attn_a_W_o)
    x = x + _L0_ffn_ref(_layernorm(x, axis=-1), L0_ffn_W_exp, L0_ffn_b_exp, L0_ffn_up_weights, L0_ffn_up_bias, L0_ffn_down_weights, L0_ffn_W_con, L0_ffn_b_con, L0_ffn_down_bias)
    x = x + _L0_attn_b_ref(_layernorm(x, axis=-1), L0_attn_b_W_Q, L0_attn_b_W_K, L0_attn_b_W_V, L0_attn_b_W_O)
    x = x + _L0_ffn_ref(_layernorm(x, axis=-1), L0_ffn_W_exp, L0_ffn_b_exp, L0_ffn_up_weights, L0_ffn_up_bias, L0_ffn_down_weights, L0_ffn_W_con, L0_ffn_b_con, L0_ffn_down_bias)
    x = x + _L1_attn_a_ref(_layernorm(x, axis=-1), L1_attn_a_Wq, L1_attn_a_Wk, L1_attn_a_Wv, L1_attn_a_Wo, L1_attn_a_bo)
    x = x + _L1_ffn_ref(_layernorm(x, axis=-1), L1_ffn_w_gate, L1_ffn_w_up, L1_ffn_w_down)
    x = x + _L1_attn_b_ref(_layernorm(x, axis=-1), L1_attn_b_Wq, L1_attn_b_bq, L1_attn_b_Wdown, L1_attn_b_bdown, L1_attn_b_Wup, L1_attn_b_bup, L1_attn_b_Wout, L1_attn_b_bout)
    x = x + _L1_ffn_ref(_layernorm(x, axis=-1), L1_ffn_w_gate, L1_ffn_w_up, L1_ffn_w_down)
    return x

_drawn_inputs = setup_inputs


def setup_inputs(seed=0):
    import zlib

    import numpy as np

    out = dict(_drawn_inputs(seed))
    spreads = {'L0_ffn_b_exp': (0.0, 0.1),
     'L0_ffn_up_bias': (0.0, 0.1),
     'L0_ffn_b_con': (0.0, 0.1),
     'L0_ffn_down_bias': (0.0, 0.1),
     'L1_attn_a_bo': (0.0, 0.1),
     'L1_attn_b_bq': (0.0, 0.8),
     'L1_attn_b_bdown': (0.0, 0.8),
     'L1_attn_b_bup': (0.0, 0.8),
     'L1_attn_b_bout': (0.0, 0.8)}
    factors = {'L0_attn_a_W_qkv': 8.0,
     'L0_attn_a_W_o': 8.0,
     'L1_attn_a_Wq': 5.707,
     'L1_attn_a_Wk': 3.257,
     'L1_attn_b_Wq': 8.0,
     'L1_attn_b_Wdown': 8.0,
     'L1_attn_b_Wup': 8.0,
     'L1_attn_b_Wout': 8.0}
    for name, (base, spread) in spreads.items():
        noise = np.random.default_rng([zlib.crc32(name.encode()), seed]).standard_normal(out[name].shape)
        drawn = base * np.exp(spread * noise) if base else spread * noise
        out[name] = jnp.asarray(drawn.astype(out[name].dtype))
    for name, factor in factors.items():
        out[name] = (out[name] * factor).astype(out[name].dtype)
    return out
```

```python
from contextlib import ExitStack

import concourse.bass as bass
from concourse import mybir

F32 = mybir.dt.float32
BF16 = mybir.dt.bfloat16
I32 = mybir.dt.int32
ACT = mybir.ActivationFunctionType
ALU = mybir.AluOpType
AX = mybir.AxisListType

P = 128
BANK = 512
S = 4096
D = 256
DK = D // P
H = 16
HD = D // H
TILES = S // P
CHUNK = 512
TPC = CHUNK // P
CHUNKS = S // CHUNK
PARTS = 3
ROWS = 6 * HD
VW = 32
MASKED = -1.0e30
LN_EPS = 1e-5
DMA = 16




class Head:

    def __init__(self, turn, r):
        self.turn, self.r = turn, r

    def at(self, per_head, c):
        return self.turn * (3 * per_head) + (self.r * per_head + c)

    def past(self, per_head, c):
        return self.at(per_head, c + 1)

    def filled(self, per_load):
        return self.turn * per_load + (self.r // 3 + 1) * per_load

    def next(self, by):
        return Head(self.turn, self.r + by)

    @property
    def index(self):
        return self.turn * 3 + self.r

    @property
    def slot(self):
        return self.r % 3


def each_head(eng, body, turns, rest):
    with eng.Fori(0, turns) as turn:
        for r in range(3):
            body(Head(turn, r), False)
    for r in range(rest):
        body(Head(turns, r), r == rest - 1)


def begin_at_one(sp, *semaphores):
    for s in semaphores:
        sp.sem_inc(s, 1)


def first_pass_jobs():
    jobs = []
    for qt in range(TILES):
        keys = (qt + 1) * P
        for n, k0 in enumerate(range(0, keys, 2 * BANK)):
            width = min(2 * BANK, keys - k0)
            last = k0 + width == keys
            jobs.append((qt, k0, width, qt * P - k0 if last else None, n))
    return jobs


def second_pass_groups():
    groups = []
    for s in range(2):
        for kt in range((s + 1) * TILES // 2):
            tiles = []
            for c in range(4):
                q0 = (4 * s + c) * BANK
                if kt * P < q0 + BANK:
                    tiles.append((kt, c, max(0, kt * P - q0), kt * P >= q0))
            groups.append((s, tiles))
    return groups


def attention(nc, sem, tag, q_parts, k_parts, v_cols_dram, heads_out, consts, beside=None):
    ident_bf, ident_f, mask_first, mask_second = consts
    jobs = first_pass_jobs()
    groups = second_pass_groups()
    J = len(jobs) + 1
    T = sum(len(tiles) for _, tiles in groups)
    upto = [sum(len(tiles) for _, tiles in groups[:g + 1]) for g in range(len(groups))]
    ends = [g + 1 == len(groups) or groups[g + 1][0] != groups[g][0] for g in range(len(groups))]
    work = [sum(job[2] for job in jobs[:j + 1]) for j in range(len(jobs))]
    job_end = [sum(w <= work[-1] * min(1.0, upto[g] / T / 0.93) for w in work) for g in range(len(groups))]
    NS, NE = 3, 8
    LOADED = 7 * DMA

    with ExitStack() as ctx:
        def sb(name, shape, dt):
            return ctx.enter_context(nc.sbuf_tensor(f"{tag}_{name}", shape, dt))

        def ps(name, shape):
            return ctx.enter_context(nc.psum_tensor(f"{tag}_{name}", shape, F32))

        q_rows = sb("q_rows", [P, 3, S], BF16)
        k_rows = sb("k_rows", [P, 3, S], BF16)
        v_cols = sb("v_cols", [P, 3, TILES, VW], F32)
        exps = sb("exps", [P, NE, BANK], F32)
        out_t = sb("out_t", [P, 2, BANK], F32)
        piece_max = sb("piece_max", [P, TILES, 4], F32)
        neg_max = sb("neg_max", [P, TILES], F32)
        shift_hi = sb("shift_hi", [TILES, P], BF16)
        shift_lo = sb("shift_lo", [TILES, P], BF16)
        first_ps = ps("first_ps", [P, 2, 2 * BANK])
        second_ps = ps("second_ps", [P, NS, BANK])
        acc_ps = ps("acc_ps", [P, BANK])

        loaded = [sem(f"{tag}_loaded{i}") for i in range(3)]
        constants_set = sem(f"{tag}_constants_set")
        first_ready = sem(f"{tag}_first_ready")
        first_read = sem(f"{tag}_first_read")
        max_ready = sem(f"{tag}_max_ready")
        hi_ready = sem(f"{tag}_hi_ready")
        shift_stored = sem(f"{tag}_shift_stored")
        second_ready = sem(f"{tag}_second_ready")
        exp_ready = sem(f"{tag}_exp_ready")
        pv_done = sem(f"{tag}_pv_done")
        acc_read = sem(f"{tag}_acc_read")
        out_stored = [sem(f"{tag}_out_stored{i}") for i in range(2)]

        block = ctx.enter_context(nc.Block())

        @block.sync
        def _(sp):
            def load(h):
                q, k, n, full = q_rows[:, h.slot, :], k_rows[:, h.slot, :], h.index, loaded[h.slot]
                sp.dma_start(q[0:3 * HD], q_parts[n]).then_inc(full, DMA)
                sp.dma_start(k[0:3 * HD], k_parts[n][0].partition_broadcast(3)).then_inc(full, DMA)
                sp.dma_start(q[3 * HD:5 * HD], q_parts[n][0:2]).then_inc(full, DMA)
                sp.dma_start(k[3 * HD:5 * HD], k_parts[n][1].partition_broadcast(2)).then_inc(full, DMA)
                sp.dma_start(q[5 * HD:6 * HD], q_parts[n][0]).then_inc(full, DMA)
                sp.dma_start(k[5 * HD:6 * HD], k_parts[n][2]).then_inc(full, DMA)
                sp.dma_start(v_cols[:, h.slot], v_cols_dram[n]).then_inc(full, DMA)

            def store_shift(h):
                sp.wait_ge(first_read, h.past(J, J))
                for row, part in ((ROWS, shift_hi), (ROWS + 1, shift_lo)):
                    sp.dma_start(q_rows[row:row + 1, h.slot, :].rearrange("o (t q) -> o t q", t=TILES),
                                 part[:, :]).then_inc(shift_stored, DMA)

            def store_out(h, s):
                sp.wait_ge(acc_read, h.past(2, s + 1))
                for c in range(4):
                    q0 = (4 * s + c) * BANK
                    sp.dma_start(heads_out[h.index][:, q0:q0 + BANK],
                                 out_t[32 * c:32 * c + HD + 1, s, :]).then_inc(out_stored[s], DMA)

            def step(h, loads, last):
                if loads:
                    sp.wait_ge(pv_done, h.at(T, NE))
                    load(h.next(2))
                store_out(h, 0)
                if not last:
                    store_shift(h.next(1))
                store_out(h, 1)

            begin_at_one(sp, first_read, acc_read, shift_stored, *out_stored)
            load(Head(0, 0))
            load(Head(0, 1))
            store_shift(Head(0, 0))
            with sp.Fori(0, 4) as turn:
                for r in range(3):
                    step(Head(turn, r), True, False)
            for r in range(4):
                step(Head(4, r), 12 + r + 2 < H, 12 + r + 1 == H)
            for s in range(2):
                sp.wait_ge(out_stored[s], 1 + H * 4 * DMA)

        @block.gpsimd
        def _(pool):
            for slot in range(3):
                pool.memset(k_rows[ROWS:ROWS + 2, slot, :], 1.0).then_inc(constants_set, 1)
            pool.wait_ge(constants_set, 3)
            pool.memset(piece_max[:, :, :], -3.0e38).then_inc(constants_set, 1)
            pool.wait_ge(constants_set, 4)
            if beside:
                beside(pool)

        @block.tensor
        def _(pe):
            def first_job(h, j):
                qt, k0, width, diagonal, _ = jobs[j]
                pe.wait_ge(first_read, h.past(J, max(0, j - 1)))
                for b in range(0, width, BANK):
                    n = min(BANK, width - b)
                    masked = diagonal is not None and b <= diagonal < b + n
                    done = pe.matmul(first_ps[:, j % 2, b:b + n], q_rows[0:ROWS, h.slot, qt * P:(qt + 1) * P],
                                     k_rows[0:ROWS, h.slot, k0 + b:k0 + b + n], start=True, stop=not masked)
                    if masked:
                        done = pe.matmul(first_ps[:, j % 2, diagonal:diagonal + P], ident_bf[:, :], mask_first[:, :],
                                         start=False, stop=True)
                done.then_inc(first_ready, 1)

            def turn_maxima(h):
                pe.wait_ge(max_ready, h.at(1, 1))
                pe.transpose(first_ps[0:TILES, 0, 0:P], neg_max[:, :], ident_f[:, :]).then_inc(first_ready, 1)

            def scores(h, t, tile):
                kt, c, start, masked = tile[1]
                q0 = (4 * tile[0] + c) * BANK
                slot = (h.r * T + t) % NS
                pe.wait_ge(exp_ready, h.at(T, t + 1))
                done = pe.matmul(second_ps[:, slot, start:BANK], k_rows[0:ROWS + 2, h.slot, kt * P:(kt + 1) * P],
                                 q_rows[0:ROWS + 2, h.slot, q0 + start:q0 + BANK], start=True, stop=not masked)
                if masked:
                    done = pe.matmul(second_ps[:, slot, start:start + P], ident_bf[:, :], mask_second[:, :],
                                     start=False, stop=True)
                done.then_inc(second_ready, 1)

            def times_v(h, g):
                s, tiles = groups[g]
                if tiles[0][0] == 0:
                    pe.wait_ge(acc_read, h.past(2, s))
                for i, (kt, c, start, _) in enumerate(tiles):
                    t = upto[g] - len(tiles) + i
                    final = kt == 4 * (4 * s + c) + 3
                    pe.wait_ge(exp_ready, h.at(T, NS + t + 1))
                    pe.matmul(acc_ps[32 * c:32 * c + VW, start:BANK], v_cols[:, h.slot, kt, :],
                              exps[:, t % NE, start:BANK], start=kt == 0, stop=final,
                              tile_position=(0, 32 * c)).then_inc(pv_done, 1)

            def step(h, second, first):
                n = h.next(1) if second else h
                if second:
                    pe.wait_ge(shift_stored, h.past(2 * DMA, 2 * DMA))
                if first:
                    pe.wait_ge(loaded[n.slot], n.filled(LOADED))
                if not second:
                    for j in range(len(jobs)):
                        first_job(n, j)
                    turn_maxima(n)
                    return
                j, turned = 0, not first
                for g, (s, tiles) in enumerate(groups):
                    t0 = upto[g] - len(tiles)
                    if first and not turned and j == len(jobs):
                        turn_maxima(n)
                        turned = True
                    for i, tile in enumerate(tiles):
                        if i == 2 and first and j < job_end[g]:
                            first_job(n, j)
                            j += 1
                        scores(h, t0 + i, (s, tile))
                    while first and j < job_end[g]:
                        first_job(n, j)
                        j += 1
                    if g:
                        times_v(h, g - 1)
                times_v(h, len(groups) - 1)

            pe.wait_ge(constants_set, 4)
            step(Head(0, 0), False, True)
            each_head(pe, lambda h, last: step(h, True, not last), 5, 1)

        @block.scalar
        def _(act):
            def step(h, _):
                waiting = None
                for g, (s, tiles) in enumerate(groups):
                    for i, (_, _, start, _) in enumerate(tiles):
                        t = upto[g] - len(tiles) + i
                        act.wait_ge(second_ready, h.at(T, t + 1))
                        act.wait_ge(pv_done, h.at(T, t + 1))
                        nc.scalar.activation(exps[:, t % NE, start:BANK], second_ps[:, (h.r * T + t) % NS, start:BANK],
                                             ACT.Exp, scale=HD ** -0.5).then_inc(exp_ready, 1)
                    if waiting is not None:
                        copy_out(h, waiting)
                        waiting = None
                    if ends[g]:
                        waiting = g
                copy_out(h, waiting)

            def copy_out(h, g):
                s = groups[g][0]
                act.wait_ge(out_stored[s], h.past(4 * DMA, 0))
                act.wait_ge(pv_done, h.at(T, NE + upto[g]))
                nc.scalar.copy(out_t[:, s, :], acc_ps[:, :]).then_inc(acc_read, 1)

            act.sem_inc(exp_ready, NS)
            act.sem_inc(pv_done, NE)
            each_head(act, step, 5, 1)

        @block.vector
        def _(dve):
            def step(h, _):
                for j, (qt, _, width, _, piece) in enumerate(jobs):
                    dve.wait_ge(first_ready, h.at(J, j + 1))
                    nc.vector.reduce_max(piece_max[:, qt, piece:piece + 1], first_ps[:, j % 2, 0:width],
                                         AX.X).then_inc(first_read, 1)
                dve.wait_ge(first_read, h.past(J, J - 1))
                nc.vector.tensor_reduce(neg_max[:, :], piece_max[:, :, :], AX.X, ALU.max,
                                        negate=True).then_inc(max_ready, 1)
                dve.wait_ge(first_ready, h.at(J, J))
                dve.wait_ge(shift_stored, h.past(2 * DMA, 0))
                nc.vector.tensor_copy(shift_hi[:, :], first_ps[0:TILES, 0, 0:P]).then_inc(hi_ready, 1)
                dve.wait_ge(hi_ready, h.at(1, 1))
                nc.vector.tensor_tensor(shift_lo[:, :], first_ps[0:TILES, 0, 0:P], shift_hi[:, :],
                                        ALU.subtract).then_inc(first_read, 1)

            dve.wait_ge(constants_set, 4)
            each_head(dve, step, 5, 1)


def set_constants(nc, sem, consts):
    ident_bf, ident_f, mask_first, mask_second = consts
    made = sem("const_made")
    with nc.Block() as block:
        @block.gpsimd
        def _(pool):
            for n, (t, compare, fill, step, channel) in enumerate((
                    (ident_bf, ALU.not_equal, 1.0, -1, 1), (ident_f, ALU.not_equal, 1.0, -1, 1),
                    (mask_first, ALU.is_ge, MASKED, -1, 1), (mask_second, ALU.is_ge, MASKED, 1, -1))):
                pool.memset(t[:, :], 0.0).then_inc(made, 1)
                pool.wait_ge(made, 2 * n + 1)
                pool.affine_select(out=t[:, :], in_=t[:, :], compare_op=compare, fill=fill, base=0,
                                   pattern=[[step, P]], channel_multiplier=channel).then_inc(made, 1)
                pool.wait_ge(made, 2 * n + 2)




class Chunk:

    def __init__(self, turn, parity):
        self.turn, self.r = turn, parity

    def at(self, per_chunk, c):
        return self.turn * (2 * per_chunk) + (self.r * per_chunk + c)

    def past(self, per_chunk, c):
        return self.at(per_chunk, c + 1)

    def next(self):
        return Chunk(self.turn, self.r + 1)

    @property
    def index(self):
        return self.turn * 2 + self.r

    @property
    def parity(self):
        return self.r % 2


def each_chunk(eng, ahead, work):
    ahead(Chunk(0, 0))
    with eng.Fori(0, CHUNKS // 2 - 1) as turn:
        for r in range(2):
            n = Chunk(turn, r)
            work(n, lambda n=n: ahead(n.next()))
    n = Chunk(CHUNKS // 2 - 1, 0)
    work(n, lambda: ahead(n.next()))
    work(n.next(), lambda: None)


def two_ahead(eng, load, work):
    load(Chunk(0, 0))
    load(Chunk(0, 1))
    with eng.Fori(0, CHUNKS // 2 - 1) as turn:
        for r in range(2):
            work(Chunk(turn, r), lambda n=Chunk(turn, r + 2): load(n))
    for r in range(2):
        work(Chunk(CHUNKS // 2 - 1, r), nothing)


def nothing(*_):
    pass


class Stage:

    def __init__(self, nc, sem, ctx, tag):
        self.nc, self.ctx, self.tag, self.new_sem = nc, ctx, tag, sem

    def sb(self, name, shape, dt=F32):
        return self.ctx.enter_context(self.nc.sbuf_tensor(f"{self.tag}_{name}", shape, dt))

    def ps(self, name, shape):
        return self.ctx.enter_context(self.nc.psum_tensor(f"{self.tag}_{name}", shape, F32))

    def sem(self, name):
        return self.new_sem(f"{self.tag}_{name}")


def by_chunk(x):
    return x.rearrange("(n t p) d -> n p t d", t=TPC, p=P)


class Normed:

    def __init__(self, st, x, ident):
        self.st, self.nc, self.x, self.ident = st, st.nc, by_chunk(x), ident
        self.raw = st.sb("raw", [P, 2, TPC, D])
        self.normed = st.sb("normed", [P, TPC, D])
        self.stats = st.sb("stats", [P, TPC, 6])
        self.moments = st.sb("moments", [P, TPC, 2])
        self.variance = st.sb("variance", [P, TPC])
        self.inverse = st.sb("inverse", [P, TPC])
        self.power_of = st.sb("power_of", [P, TPC])
        self.xt = st.sb("xt", [P, 2, DK, CHUNK])
        self.turned_ps = st.ps("turned_ps", [P, DK, CHUNK])
        self.x_loaded = [st.sem("x_loaded0"), st.sem("x_loaded1")]
        self.stats_ready = st.sem("stats_ready")
        self.passed = st.sem("passed")
        self.moments_ready = st.sem("moments_ready")
        self.variance_ready = st.sem("variance_ready")
        self.inverse_ready = st.sem("inverse_ready")
        self.normed_ready = st.sem("normed_ready")
        self.turned_ready = st.sem("turned_ready")
        self.xt_ready = st.sem("xt_ready")
        self.from_one = (self.normed_ready, self.turned_ready, self.xt_ready)

    def load(self, sp, n):
        sp.dma_start(self.raw[:, n.parity], self.x[n.index]).then_inc(self.x_loaded[n.parity], DMA)

    def start_power(self, pool):
        pool.memset(self.power_of[:, :], -0.5).then_inc(self.inverse_ready, 1)
        pool.wait_ge(self.inverse_ready, 1)

    def power(self, pool, n):
        pool.wait_ge(self.variance_ready, n.at(1, 1))
        pool.tensor_tensor(self.inverse[:, :], self.variance[:, :], self.power_of[:, :],
                           ALU.pow).then_inc(self.inverse_ready, 1)

    def normalise(self, dve, n):
        raw = self.raw[:, n.parity]
        dve.wait_ge(self.x_loaded[n.parity], n.turn * DMA + (n.r // 2 + 1) * DMA)
        for t in range(TPC):
            self.nc.vector.bn_stats(self.stats[:, t, :], raw[:, t, :]).then_inc(self.stats_ready, 1)
        dve.wait_ge(self.stats_ready, n.at(TPC, TPC))
        dve.sem_inc(self.passed, 1)
        for t in range(TPC):
            self.nc.vector.bn_aggr(self.moments[:, t, :], self.stats[:, t, :]).then_inc(self.moments_ready, 1)
        dve.wait_ge(self.moments_ready, n.at(TPC, TPC))
        self.nc.vector.tensor_scalar(self.variance[:, :], self.moments[:, :, 1], LN_EPS, None,
                                     ALU.add).then_inc(self.variance_ready, 1)
        dve.wait_ge(self.inverse_ready, n.at(1, 2))
        dve.wait_ge(self.turned_ready, n.past(DK, 0))
        for t in range(TPC):
            self.nc.vector.tensor_scalar(self.normed[:, t, :], raw[:, t, :], self.moments[:, t, 0:1],
                                         self.inverse[:, t:t + 1], ALU.subtract, ALU.mult).then_inc(self.normed_ready, 1)

    def turn(self, pe, n):
        pe.wait_ge(self.normed_ready, n.past(TPC, TPC))
        pe.wait_ge(self.xt_ready, n.past(DK, 0))
        for k in range(DK):
            for t in range(TPC):
                done = pe.transpose(self.turned_ps[:, k, t * P:(t + 1) * P], self.normed[:, t, k * P:(k + 1) * P],
                                    self.ident[:, :])
            done.then_inc(self.turned_ready, 1)

    def copy(self, act, n):
        for k in range(DK):
            act.wait_ge(self.turned_ready, n.past(DK, k + 1))
            self.nc.scalar.copy(self.xt[:, n.parity, k, :], self.turned_ps[:, k, :]).then_inc(self.xt_ready, 1)


def turn_weights(nc, sem, tag, ident, matrices):
    pieces = []
    for src, dst, factor in matrices:
        rows, cols = src.shape
        for r in range(0, rows, P):
            for c in range(0, cols, D):
                pieces.append((src[r:r + P, c:c + D],
                               dst[c:c + D, r:r + P].rearrange("(k p) r -> p k r", p=P), factor))
    with ExitStack() as ctx:
        st = Stage(nc, sem, ctx, tag)
        N = 4
        raw = [st.sb(f"raw{i}", [P, D]) for i in range(N)]
        raw_int = [st.sb(f"raw_int{i}", [P, D], I32) for i in range(N)]
        turned = st.sb("turned", [P, N, DK, P])
        turned_ps = st.ps("turned_ps", [P, N, BANK])
        piece_loaded = [st.sem(f"piece_loaded{i}") for i in range(N)]
        dequantised, turned_ready, copied = st.sem("dequantised"), st.sem("turned_ready"), st.sem("copied")
        stored = [st.sem(f"stored{i}") for i in range(N)]
        quantised = [sum(f is not None for _, _, f in pieces[:i]) for i in range(len(pieces) + 1)]
        block = ctx.enter_context(nc.Block())

        @block.sync
        def _(sp):
            for i, (src, _, factor) in enumerate(pieces):
                if i >= N:
                    sp.wait_ge(turned_ready, i - N + 1)
                sp.dma_start((raw if factor is None else raw_int)[i % N][:, :], src).then_inc(piece_loaded[i % N], DMA)

        @block.vector
        def _(dve):
            for i, (_, _, factor) in enumerate(pieces):
                if factor is not None:
                    dve.wait_ge(piece_loaded[i % N], (i // N + 1) * DMA)
                    if i >= N:
                        dve.wait_ge(turned_ready, i - N + 1)
                    nc.vector.tensor_scalar(raw[i % N][:, :], raw_int[i % N][:, :], factor, None,
                                            ALU.mult).then_inc(dequantised, 1)

        @block.tensor
        def _(pe):
            for i, (_, _, factor) in enumerate(pieces):
                if factor is None:
                    pe.wait_ge(piece_loaded[i % N], (i // N + 1) * DMA)
                else:
                    pe.wait_ge(dequantised, quantised[i + 1])
                if i >= N:
                    pe.wait_ge(copied, i - N + 1)
                for k in range(DK):
                    done = pe.transpose(turned_ps[:, i % N, k * P:(k + 1) * P], raw[i % N][:, k * P:(k + 1) * P],
                                        ident[:, :])
                done.then_inc(turned_ready, 1)

        @block.scalar
        def _(act):
            for i, (_, dst, _) in enumerate(pieces):
                act.wait_ge(turned_ready, i + 1)
                if i >= N:
                    act.wait_ge(stored[i % N], (i // N) * DMA)
                nc.scalar.copy(turned[:, i % N].rearrange("p k r -> p (k r)"),
                               turned_ps[:, i % N, 0:D]).then_inc(copied, 1)
                act.wait_ge(copied, i + 1)
                act.dma_start(dst, turned[:, i % N]).then_inc(stored[i % N], DMA)
            for i in range(N):
                act.wait_ge(stored[i], len(range(i, len(pieces), N)) * DMA)


def swapped_columns(nc, eng, dst, src, done):
    a, b = (t.rearrange("p (g two) -> p g two", two=2) for t in (src, dst))
    for half in range(2):
        eng.tensor_copy(b[:, :, half], a[:, :, 1 - half]).then_inc(done, 1)


def project(nc, sem, tag, x, ident, q_parts, k_parts, v_cols_dram, weights, rotary=None):
    with ExitStack() as ctx:
        st = Stage(nc, sem, ctx, tag)
        front = Normed(st, x, ident)
        wq, wk, wv = (st.sb(n, [P, DK, D]) for n in ("wq", "wk", "wv"))
        partner_w = rotary is not None
        if partner_w:
            wq_partner = st.sb("wq_partner", [P, DK, D])
            wk_partner = st.sb("wk_partner", [P, DK, D])
            cos_sin = st.sb("cos_sin", [P, 2, 2, CHUNK])
        rot_a = st.sb("rot_a", [P, 2, CHUNK])
        rot_b = st.sb("rot_b", [P, 2, CHUNK])
        value = st.sb("value", [P, 2, CHUNK])
        rest = st.sb("rest", [P, 2, CHUNK])
        parts = st.sb("parts", [P, 2, PARTS, CHUNK], BF16)
        v_tiles = st.sb("v_tiles", [P, H, TPC, VW])
        pair_ps = st.ps("pair_ps", [P, 2, 2, BANK])
        v_ps = st.ps("v_ps", [P, 2, BANK])
        w_loaded, w_made = st.sem("w_loaded"), st.sem("w_made")
        v_tiles_set = st.sem("v_tiles_set")
        table_loaded = [st.sem("table_loaded0"), st.sem("table_loaded1")]
        pair_ready, pair_read = st.sem("pair_ready"), st.sem("pair_read")
        v_ready, v_read = st.sem("v_ready"), st.sem("v_read")
        v_stored = st.sem("v_stored")
        passed = [st.sem(f"passed{i}") for i in range(3)]
        cut_step = [st.sem("cut_step0"), st.sem("cut_step1")]
        cut_done = [st.sem("cut_done0"), st.sem("cut_done1")]
        parts_stored = [st.sem("parts_stored0"), st.sem("parts_stored1")]
        UNITS = [(0, 0), (0, 1), (1, 0), (1, 1)]
        W_LOADS, W_MADE = 3 * DMA, 8 if partner_w else 0
        CUT = 4
        block = ctx.enter_context(nc.Block())

        @block.sync
        def _(sp):
            begin_at_one(sp, v_stored, *parts_stored, *cut_done, *front.from_one)
            for w, src in zip((wq, wk, wv), weights):
                sp.dma_start(w[:, :, :], src.rearrange("(k p) n -> p k n", p=P)).then_inc(w_loaded, DMA)

            def ahead(n, first=False):
                sp.wait_ge(front.normed_ready, n.past(TPC, 0))
                front.load(sp, n)
                if partner_w:
                    if not first:
                        sp.wait_ge(pair_read, n.at(4, -2))
                    for i in range(2):
                        sp.dma_start(cos_sin[:, n.parity, i, :], rotary[i].rearrange("p (n s) -> n p s", s=CHUNK)[n.index]
                                     ).then_inc(table_loaded[n.parity], DMA)

            def work(n, ahead_next):
                ahead_next()
                sp.wait_ge(v_read, n.at(2, 4))
                sp.dma_start(v_cols_dram.rearrange("h p (n t) c -> n p h (t c)", t=TPC)[n.index],
                             v_tiles[:, :, :, :].rearrange("p h t c -> p h (t c)")).then_inc(v_stored, DMA)
                for u, (kind, m) in enumerate(UNITS):
                    b = u % 2
                    sp.wait_ge(cut_done[b], n.past(2, u // 2 + 1))
                    sp.sem_inc(passed[2], 1)
                    dst = (q_parts, k_parts)[kind].rearrange("a (m p) (n s) -> n m p a s", p=P, s=CHUNK)[n.index][m]
                    sp.dma_start(dst, parts[:, b]).then_inc(parts_stored[b], DMA)

            ahead(Chunk(0, 0), True)
            with sp.Fori(0, CHUNKS // 2 - 1) as turn:
                for r in range(2):
                    work(Chunk(turn, r), lambda: ahead(Chunk(turn, r + 1)))
            work(Chunk(CHUNKS // 2 - 1, 0), lambda: ahead(Chunk(CHUNKS // 2 - 1, 1)))
            work(Chunk(CHUNKS // 2 - 1, 1), nothing)
            sp.wait_ge(v_stored, 1 + CHUNKS * DMA)
            for b in range(2):
                sp.wait_ge(parts_stored[b], 1 + CHUNKS * 2 * DMA)

        def cut(eng, n, u):
            b = u % 2
            step = cut_step[b]
            if partner_w:
                eng.wait_ge(pair_read, n.at(4, u + 3))
                eng.tensor_tensor(value[:, b], rot_a[:, b], rot_b[:, b], ALU.add).then_inc(step, 1)
                eng.wait_ge(step, n.at(2 * CUT, CUT * (u // 2) + 1))
            else:
                eng.wait_ge(pair_read, n.at(4, u + 3))
            eng.wait_ge(parts_stored[b], n.past(2 * DMA, u // 2 * DMA))
            base = 1 if partner_w else 0
            eng.sem_inc(passed[b], 1)
            eng.tensor_copy(parts[:, b, 0], value[:, b]).then_inc(step, 1)
            eng.wait_ge(step, n.at(2 * CUT, CUT * (u // 2) + base + 1))
            eng.tensor_tensor(rest[:, b], value[:, b], parts[:, b, 0], ALU.subtract).then_inc(step, 1)
            eng.wait_ge(step, n.at(2 * CUT, CUT * (u // 2) + base + 2))
            eng.sem_inc(passed[b], 1)
            eng.tensor_copy(parts[:, b, 1], rest[:, b]).then_inc(step, 1 if partner_w else 2)
            eng.wait_ge(step, n.at(2 * CUT, CUT * (u // 2) + CUT))
            eng.tensor_tensor(parts[:, b, 2], rest[:, b], parts[:, b, 1], ALU.subtract).then_inc(cut_done[b], 1)

        @block.gpsimd
        def _(pool):
            front.start_power(pool)
            pool.memset(v_tiles[:, :, :, HD:VW], 0.0).then_inc(v_tiles_set, 1)
            pool.wait_ge(v_tiles_set, 1)
            pool.memset(v_tiles[:, :, :, HD:HD + 1], 1.0).then_inc(v_tiles_set, 1)
            pool.wait_ge(v_tiles_set, 2)

            def work(n, ahead_next):
                cut(pool, n, 1)
                ahead_next()
                cut(pool, n, 3)

            each_chunk(pool, lambda n: front.power(pool, n), work)

        @block.tensor
        def _(pe):
            pe.wait_ge(w_loaded, W_LOADS)
            if W_MADE:
                pe.wait_ge(w_made, W_MADE)

            def work(n, ahead_next):
                xt = front.xt[:, n.parity]
                pe.wait_ge(front.xt_ready, n.past(DK, DK))
                for i in range(2):
                    pe.wait_ge(v_read, n.at(2, i + 1))
                    for j in range(2):
                        t = 2 * i + j
                        for k in range(DK):
                            done = pe.matmul(v_ps[:, i, j * D:(j + 1) * D], xt[:, k, t * P:(t + 1) * P], wv[:, k, :],
                                             start=k == 0, stop=k == DK - 1)
                    done.then_inc(v_ready, 1)
                for u in range(4):
                    if u == 3:
                        ahead_next()
                    pair(n, u, xt)

            def pair(n, u, xt):
                kind, m = UNITS[u]
                pe.wait_ge(pair_read, n.at(4, u + 1))
                w = [(wq, wk)[kind]] + ([(wq_partner, wk_partner)[kind]] if partner_w else [])
                for i, wi in enumerate(w):
                    for k in range(DK):
                        done = pe.matmul(pair_ps[:, u % 2, i, :], wi[:, k, m * P:(m + 1) * P], xt[:, k, :],
                                         start=k == 0, stop=k == DK - 1)
                done.then_inc(pair_ready, 1)

            each_chunk(pe, lambda n: front.turn(pe, n), work)

        @block.scalar
        def _(act):
            act.wait_ge(v_tiles_set, 2)
            act.sem_inc(pair_read, 2)
            act.sem_inc(v_read, 2)

            def work(n, ahead_next):
                act.wait_ge(v_stored, n.past(DMA, 0))
                for i in range(2):
                    act.wait_ge(v_ready, n.at(2, i + 1))
                    nc.scalar.copy(v_tiles[:, :, 2 * i:2 * i + 2, 0:HD].rearrange("p h t c -> p t h c"),
                                   v_ps[:, i, :].rearrange("p (t h c) -> p t h c", t=2, h=H)).then_inc(v_read, 1)
                if not partner_w:
                    for u in range(4):
                        b = u % 2
                        if u == 3:
                            ahead_next()
                        act.wait_ge(pair_ready, n.at(4, u + 1))
                        act.wait_ge(cut_done[b], n.past(2, u // 2))
                        nc.scalar.copy(value[:, b], pair_ps[:, b, 0, :]).then_inc(pair_read, 1)
                else:
                    ahead_next()

            each_chunk(act, lambda n: front.copy(act, n), work)

        @block.vector
        def _(dve):
            if partner_w:
                dve.wait_ge(w_loaded, W_LOADS)
                for k in range(DK):
                    swapped_columns(nc, nc.vector, wq_partner[:, k, :], wq[:, k, :], w_made)
                    swapped_columns(nc, nc.vector, wk_partner[:, k, :], wk[:, k, :], w_made)

            def work(n, ahead_next):
                for u, (kind, m) in enumerate(UNITS):
                    b = u % 2
                    if partner_w:
                        dve.wait_ge(pair_ready, n.at(4, u + 1))
                        dve.wait_ge(cut_done[b], n.past(2, u // 2))
                        if u == 0:
                            dve.wait_ge(table_loaded[n.parity], n.turn * 2 * DMA + (n.r // 2 + 1) * 2 * DMA)
                        for i, rot in enumerate((rot_a, rot_b)):
                            table = cos_sin[:, n.parity, i, :]
                            done = nc.vector.tensor_tensor(rot[:, b], pair_ps[:, b, i, :], table, ALU.mult)
                        done.then_inc(pair_read, 1)
                    if u == 1:
                        ahead_next()
                    if b == 0:
                        cut(dve, n, u)

            dve.wait_ge(v_tiles_set, 2)
            each_chunk(dve, lambda n: front.normalise(dve, n), work)


def merge_heads(nc, sem, tag, x, x_out, heads_out, w_out):
    with ExitStack() as ctx:
        st = Stage(nc, sem, ctx, tag)
        w = st.sb("w", [P, DK, D])
        spread = st.sb("spread", [H, DK, P])
        raw = st.sb("raw", [P, 2, TPC, D])
        rows = st.sb("rows", [P, 2, DK, CHUNK])
        sums = st.sb("sums", [H, 2, CHUNK])
        over = st.sb("over", [H, CHUNK])
        scaled = st.sb("scaled", [P, 2, DK, CHUNK])
        y = st.sb("y", [P, 2, TPC, D])
        over_ps = st.ps("over_ps", [P, DK, BANK])
        y_ps = st.ps("y_ps", [P, 2, BANK])
        w_loaded, spread_set = st.sem("w_loaded"), st.sem("spread_set")
        loaded = [st.sem("loaded0"), st.sem("loaded1")]
        over_ready, spread_ready, scaled_ready = st.sem("over_ready"), st.sem("spread_ready"), st.sem("scaled_ready")
        y_ready, y_added = st.sem("y_ready"), st.sem("y_added")
        y_stored = [st.sem("y_stored0"), st.sem("y_stored1")]
        LOADS = 4 * DMA
        block = ctx.enter_context(nc.Block())

        @block.sync
        def _(sp):
            begin_at_one(sp, scaled_ready, spread_ready, y_added, *y_stored)
            sp.dma_start(w[:, :, :], w_out.rearrange("(k p) n -> p k n", p=P)).then_inc(w_loaded, DMA)

            def load(n):
                full = loaded[n.parity]
                sp.dma_start(raw[:, n.parity], by_chunk(x)[n.index]).then_inc(full, DMA)
                cut = heads_out.rearrange("h r (n s) -> n h r s", s=CHUNK)[n.index]
                for m in range(DK):
                    sp.dma_start(rows[:, n.parity, m, :], cut[m * H // 2:(m + 1) * H // 2, 0:HD, :]).then_inc(full, DMA)
                sp.dma_start(sums[:, n.parity, :], cut[:, HD, :]).then_inc(full, DMA)

            def work(n, load_later):
                sp.wait_ge(y_added, n.past(2, 2))
                sp.dma_start(by_chunk(x_out)[n.index], y[:, n.parity]).then_inc(y_stored[n.parity], DMA)
                load_later()

            two_ahead(sp, load, work)
            for b in range(2):
                sp.wait_ge(y_stored[b], 1 + CHUNKS // 2 * DMA)

        @block.gpsimd
        def _(pool):
            pool.memset(spread[:, :, :], 1.0).then_inc(spread_set, 1)
            pool.wait_ge(spread_set, 1)
            flat = spread[:, :, :].rearrange("h m p -> h (m p)")
            pool.affine_select(out=flat, in_=flat, compare_op=ALU.is_ge, fill=0.0, base=0,
                               pattern=[[1, D]], channel_multiplier=-HD).then_inc(spread_set, 1)
            pool.wait_ge(spread_set, 2)
            pool.affine_select(out=flat, in_=flat, compare_op=ALU.is_ge, fill=0.0, base=HD - 1,
                               pattern=[[-1, D]], channel_multiplier=HD).then_inc(spread_set, 1)
            pool.wait_ge(spread_set, 3)

        @block.tensor
        def _(pe):
            pe.wait_ge(w_loaded, DMA)
            pe.wait_ge(spread_set, 3)

            def ahead(n):
                pe.wait_ge(over_ready, n.at(1, 1))
                pe.wait_ge(scaled_ready, n.past(DK, 0))
                for m in range(DK):
                    pe.matmul(over_ps[:, m, :], spread[:, m, :], over[:, :], start=True,
                              stop=True).then_inc(spread_ready, 1)

            def work(n, ahead_next):
                ahead_next()
                pe.wait_ge(scaled_ready, n.past(DK, DK))
                pe.wait_ge(y_added, n.past(2, 0))
                for i in range(2):
                    for j in range(2):
                        t = 2 * i + j
                        for m in range(DK):
                            done = pe.matmul(y_ps[:, i, j * D:(j + 1) * D], scaled[:, n.parity, m, t * P:(t + 1) * P],
                                             w[:, m, :], start=m == 0, stop=m == DK - 1)
                    done.then_inc(y_ready, 1)

            each_chunk(pe, ahead, work)

        @block.vector
        def _(dve):
            def ahead(n):
                dve.wait_ge(loaded[n.parity], n.turn * LOADS + (n.r // 2 + 1) * LOADS)
                dve.wait_ge(spread_ready, n.past(DK, 0))
                nc.vector.reciprocal(over[:, :], sums[:, n.parity, :]).then_inc(over_ready, 1)
                for m in range(DK):
                    dve.wait_ge(spread_ready, n.past(DK, m + 1))
                    nc.vector.tensor_tensor(scaled[:, n.parity, m, :], over_ps[:, m, :], rows[:, n.parity, m, :],
                                            ALU.mult).then_inc(scaled_ready, 1)

            def work(n, ahead_next):
                ahead_next()
                dve.wait_ge(y_stored[n.parity], 1 + n.turn * DMA + n.r // 2 * DMA)
                for i in range(2):
                    dve.wait_ge(y_ready, n.at(2, i + 1))
                    nc.vector.tensor_tensor(y[:, n.parity, 2 * i:2 * i + 2, :].rearrange("p t d -> p (t d)"), y_ps[:, i, :],
                                            raw[:, n.parity, 2 * i:2 * i + 2, :].rearrange("p t d -> p (t d)"),
                                            ALU.add).then_inc(y_added, 1)

            each_chunk(dve, ahead, work)


def feed_forward(nc, sem, tag, x, x_out, ident, hidden, w_in, w_gate, w_down, in_bias=None, out_biases=()):
    M = hidden // P
    gated = w_gate is not None
    with ExitStack() as ctx:
        st = Stage(nc, sem, ctx, tag)
        front = Normed(st, x, ident)
        wi = st.sb("wi", [P, DK, hidden])
        wg = st.sb("wg", [P, DK, hidden if gated else 1])
        wd = st.sb("wd", [P, M, D])
        bias_in = st.sb("bias_in", [P, M])
        bias_out = st.sb("bias_out", [P, 2, 2 * D])
        act_t = st.sb("act_t", [P, M, CHUNK])
        silu_t = st.sb("silu_t", [P, 2, CHUNK])
        y = st.sb("y", [P, 2, TPC, D])
        G = 2 if gated else 1
        up_ps = st.ps("up_ps", [P, 2, G, BANK])
        y_ps = st.ps("y_ps", [P, 2, BANK])
        w_loaded, bias_added = st.sem("w_loaded"), st.sem("bias_added")
        up_ready, act_ready = st.sem("up_ready"), st.sem("act_ready")
        silu_ready = st.sem("silu_ready")
        y_ready, y_added = st.sem("y_ready"), st.sem("y_added")
        biased = st.sem("biased")
        y_stored = [st.sem("y_stored0"), st.sem("y_stored1")]
        loads = [(wi[:, :, :], w_in.rearrange("(k p) n -> p k n", p=P)), (wd[:, :, :], w_down.rearrange("(k p) n -> p k n", p=P))]
        if gated:
            loads.append((wg[:, :, :], w_gate.rearrange("(k p) n -> p k n", p=P)))
        else:
            loads.append((bias_in[:, :], in_bias.rearrange("(m p) -> p m", p=P)))
        for i, b in enumerate(out_biases):
            loads.append((bias_out[:, i, 0:D], b.partition_broadcast(P)))
            loads.append((bias_out[:, i, D:2 * D], b.partition_broadcast(P)))
        W_LOADS = len(loads) * DMA
        block = ctx.enter_context(nc.Block())

        @block.sync
        def _(sp):
            begin_at_one(sp, y_added, *y_stored, *front.from_one)
            with nc.allow_non_contiguous_dma(reason="1024 bias values by partition"):
                for dst, src in loads:
                    sp.dma_start(dst, src).then_inc(w_loaded, DMA)

            def work(n, load_later):
                sp.wait_ge(y_added, n.past(2, 2))
                sp.dma_start(by_chunk(x_out)[n.index], y[:, n.parity]).then_inc(y_stored[n.parity], DMA)
                load_later()

            two_ahead(sp, lambda n: front.load(sp, n), work)
            for b in range(2):
                sp.wait_ge(y_stored[b], 1 + CHUNKS // 2 * DMA)

        @block.gpsimd
        def _(pool):
            front.start_power(pool)
            if out_biases:
                pool.wait_ge(w_loaded, W_LOADS)
                pool.tensor_tensor(bias_out[:, 0, :], bias_out[:, 0, :], bias_out[:, 1, :], ALU.add).then_inc(bias_added, 1)
                pool.wait_ge(bias_added, 1)

            def work(n, ahead_next):
                ahead_next()
                if out_biases:
                    pool.wait_ge(front.normed_ready, n.past(TPC, TPC))
                    flat_x = front.raw[:, n.parity].rearrange("p (i t) d -> p i (t d)", i=2)
                    for i in range(2):
                        pool.tensor_tensor(flat_x[:, i, :], flat_x[:, i, :], bias_out[:, 0, :], ALU.add).then_inc(biased, 1)
                        pool.wait_ge(biased, n.at(2, i + 1))

            each_chunk(pool, lambda n: front.power(pool, n), work)

        @block.tensor
        def _(pe):
            pe.wait_ge(w_loaded, W_LOADS)

            def work(n, ahead_next):
                xt = front.xt[:, n.parity]
                pe.wait_ge(front.xt_ready, n.past(DK, DK))
                for m in range(M):
                    pe.wait_ge(act_ready, n.at(M, m + 1))
                    for g, w in enumerate((wg, wi) if gated else (wi,)):
                        for k in range(DK):
                            done = pe.matmul(up_ps[:, m % 2, g, :], w[:, k, m * P:(m + 1) * P], xt[:, k, :],
                                             start=k == 0, stop=k == DK - 1)
                    done.then_inc(up_ready, 1)
                ahead_next()
                pe.wait_ge(y_added, n.past(2, 0))
                for i in range(2):
                    for j in range(2):
                        t = 2 * i + j
                        for m in range(M):
                            if i == 0 and j == 0:
                                pe.wait_ge(act_ready, n.at(M, m + 3))
                            done = pe.matmul(y_ps[:, i, j * D:(j + 1) * D], act_t[:, m, t * P:(t + 1) * P], wd[:, m, :],
                                             start=m == 0, stop=m == M - 1)
                    done.then_inc(y_ready, 1)

            each_chunk(pe, lambda n: front.turn(pe, n), work)

        @block.scalar
        def _(act):
            act.wait_ge(w_loaded, W_LOADS)
            act.sem_inc(act_ready, 2)

            def work(n, ahead_next):
                for m in range(M):
                    act.wait_ge(up_ready, n.at(M, m + 1))
                    if gated:
                        act.wait_ge(act_ready, n.at(M, m + 1))
                        nc.scalar.activation(silu_t[:, m % 2, :], up_ps[:, m % 2, 0, :], ACT.Silu).then_inc(silu_ready, 1)
                    else:
                        nc.scalar.activation(act_t[:, m, :], up_ps[:, m % 2, 0, :], ACT.Gelu,
                                             bias=bias_in[:, m:m + 1]).then_inc(act_ready, 1)
                ahead_next()

            each_chunk(act, lambda n: front.copy(act, n), work)

        @block.vector
        def _(dve):
            def work(n, ahead_next):
                for m in range(M if gated else 0):
                    if m == M - 2:
                        ahead_next()
                    dve.wait_ge(silu_ready, n.at(M, m + 1))
                    nc.vector.tensor_tensor(act_t[:, m, :], up_ps[:, m % 2, 1, :], silu_t[:, m % 2, :],
                                            ALU.mult).then_inc(act_ready, 1)
                if not gated:
                    ahead_next()
                if out_biases:
                    dve.wait_ge(biased, n.at(2, 2))
                dve.wait_ge(y_stored[n.parity], 1 + n.turn * DMA + n.r // 2 * DMA)
                for i in range(2):
                    dve.wait_ge(y_ready, n.at(2, i + 1))
                    nc.vector.tensor_tensor(y[:, n.parity, 2 * i:2 * i + 2, :].rearrange("p t d -> p (t d)"), y_ps[:, i, :],
                                            front.raw[:, n.parity, 2 * i:2 * i + 2, :].rearrange("p t d -> p (t d)"),
                                            ALU.add).then_inc(y_added, 1)

            each_chunk(dve, lambda n: front.normalise(dve, n), work)


HL, EL = 16, 64
WL = HL * EL
PAIRS = WL // P
VP = 2 * (EL + 1)
Z_EPS = 1e-6


def linear_state(nc, sem, tag, x, ident, w_k, w_v, state_out):
    with ExitStack() as ctx:
        st = Stage(nc, sem, ctx, tag)
        front = Normed(st, x, ident)
        wk, wv = st.sb("wk", [P, DK, WL]), st.sb("wv", [P, DK, WL])
        low = st.sb("low", [P, 2, BANK])
        phi = st.sb("phi", [P, 2, WL])
        v_ones = st.sb("v_ones", [P, 2, HL, EL + 1])
        state = st.sb("state", [P, PAIRS, VP])
        wide = st.sb("wide", [P, 2, PAIRS, P])
        k_ps = st.ps("k_ps", [P, 2, BANK])
        v_ps = st.ps("v_ps", [P, BANK])
        state_ps = st.ps("state_ps", [P, 3, BANK])
        w_loaded, ones_set, state_set = st.sem("w_loaded"), st.sem("ones_set"), st.sem("state_set")
        k_ready, v_ready = st.sem("k_ready"), st.sem("v_ready")
        low_ready, exp_ready = st.sem("low_ready"), st.sem("exp_ready")
        phi_ready = st.sem("phi_ready")
        v_copied = st.sem("v_copied")
        state_ready, state_added = st.sem("state_ready"), st.sem("state_added")
        products = st.sem("products")
        wide_set, stored = st.sem("wide_set"), st.sem("stored")
        HALVES = WL // BANK
        block = ctx.enter_context(nc.Block())

        @block.sync
        def _(sp):
            begin_at_one(sp, state_added, *front.from_one)
            sp.dma_start(wk[:, :, :], w_k.rearrange("(k p) n -> p k n", p=P)).then_inc(w_loaded, DMA)
            sp.dma_start(wv[:, :, :], w_v.rearrange("(k p) n -> p k n", p=P)).then_inc(w_loaded, DMA)

            def ahead(n):
                sp.wait_ge(front.normed_ready, n.past(TPC, 0))
                front.load(sp, n)

            each_chunk(sp, ahead, lambda n, ahead_next: ahead_next())
            sp.wait_ge(wide_set, 5)
            sp.dma_start(state_out.rearrange("i p a c -> p i a c"), wide[:, :, :, :]).then_inc(stored, DMA)
            sp.wait_ge(stored, DMA)

        @block.gpsimd
        def _(pool):
            front.start_power(pool)
            pool.memset(v_ones[:, :, :, EL:EL + 1], 1.0).then_inc(ones_set, 1)
            pool.wait_ge(ones_set, 1)
            pool.memset(state[:, :, :], 0.0).then_inc(state_set, 1)
            pool.wait_ge(state_set, 1)
            pool.memset(wide[:, :, :, :], 0.0).then_inc(wide_set, 1)
            pool.wait_ge(wide_set, 1)
            each_chunk(pool, lambda n: front.power(pool, n), lambda n, ahead_next: ahead_next())

        @block.tensor
        def _(pe):
            pe.wait_ge(w_loaded, 2 * DMA)

            def work(n, ahead_next):
                xt = front.xt[:, n.parity]
                pe.wait_ge(front.xt_ready, n.past(DK, DK))
                for t in range(TPC):
                    if t == 3:
                        ahead_next()
                    for f in range(HALVES):
                        pe.wait_ge(phi_ready, n.at(TPC * HALVES, HALVES * t + f + 1))
                        for k in range(DK):
                            done = pe.matmul(k_ps[:, f, :], xt[:, k, t * P:(t + 1) * P], wk[:, k, f * BANK:(f + 1) * BANK],
                                             start=k == 0, stop=k == DK - 1)
                        done.then_inc(k_ready, 1)
                    for f in range(HALVES):
                        pe.wait_ge(v_copied, n.at(TPC * HALVES, HALVES * t + f + 1))
                        for k in range(DK):
                            done = pe.matmul(v_ps[:, :], xt[:, k, t * P:(t + 1) * P], wv[:, k, f * BANK:(f + 1) * BANK],
                                             start=k == 0, stop=k == DK - 1)
                        done.then_inc(v_ready, 1)
                    if t:
                        product(n, t - 1)
                product(n, TPC - 1)

            def product(n, t):
                pe.wait_ge(phi_ready, n.at(TPC * HALVES, HALVES * t + HALVES + 2))
                pe.wait_ge(v_copied, n.at(TPC * HALVES, HALVES * t + HALVES + 1))
                if t == 0:
                    pe.wait_ge(state_added, n.past(3, 0))
                for a in range(PAIRS):
                    done = pe.matmul(state_ps[:, a // 3, a % 3 * VP:(a % 3 + 1) * VP], phi[:, t % 2, a * P:(a + 1) * P],
                                     v_ones[:, t % 2, 2 * a:2 * a + 2, :].rearrange("p h c -> p (h c)"),
                                     start=t == 0 and a % 3 == 0, stop=t == TPC - 1, skip_group_check=True)
                done.then_inc(products, 1)

            each_chunk(pe, lambda n: front.turn(pe, n), work)

        @block.scalar
        def _(act):
            act.sem_inc(v_copied, 1)
            act.sem_inc(products, 2)
            act.wait_ge(ones_set, 1)

            def work(n, ahead_next):
                for t in range(TPC):
                    for f in range(HALVES):
                        act.wait_ge(low_ready, n.at(TPC * HALVES, HALVES * t + f + 1))
                        nc.scalar.activation(low[:, f, :], low[:, f, :], ACT.Exp).then_inc(exp_ready, 1)
                    act.wait_ge(products, n.at(TPC, t + 1))
                    for f in range(HALVES):
                        act.wait_ge(v_ready, n.at(TPC * HALVES, HALVES * t + f + 1))
                        nc.scalar.copy(v_ones[:, t % 2, f * HL // 2:(f + 1) * HL // 2, 0:EL],
                                       v_ps[:, :].rearrange("p (h c) -> p h c", c=EL)).then_inc(v_copied, 1)
                ahead_next()

            each_chunk(act, lambda n: front.copy(act, n), work)

        @block.vector
        def _(dve):
            dve.sem_inc(phi_ready, 2)
            dve.wait_ge(state_set, 1)

            def work(n, ahead_next):
                for t in range(TPC):
                    for f in range(HALVES):
                        j = HALVES * t + f
                        dve.wait_ge(k_ready, n.at(TPC * HALVES, j + 1))
                        nc.vector.tensor_scalar(low[:, f, :], k_ps[:, f, :], 0.0, None, ALU.min).then_inc(low_ready, 1)
                    if t == 1:
                        ahead_next()
                    dve.wait_ge(products, n.at(TPC, t + 1))
                    for f in range(HALVES):
                        j = HALVES * t + f
                        dve.wait_ge(exp_ready, n.at(TPC * HALVES, j + 1))
                        nc.vector.scalar_tensor_tensor(phi[:, t % 2, f * BANK:(f + 1) * BANK], k_ps[:, f, :], 0.0,
                                                       low[:, f, :], ALU.max, ALU.add).then_inc(phi_ready, 1)
                dve.wait_ge(products, n.at(TPC, TPC + 2))
                for i in range(3):
                    w = min(3, PAIRS - 3 * i)
                    nc.vector.tensor_tensor(state[:, 3 * i:3 * i + w, :].rearrange("p a c -> p (a c)"),
                                            state[:, 3 * i:3 * i + w, :].rearrange("p a c -> p (a c)"),
                                            state_ps[:, i, 0:w * VP], ALU.add).then_inc(state_added, 1)

            each_chunk(dve, lambda n: front.normalise(dve, n), work)
            dve.wait_ge(state_added, 1 + CHUNKS * 3)
            dve.wait_ge(wide_set, 1)
            for h in range(2):
                rows, c0 = slice(h * EL, (h + 1) * EL), h * (EL + 1)
                nc.vector.tensor_copy(wide[rows, 0, :, h * EL:(h + 1) * EL], state[rows, :, c0:c0 + EL]).then_inc(wide_set, 1)
                nc.vector.tensor_copy(wide[rows, 1, :, h * EL:(h + 1) * EL],
                                      state[rows, :, c0 + EL:c0 + EL + 1].broadcast_to([EL, PAIRS, EL])).then_inc(wide_set, 1)


def linear_output(nc, sem, tag, x, x_out, ident, w_q, state_in, w_out, bias):
    with ExitStack() as ctx:
        st = Stage(nc, sem, ctx, tag)
        front = Normed(st, x, ident)
        wq = st.sb("wq", [P, DK, WL])
        wo = st.sb("wo", [P, PAIRS, D])
        state = st.sb("state", [P, 2, PAIRS, P])
        bias_all = st.sb("bias_all", [P, 2 * D])
        low = st.sb("low", [P, 2, CHUNK])
        phi = st.sb("phi", [P, 2, CHUNK])
        z = st.sb("z", [P, 2, CHUNK])
        outs = st.sb("outs", [P, PAIRS, CHUNK])
        y = st.sb("y", [P, 2, TPC, D])
        eps = st.sb("eps", [P, 1])
        q_ps = st.ps("q_ps", [P, 2, BANK])
        top_ps, z_ps = st.ps("top_ps", [P, BANK]), st.ps("z_ps", [P, BANK])
        y_ps = st.ps("y_ps", [P, 2, BANK])
        w_loaded, eps_set = st.sem("w_loaded"), st.sem("eps_set")
        q_ready, low_ready, exp_ready = st.sem("q_ready"), st.sem("low_ready"), st.sem("exp_ready")
        phi_ready = st.sem("phi_ready")
        top_ready, z_ready, z_copied = st.sem("top_ready"), st.sem("z_ready"), st.sem("z_copied")
        over_ready, out_ready = st.sem("over_ready"), st.sem("out_ready")
        y_ready, y_added, biased = st.sem("y_ready"), st.sem("y_added"), st.sem("biased")
        y_stored = [st.sem("y_stored0"), st.sem("y_stored1")]
        W_LOADS = 5 * DMA
        block = ctx.enter_context(nc.Block())

        @block.sync
        def _(sp):
            begin_at_one(sp, z_copied, out_ready, top_ready, y_added, *y_stored, *front.from_one)
            sp.dma_start(wq[:, :, :], w_q.rearrange("(k p) n -> p k n", p=P)).then_inc(w_loaded, DMA)
            sp.dma_start(wo[:, :, :], w_out.rearrange("(k p) n -> p k n", p=P)).then_inc(w_loaded, DMA)
            sp.dma_start(state[:, :, :, :], state_in.rearrange("i p a c -> p i a c")).then_inc(w_loaded, DMA)
            for i in range(2):
                sp.dma_start(bias_all[:, i * D:(i + 1) * D], bias.partition_broadcast(P)).then_inc(w_loaded, DMA)
            def work(n, load_later):
                sp.wait_ge(y_added, n.past(2, 2))
                sp.dma_start(by_chunk(x_out)[n.index], y[:, n.parity]).then_inc(y_stored[n.parity], DMA)
                load_later()

            two_ahead(sp, lambda n: front.load(sp, n), work)
            for b in range(2):
                sp.wait_ge(y_stored[b], 1 + CHUNKS // 2 * DMA)

        @block.gpsimd
        def _(pool):
            front.start_power(pool)
            pool.memset(eps[:, :], Z_EPS).then_inc(eps_set, 1)
            pool.wait_ge(eps_set, 1)
            pool.wait_ge(w_loaded, W_LOADS)

            def work(n, ahead_next):
                ahead_next()
                pool.wait_ge(front.normed_ready, n.past(TPC, TPC))
                flat_x = front.raw[:, n.parity].rearrange("p (i t) d -> p i (t d)", i=2)
                for i in range(2):
                    pool.tensor_tensor(flat_x[:, i, :], flat_x[:, i, :], bias_all[:, :], ALU.add).then_inc(biased, 1)
                    pool.wait_ge(biased, n.at(2, i + 1))

            each_chunk(pool, lambda n: front.power(pool, n), work)

        @block.tensor
        def _(pe):
            pe.wait_ge(w_loaded, W_LOADS)

            def query(n, a):
                pe.wait_ge(phi_ready, n.at(PAIRS, a + 1))
                for k in range(DK):
                    done = pe.matmul(q_ps[:, a % 2, :], wq[:, k, a * P:(a + 1) * P], front.xt[:, n.parity, k, :],
                                     start=k == 0, stop=k == DK - 1)
                done.then_inc(q_ready, 1)

            def work(n, ahead_next):
                pe.wait_ge(front.xt_ready, n.past(DK, DK))
                query(n, 0)
                for a in range(PAIRS):
                    if a + 1 < PAIRS:
                        query(n, a + 1)
                    else:
                        ahead_next()
                    pe.wait_ge(phi_ready, n.at(PAIRS, a + 3))
                    pe.wait_ge(z_copied, n.past(PAIRS, a))
                    pe.matmul(z_ps[:, :], state[:, 1, a, :], phi[:, a % 2, :], start=True, stop=True).then_inc(z_ready, 1)
                    pe.wait_ge(out_ready, n.past(PAIRS, a))
                    pe.matmul(top_ps[:, :], state[:, 0, a, :], phi[:, a % 2, :], start=True, stop=True).then_inc(top_ready, 1)
                pe.wait_ge(y_added, n.past(2, 0))
                for i in range(2):
                    for j in range(2):
                        t = 2 * i + j
                        for a in range(PAIRS):
                            if i == 0 and j == 0:
                                pe.wait_ge(out_ready, n.past(PAIRS, a + 1))
                            done = pe.matmul(y_ps[:, i, j * D:(j + 1) * D], outs[:, a, t * P:(t + 1) * P], wo[:, a, :],
                                             start=a == 0, stop=a == PAIRS - 1)
                    done.then_inc(y_ready, 1)

            each_chunk(pe, lambda n: front.turn(pe, n), work)

        @block.scalar
        def _(act):
            act.wait_ge(eps_set, 1)

            def work(n, ahead_next):
                def exp(a):
                    act.wait_ge(low_ready, n.at(PAIRS, a + 1))
                    nc.scalar.activation(low[:, a % 2, :], low[:, a % 2, :], ACT.Exp).then_inc(exp_ready, 1)

                exp(0)
                for a in range(PAIRS):
                    if a + 1 < PAIRS:
                        exp(a + 1)
                    act.wait_ge(z_ready, n.at(PAIRS, a + 1))
                    if a > 1:
                        act.wait_ge(out_ready, n.past(PAIRS, a - 1))
                    nc.scalar.activation(z[:, a % 2, :], z_ps[:, :], ACT.Identity, bias=eps[:, 0:1]).then_inc(z_copied, 1)
                ahead_next()

            each_chunk(act, lambda n: front.copy(act, n), work)

        @block.vector
        def _(dve):
            dve.sem_inc(phi_ready, 2)

            def work(n, ahead_next):
                def low_of(a):
                    dve.wait_ge(q_ready, n.at(PAIRS, a + 1))
                    nc.vector.tensor_scalar(low[:, a % 2, :], q_ps[:, a % 2, :], 0.0, None, ALU.min).then_inc(low_ready, 1)

                def phi_of(a):
                    dve.wait_ge(exp_ready, n.at(PAIRS, a + 1))
                    dve.wait_ge(top_ready, n.past(PAIRS, max(0, a - 1)))
                    nc.vector.scalar_tensor_tensor(phi[:, a % 2, :], q_ps[:, a % 2, :], 0.0, low[:, a % 2, :],
                                                   ALU.max, ALU.add).then_inc(phi_ready, 1)

                def divide(a):
                    dve.wait_ge(z_copied, n.past(PAIRS, a + 1))
                    nc.vector.reciprocal(z[:, a % 2, :], z[:, a % 2, :]).then_inc(over_ready, 1)
                    dve.wait_ge(over_ready, n.at(PAIRS, a + 1))
                    dve.wait_ge(top_ready, n.past(PAIRS, a + 1))
                    nc.vector.tensor_tensor(outs[:, a, :], top_ps[:, :], z[:, a % 2, :], ALU.mult).then_inc(out_ready, 1)

                low_of(0)
                phi_of(0)
                for a in range(PAIRS):
                    if a + 1 < PAIRS:
                        low_of(a + 1)
                        phi_of(a + 1)
                    if a == PAIRS - 2:
                        ahead_next()
                    divide(a)
                dve.wait_ge(biased, n.at(2, 2))
                dve.wait_ge(y_stored[n.parity], 1 + n.turn * DMA + n.r // 2 * DMA)
                for i in range(2):
                    dve.wait_ge(y_ready, n.at(2, i + 1))
                    nc.vector.tensor_tensor(y[:, n.parity, 2 * i:2 * i + 2, :].rearrange("p t d -> p (t d)"), y_ps[:, i, :],
                                            front.raw[:, n.parity, 2 * i:2 * i + 2, :].rearrange("p t d -> p (t d)"),
                                            ALU.add).then_inc(y_added, 1)

            each_chunk(dve, lambda n: front.normalise(dve, n), work)


LATENT = 64
TURN = 2 * TPC


class Tile:

    def __init__(self, turn, r):
        self.turn, self.r = turn, r

    def at(self, c):
        return self.turn * TURN + (self.r + c)

    def steps(self, per_tile, c):
        return self.turn * (TURN * per_tile) + (self.r * per_tile + c)

    @property
    def slot(self):
        return self.r % 2

    @property
    def chunk(self):
        return Chunk(self.turn, self.r // TPC)


def each_tile(eng, steps, ahead):
    def body(turn, r, present=lambda r: True):
        for lag, step in steps:
            if present(r - lag):
                step(Tile(turn, r - lag))

    ahead(Chunk(0, 0))
    for r in range(TPC):
        if r == TPC - 1:
            ahead(Chunk(0, 1))
        body(0, r, lambda r: r >= 0)
    with eng.Fori(0, CHUNKS // 2 - 1) as turn:
        for r in range(TPC, TPC + TURN):
            if r % TPC == TPC - 1:
                ahead(Chunk(turn, r // TPC + 1))
            body(turn, r)
    for r in range(TPC, TURN + max(lag for lag, _ in steps)):
        body(CHUNKS // 2 - 1, r, lambda r: r < TURN)


def attention_over_heads(nc, sem, tag, x, x_out, ident, weights, rotary):
    Wq, bq, Wdown, bdown, Wup, bup, Wout, bout = weights
    with ExitStack() as ctx:
        st = Stage(nc, sem, ctx, tag)
        front = Normed(st, x, ident)
        wq, w_down = st.sb("wq", [P, DK, D]), st.sb("w_down", [P, DK, LATENT])
        w_up = st.sb("w_up", [LATENT + 1, 2, D])
        w_out = st.sb("w_out", [P, DK, D])
        b_rows, ones = st.sb("b_rows", [1, 2, D]), st.sb("ones", [1, P])
        b_down = st.sb("b_down", [LATENT, 1])
        cos_sin = st.sb("cos_sin", [P, 2, TILES, HD])
        latent = st.sb("latent", [LATENT + 1, 2, CHUNK])
        rot_a, rot_b = st.sb("rot_a", [P, 2 * D]), st.sb("rot_b", [P, 2 * D])
        qk = st.sb("qk", [P, 2, 2 * D])
        v_t = st.sb("v_t", [P, 2, HD, H])
        score_terms = st.sb("score_terms", [P, 2, H, H, HD])
        scores = st.sb("scores", [P, 2, H, H])
        exps = st.sb("exps", [P, 2, H, H])
        out_terms = st.sb("out_terms", [P, 2, H, HD, H])
        row_max, row_sum = st.sb("row_max", [P, H]), st.sb("row_sum", [P, H])
        over = st.sb("over", [P, H])
        sums = st.sb("sums", [P, H, HD])
        attended = st.sb("attended", [P, 2, H, HD])
        attended_t = st.sb("attended_t", [P, 2, DK, P])
        y = st.sb("y", [P, 2, TPC, D])
        qk_ps = st.ps("qk_ps", [P, 2, BANK])
        v_ps, latent_ps = st.ps("v_ps", [P, D]), st.ps("latent_ps", [LATENT, CHUNK])
        back_ps, y_ps = st.ps("back_ps", [P, DK, P]), st.ps("y_ps", [P, D])
        w_loaded, ones_set = st.sem("w_loaded"), st.sem("ones_set")
        latent_ready, latent_read = st.sem("latent_ready"), st.sem("latent_read")
        qk_ready, v_ready, v_copied = st.sem("qk_ready"), st.sem("v_ready"), st.sem("v_copied")
        products_made = st.sem("products_made")
        qk_rotated = st.sem("qk_rotated")
        terms_made, scores_made = st.sem("terms_made"), st.sem("scores_made")
        max_made, shifted, exp_made = st.sem("max_made"), st.sem("shifted"), st.sem("exp_made")
        sum_made, over_made = st.sem("sum_made"), st.sem("over_made")
        out_terms_made = st.sem("out_terms_made")
        sums_made = st.sem("sums_made")
        scaled = st.sem("scaled")
        back_ready, back_copied = st.sem("back_ready"), st.sem("back_copied")
        y_ready, y_added = st.sem("y_ready"), st.sem("y_added")
        y_stored = [st.sem("y_stored0"), st.sem("y_stored1")]
        loads = [(wq[:, :, :], Wq.rearrange("(k p) n -> p k n", p=P)), (w_out[:, :, :], Wout.rearrange("(k p) n -> p k n", p=P)),
                 (w_down[:, :, :], Wdown.rearrange("(k p) n -> p k n", p=P)),
                 (b_down[:, :], bdown.rearrange("(p o) -> p o", o=1)),
                 (b_rows[:, 0, :], bq.rearrange("(o n) -> o n", o=1)), (b_rows[:, 1, :], bout.rearrange("(o n) -> o n", o=1)),
                 (cos_sin[:, 0], rotary[0]), (cos_sin[:, 1], rotary[1])]
        for i in range(2):
            loads.append((w_up[0:LATENT, i, :].rearrange("p (h c) -> p h c", c=HD),
                          Wup.rearrange("p (h two c) -> two p h c", two=2, c=HD)[i]))
            loads.append((w_up[LATENT:LATENT + 1, i, :].rearrange("p (h c) -> p h c", c=HD),
                          bup.rearrange("(o h two c) -> two o h c", o=1, two=2, c=HD)[i]))
        W_LOADS = len(loads) * DMA
        block = ctx.enter_context(nc.Block())

        @block.sync
        def _(sp):
            begin_at_one(sp, latent_read, *y_stored, *front.from_one)
            for dst, src in loads:
                sp.dma_start(dst, src).then_inc(w_loaded, DMA)

            def work(n, load_later):
                sp.wait_ge(y_added, n.at(TPC, TPC + 2))
                sp.dma_start(by_chunk(x_out)[n.index], y[:, n.parity]).then_inc(y_stored[n.parity], DMA)
                load_later()

            two_ahead(sp, lambda n: front.load(sp, n), work)
            for b in range(2):
                sp.wait_ge(y_stored[b], 1 + CHUNKS // 2 * DMA)

        @block.gpsimd
        def _(pool):
            front.start_power(pool)
            pool.memset(ones[:, :], 1.0).then_inc(ones_set, 1)
            pool.wait_ge(ones_set, 1)
            pool.memset(latent[LATENT:LATENT + 1, :, :], 1.0).then_inc(ones_set, 1)
            pool.wait_ge(ones_set, 2)
            pool.sem_inc(terms_made, 2)
            pool.sem_inc(out_terms_made, 2)

            def multiply_qk(i):
                pool.wait_ge(qk_rotated, i.at(3))
                pool.wait_ge(scores_made, i.at(1))
                q = qk[:, i.slot, 0:D].rearrange("p (h o d) -> p h o d", o=1, d=HD).broadcast_to([P, H, H, HD])
                k = qk[:, i.slot, D:2 * D].rearrange("p (o g d) -> p o g d", o=1, d=HD).broadcast_to([P, H, H, HD])
                pool.tensor_tensor(score_terms[:, i.slot], q, k, ALU.mult).then_inc(terms_made, 1)
                pool.wait_ge(terms_made, i.at(3))

            def multiply_v(i):
                pool.wait_ge(exp_made, i.at(1))
                pool.wait_ge(v_copied, i.at(3))
                pool.wait_ge(sums_made, i.at(1))
                e = exps[:, i.slot, :, :].rearrange("p h (o g) -> p h o g", o=1).broadcast_to([P, H, HD, H])
                v = v_t[:, i.slot, :, :].rearrange("p (o d) g -> p o d g", o=1).broadcast_to([P, H, HD, H])
                pool.tensor_tensor(out_terms[:, i.slot], e, v, ALU.mult).then_inc(out_terms_made, 1)
                pool.wait_ge(out_terms_made, i.at(3))

            each_tile(pool, [(0, multiply_qk), (1, multiply_v)], lambda n: front.power(pool, n))

        @block.tensor
        def _(pe):
            pe.wait_ge(w_loaded, W_LOADS)
            pe.wait_ge(ones_set, 2)
            pe.sem_inc(back_ready, 2)

            def make_latent(n):
                pe.wait_ge(front.xt_ready, n.past(DK, DK))
                pe.wait_ge(latent_read, n.past(1, 0))
                for k in range(DK):
                    done = pe.matmul(latent_ps[:, :], w_down[:, k, :], front.xt[:, n.parity, k, :],
                                     start=k == 0, stop=k == DK - 1)
                done.then_inc(latent_ready, 1)

            def project_tile(i):
                n, tokens = i.chunk, slice(i.r % TPC * P, (i.r % TPC + 1) * P)
                if i.r % TPC == 0:
                    make_latent(n)
                pe.wait_ge(qk_rotated, i.at(1))
                for k in range(DK):
                    pe.matmul(qk_ps[:, i.slot, 0:D], front.xt[:, n.parity, k, tokens], wq[:, k, :], start=k == 0, stop=False)
                pe.matmul(qk_ps[:, i.slot, 0:D], ones[:, :], b_rows[:, 0, :], start=False, stop=True)
                pe.wait_ge(latent_read, n.past(1, 1))
                pe.matmul(qk_ps[:, i.slot, D:2 * D], latent[:, n.parity, tokens], w_up[:, 0, :],
                          start=True, stop=True).then_inc(qk_ready, 1)
                pe.wait_ge(v_copied, i.at(2))
                pe.matmul(v_ps[:, :], latent[:, n.parity, tokens], w_up[:, 1, :],
                          start=True, stop=True).then_inc(v_ready, 1)

            def turn_back(i):
                pe.wait_ge(scaled, i.at(1))
                pe.wait_ge(back_copied, i.at(2))
                for k in range(DK):
                    done = pe.transpose(back_ps[:, k, :], attended[:, i.slot, k * H // 2:(k + 1) * H // 2, :]
                                        .rearrange("p h d -> p (h d)"), ident[:, :])
                done.then_inc(back_ready, 1)

            def project_out(i):
                pe.wait_ge(back_copied, i.at(3))
                pe.wait_ge(y_added, i.at(2))
                for k in range(DK):
                    pe.matmul(y_ps[:, :], attended_t[:, i.slot, k, :], w_out[:, k, :], start=k == 0, stop=False)
                pe.matmul(y_ps[:, :], ones[:, :], b_rows[:, 1, :], start=False, stop=True).then_inc(y_ready, 1)

            each_tile(pe, [(0, project_tile), (3, project_out), (2, turn_back)], lambda n: front.turn(pe, n))

        @block.scalar
        def _(act):
            act.wait_ge(w_loaded, W_LOADS)
            act.sem_inc(v_copied, 2)
            act.sem_inc(back_copied, 2)

            def copy_latent(n):
                act.wait_ge(latent_ready, n.at(1, 1))
                nc.scalar.activation(latent[0:LATENT, n.parity, :], latent_ps[:, :], ACT.Identity,
                                     bias=b_down[:, 0:1]).then_inc(latent_read, 1)

            def copy_v(i):
                if i.r % TPC == 0:
                    copy_latent(i.chunk)
                act.wait_ge(v_ready, i.at(1))
                act.wait_ge(out_terms_made, i.at(1))
                nc.scalar.copy(v_t[:, i.slot, :, :].rearrange("p d g -> p g d"),
                               v_ps[:, :].rearrange("p (g d) -> p g d", d=HD)).then_inc(v_copied, 1)

            def exponentials(i):
                act.wait_ge(shifted, i.at(1))
                act.wait_ge(out_terms_made, i.at(1))
                nc.scalar.activation(exps[:, i.slot, :, :], scores[:, i.slot, :, :], ACT.Exp,
                                     scale=HD ** -0.5).then_inc(exp_made, 1)

            def copy_back(i):
                act.wait_ge(back_ready, i.at(3))
                nc.scalar.copy(attended_t[:, i.slot, :, :], back_ps[:, :, :]).then_inc(back_copied, 1)

            each_tile(act, [(0, copy_v), (1, exponentials), (2, copy_back)], lambda n: front.copy(act, n))

        @block.vector
        def _(dve):
            dve.wait_ge(w_loaded, W_LOADS)
            dve.sem_inc(qk_rotated, 2)
            dve.sem_inc(scores_made, 2)
            dve.sem_inc(sums_made, 2)
            dve.sem_inc(y_added, 2)

            def rotate(i):
                def halves(t):
                    return t.rearrange("p (h two j) -> p h two j", two=2, j=HD // 2)

                dve.wait_ge(qk_ready, i.at(1))
                dve.wait_ge(qk_rotated, i.at(2))
                both = qk_ps[:, i.slot, :]
                tile = bass.ds(i.turn * TURN + i.r, 1)
                nc.vector.tensor_tensor(rot_a[:, :].rearrange("p (h d) -> p h d", d=HD),
                                        both.rearrange("p (h d) -> p h d", d=HD),
                                        cos_sin[:, 0, tile, :].broadcast_to([P, 2 * H, HD]),
                                        ALU.mult).then_inc(products_made, 1)
                for half in range(2):
                    nc.vector.tensor_tensor(halves(rot_b[:, :])[:, :, half, :], halves(both)[:, :, 1 - half, :],
                                            cos_sin[:, 1, tile, half * HD // 2:(half + 1) * HD // 2]
                                            .broadcast_to([P, 2 * H, HD // 2]),
                                            ALU.mult).then_inc(products_made, 1)
                dve.wait_ge(products_made, i.steps(3, 3))
                dve.wait_ge(terms_made, i.at(1))
                nc.vector.tensor_tensor(qk[:, i.slot, :], rot_a[:, :], rot_b[:, :], ALU.add).then_inc(qk_rotated, 1)

            def shift_scores(i):
                dve.wait_ge(terms_made, i.at(3))
                nc.vector.tensor_reduce(scores[:, i.slot, :, :], score_terms[:, i.slot], AX.X, ALU.add).then_inc(scores_made, 1)
                dve.wait_ge(scores_made, i.at(3))
                nc.vector.tensor_reduce(row_max[:, :], scores[:, i.slot, :, :], AX.X, ALU.max).then_inc(max_made, 1)
                dve.wait_ge(max_made, i.at(1))
                nc.vector.tensor_tensor(scores[:, i.slot, :, :], scores[:, i.slot, :, :],
                                        row_max[:, :].rearrange("p (h o) -> p h o", o=1).broadcast_to([P, H, H]),
                                        ALU.subtract).then_inc(shifted, 1)

            def attend(i):
                dve.wait_ge(exp_made, i.at(1))
                nc.vector.tensor_reduce(row_sum[:, :], exps[:, i.slot, :, :], AX.X, ALU.add).then_inc(sum_made, 1)
                dve.wait_ge(sum_made, i.at(1))
                nc.vector.reciprocal(over[:, :], row_sum[:, :]).then_inc(over_made, 1)
                dve.wait_ge(out_terms_made, i.at(3))
                nc.vector.tensor_reduce(sums[:, :, :], out_terms[:, i.slot], AX.X, ALU.add).then_inc(sums_made, 1)
                dve.wait_ge(over_made, i.at(1))
                dve.wait_ge(sums_made, i.at(3))
                dve.wait_ge(back_ready, i.at(1))
                nc.vector.tensor_tensor(attended[:, i.slot, :, :], sums[:, :, :],
                                        over[:, :].rearrange("p (h o) -> p h o", o=1).broadcast_to([P, H, HD]),
                                        ALU.mult).then_inc(scaled, 1)

            def add_y(i):
                n, t = i.chunk, i.r % TPC
                dve.wait_ge(y_ready, i.at(1))
                if t == 0:
                    dve.wait_ge(y_stored[n.parity], 1 + n.turn * DMA + n.r // 2 * DMA)
                nc.vector.tensor_tensor(y[:, n.parity, t, :], y_ps[:, :], front.raw[:, n.parity, t, :],
                                        ALU.add).then_inc(y_added, 1)

            each_tile(dve, [(0, rotate), (3, add_y), (1, shift_scores), (2, attend)], lambda n: front.normalise(dve, n))


BF_STAGES, PAIRS_BF = 10, 512


def fold_butterflies(nc, sem, ctx, w_exp, b_exp, up_weights, up_bias, w_con_turned, down_weights,
                     dma_sems, w_up_out, bias_out, w_down_out):
    W = 2 * PAIRS_BF
    st = Stage(nc, sem, ctx, "fold")
    rows = [st.sb("rows0", [P, DK, W]), st.sb("rows1", [P, DK, W])]
    line = [st.sb("line0", [1, W]), st.sb("line1", [1, W])]
    product, line_product = st.sb("product", [P, DK, PAIRS_BF]), st.sb("line_product", [1, PAIRS_BF])
    pair_w = [st.sb("pair_w0", [P, PAIRS_BF, 2, 2]), st.sb("pair_w1", [P, PAIRS_BF, 2, 2])]
    last_bias = st.sb("last_bias", [1, W])
    rows_loaded, line_loaded, *pair_loaded, stored = dma_sems
    step = st.sem("step")

    def program(pool):
        done = [0]

        def chained(ins):
            done[0] += 1
            ins.then_inc(step, 1)
            pool.wait_ge(step, done[0])

        def load_pairs(n):
            weights = up_weights[n] if n < BF_STAGES else down_weights[2 * BF_STAGES - 1 - n]
            pool.dma_start(pair_w[n % 2][:, :, :, :].rearrange("p k i j -> p (k i j)"),
                           weights.rearrange("k i j -> (k i j)").partition_broadcast(P)).then_inc(pair_loaded[n % 2], DMA)

        def stage(src, dst, tmp, weights, stride, transposed, count):
            halves = [t.rearrange("p (n two s) -> p n two s", two=2, s=stride) for t in (src, dst)]
            t = tmp.rearrange("p (n s) -> p n s", s=stride)
            w = weights.rearrange("p (n s) i j -> p n s i j", s=stride)
            for i in range(2):
                for j in range(2):
                    wij = w[:, :, :, j, i] if transposed else w[:, :, :, i, j]
                    out = t if j else halves[1][:, :, i, :]
                    chained(pool.tensor_tensor(out, halves[0][:, :, j, :], wij, ALU.mult))
                chained(pool.tensor_tensor(halves[1][:, :, i, :], halves[1][:, :, i, :], t, ALU.add))

        pool.dma_start(rows[0][:, :, :], w_exp.rearrange("(k p) n -> p k n", p=P)).then_inc(rows_loaded, DMA)
        pool.dma_start(line[0][:, :], b_exp.rearrange("(o n) -> o n", o=1)).then_inc(line_loaded, DMA)
        pool.dma_start(last_bias[:, :], up_bias.rearrange("(o n) -> o n", o=1)).then_inc(line_loaded, DMA)
        load_pairs(0)
        load_pairs(1)
        pool.wait_ge(rows_loaded, DMA)
        pool.wait_ge(line_loaded, 2 * DMA)
        for n in range(2 * BF_STAGES):
            down = n >= BF_STAGES
            stride = 1 << (2 * BF_STAGES - 1 - n if down else n)
            if n == BF_STAGES:
                chained(pool.tensor_tensor(line[0][:, :], line[0][:, :], last_bias[:, :], ALU.add))
                pool.dma_start(w_up_out.rearrange("(k p) n -> p k n", p=P), rows[0][:, :, :]).then_inc(stored, DMA)
                pool.dma_start(bias_out.rearrange("(o n) -> o n", o=1), line[0][:, :]).then_inc(stored, DMA)
                pool.wait_ge(stored, 2 * DMA)
                pool.dma_start(rows[0][:, :, :], w_con_turned.rearrange("(k p) n -> p k n", p=P)).then_inc(rows_loaded, DMA)
                pool.wait_ge(rows_loaded, 2 * DMA)
            pool.wait_ge(pair_loaded[n % 2], (n // 2 + 1) * DMA)
            w = pair_w[n % 2][:, :, :, :]
            for k in range(DK):
                stage(rows[n % 2][:, k, :], rows[1 - n % 2][:, k, :], product[:, k, :], w, stride, down, n)
            if not down:
                stage(line[n % 2][:, :], line[1 - n % 2][:, :], line_product[:, :], w[0:1], stride, False, n)
            if n + 2 < 2 * BF_STAGES:
                load_pairs(n + 2)
        pool.dma_start(w_down_out.rearrange("(k p) n -> p k n", p=P), rows[0][:, :, :]).then_inc(stored, DMA)
        pool.wait_ge(stored, 3 * DMA)

    return program


HID0, HID1 = 1024, 768


def run_stage(nc, stage, *args, **kwargs):
    with ExitStack() as ctx:
        used = []

        def sem(name):
            used.append(ctx.enter_context(nc.semaphore(name)))
            return used[-1]

        stage(nc, sem, *args, **kwargs)
        with nc.Block() as block:
            @block.gpsimd
            def _(pool):
                for s in used:
                    pool.sem_clear(s)


def first_attention(nc, sem, ins, by_head, v_cols, heads_out, consts, w_con_t, folded):
    with ExitStack() as ctx:
        beside = fold_butterflies(nc, sem, ctx, ins["L0_ffn_W_exp"], ins["L0_ffn_b_exp"],
                                  ins["L0_ffn_up_weights"], ins["L0_ffn_up_bias"], w_con_t,
                                  ins["L0_ffn_down_weights"], *folded)
        attention(nc, sem, "a0", *by_head, v_cols, heads_out, consts, beside)


def program(nc, ins, out):
    with ExitStack() as ctx:
        def dram(name, shape, dt=F32):
            return nc.dram_tensor(name, shape, dt, kind="Internal").ap()

        ident_bf = ctx.enter_context(nc.sbuf_tensor("ident_bf", [P, P], BF16))
        ident = ctx.enter_context(nc.sbuf_tensor("ident", [P, P], F32))
        mask_first = ctx.enter_context(nc.sbuf_tensor("mask_first", [P, P], BF16))
        mask_second = ctx.enter_context(nc.sbuf_tensor("mask_second", [P, P], BF16))
        consts = (ident_bf, ident, mask_first, mask_second)

        wqkv_t, wo0_t = dram("wqkv_t", [D, 3 * D]), dram("wo0_t", [D, D])
        w1_t = {n: dram(f"w1_{n}_t", [D, D]) for n in "QKVO"}
        w_con_t, w_up0, bias0 = dram("w_con_t", [D, HID0]), dram("w_up0", [D, HID0]), dram("bias0", [HID0])
        w_down0_t, w_down0 = dram("w_down0_t", [D, HID0]), dram("w_down0", [HID0, D])
        w_gate1, w_up1, w_down1 = dram("w_gate1", [D, HID1]), dram("w_up1", [D, HID1]), dram("w_down1", [HID1, D])
        xs = [dram(f"x{i}", [S, D]) for i in range(7)]
        q_parts, k_parts = (dram(n, [PARTS, D, S], BF16) for n in ("q_parts", "k_parts"))
        v_cols = dram("v_cols", [H, P, TILES, VW])
        heads_out = dram("heads_out", [H, HD + 1, S])
        state = dram("state", [2, P, PAIRS, P])
        by_head = [t.rearrange("a (h d) s -> h a d s", d=HD) for t in (q_parts, k_parts)]

        fold_sems = [ctx.enter_context(nc.semaphore(f"fold_{n}"))
                     for n in ("rows_loaded", "line_loaded", "pair_loaded0", "pair_loaded1", "stored")]
        scale = 1.0 / 127.0
        run_stage(nc, set_constants, consts)
        run_stage(nc, turn_weights, "turn", ident, [
            (ins["L0_attn_a_W_qkv"], wqkv_t, None), (ins["L0_attn_a_W_o"], wo0_t, None),
            (ins["L0_ffn_W_con"], w_con_t, None)]
            + [(ins[f"L0_attn_b_W_{n}"], w1_t[n], None) for n in "QKVO"]
            + [(ins["L1_ffn_w_gate"], w_gate1, scale), (ins["L1_ffn_w_up"], w_up1, scale),
               (ins["L1_ffn_w_down"], w_down1, scale)])

        x0 = ins["L0_attn_a_x"].rearrange("b s d -> (b s) d")
        run_stage(nc, project, "p0", x0, ident, q_parts, k_parts, v_cols,
                [wqkv_t[:, i * D:(i + 1) * D] for i in range(3)], rotary=(ins["cos0"], ins["sin0"]))
        run_stage(nc, first_attention, ins, by_head, v_cols, heads_out, consts, w_con_t, (fold_sems, w_up0, bias0, w_down0_t))
        run_stage(nc, turn_weights, "turn2", ident, [(w_down0_t, w_down0, None)])
        run_stage(nc, merge_heads, "m0", x0, xs[0], heads_out, wo0_t)
        ffn0 = dict(hidden=HID0, w_in=w_up0, w_gate=None, w_down=w_down0, in_bias=bias0,
                    out_biases=(ins["L0_ffn_b_con"], ins["L0_ffn_down_bias"]))
        run_stage(nc, feed_forward, "f0", xs[0], xs[1], ident, **ffn0)

        run_stage(nc, project, "p1", xs[1], ident, q_parts, k_parts, v_cols, [w1_t[n] for n in "QKV"])
        run_stage(nc, attention, "a1", *by_head, v_cols, heads_out, consts)
        run_stage(nc, merge_heads, "m1", xs[1], xs[2], heads_out, w1_t["O"])
        run_stage(nc, feed_forward, "f1", xs[2], xs[3], ident, **ffn0)

        run_stage(nc, linear_state, "s2", xs[3], ident, ins["L1_attn_a_Wk"], ins["L1_attn_a_Wv"], state)
        run_stage(nc, linear_output, "o2", xs[3], xs[4], ident, ins["L1_attn_a_Wq"], state, ins["L1_attn_a_Wo"],
                      ins["L1_attn_a_bo"])
        ffn1 = dict(hidden=HID1, w_in=w_up1, w_gate=w_gate1, w_down=w_down1)
        run_stage(nc, feed_forward, "f2", xs[4], xs[5], ident, **ffn1)

        run_stage(nc, attention_over_heads, "a3", xs[5], xs[6], ident,
                  [ins[f"L1_attn_b_{n}"] for n in ("Wq", "bq", "Wdown", "bdown", "Wup", "bup", "Wout", "bout")],
                  (ins["cos1"], ins["sin1"]))
        run_stage(nc, feed_forward, "f3", xs[6], out.rearrange("b s d -> (b s) d"), ident, **ffn1)




def rotary_tables():
    import numpy as np

    theta = np.float32(10000.0) ** (np.arange(0, HD, 2, dtype=np.float32) / np.float32(HD))
    tokens = np.arange(S, dtype=np.float32)
    near = (tokens[:, None] / theta[None, :]).astype(np.float64)
    far = (tokens[:, None] * (np.float32(1.0) / theta)[None, :]).astype(np.float64)
    feature = np.arange(HD)
    sign_near, sign_far = np.where(feature % 2 == 0, -1.0, 1.0), np.where(feature < HD // 2, -1.0, 1.0)
    near, far = near[:, feature // 2], far[:, feature % (HD // 2)]

    def by_feature(t):
        return np.ascontiguousarray(np.tile(t, (1, P // HD)).T.astype(np.float32))

    def by_token(t):
        return np.ascontiguousarray(t.reshape(TILES, P, HD).transpose(1, 0, 2).astype(np.float32))

    return {"cos0": by_feature(np.cos(near)), "sin0": by_feature(np.sin(near) * sign_near),
            "cos1": by_token(np.cos(far)), "sin1": by_token(np.sin(far) * sign_far)}


_INS = [
    "L0_attn_a_x", "L0_attn_a_W_qkv", "L0_attn_a_W_o", "L0_attn_b_W_Q", "L0_attn_b_W_K", "L0_attn_b_W_V",
    "L0_attn_b_W_O", "L0_ffn_W_exp", "L0_ffn_b_exp", "L0_ffn_up_weights", "L0_ffn_up_bias", "L0_ffn_down_weights",
    "L0_ffn_W_con", "L0_ffn_b_con", "L0_ffn_down_bias", "L1_attn_a_Wq", "L1_attn_a_Wk", "L1_attn_a_Wv",
    "L1_attn_a_Wo", "L1_attn_a_bo", "L1_attn_b_Wq", "L1_attn_b_bq", "L1_attn_b_Wdown", "L1_attn_b_bdown",
    "L1_attn_b_Wup", "L1_attn_b_bup", "L1_attn_b_Wout", "L1_attn_b_bout", "L1_ffn_w_gate", "L1_ffn_w_up",
    "L1_ffn_w_down",
]


def kernel(**inputs):
    import concourse.bacc as bacc
    import numpy as np
    from concourse.bass_utils import run_bass_kernel_spmd

    nc = bacc.Bacc("TRN2", target_bir_lowering=False, num_devices=1)
    arrays, ins = {}, {}

    def give(name, a):
        arrays[f"in_{name}_dram"] = a
        ins[name] = nc.dram_tensor(f"in_{name}_dram", a.shape, mybir.dt.from_np(a.dtype), kind="ExternalInput").ap()

    for name in _INS:
        give(name, np.ascontiguousarray(inputs[name]))
    for name, table in rotary_tables().items():
        give(name, table)
    out = nc.dram_tensor("out_0_dram", (1, S, D), F32, kind="ExternalOutput").ap()
    program(nc, ins, out)
    r = run_bass_kernel_spmd(nc, [arrays], core_ids=[0])
    return r.results[0]["out_0_dram"]
```

```python
from contextlib import ExitStack

import concourse.bass as bass
from concourse import mybir

F32 = mybir.dt.float32
BF16 = mybir.dt.bfloat16
I32 = mybir.dt.int32
ACT = mybir.ActivationFunctionType
ALU = mybir.AluOpType
AX = mybir.AxisListType

P = 128
BANK = 512
S = 4096
D = 256
DK = D // P
H = 16
HD = D // H
TILES = S // P
CHUNK = 512
TPC = CHUNK // P
CHUNKS = S // CHUNK
PARTS = 3
ROWS = 6 * HD
VW = 32
MASKED = -1.0e30
LN_EPS = 1e-5
DMA = 16




class Head:

    def __init__(self, turn, r):
        self.turn, self.r = turn, r

    def at(self, per_head, c):
        return self.turn * (3 * per_head) + (self.r * per_head + c)

    def past(self, per_head, c):
        return self.at(per_head, c + 1)

    def filled(self, per_load):
        return self.turn * per_load + (self.r // 3 + 1) * per_load

    def next(self, by):
        return Head(self.turn, self.r + by)

    @property
    def index(self):
        return self.turn * 3 + self.r

    @property
    def slot(self):
        return self.r % 3


def each_head(eng, body, turns, rest):
    with eng.Fori(0, turns) as turn:
        for r in range(3):
            body(Head(turn, r), False)
    for r in range(rest):
        body(Head(turns, r), r == rest - 1)


def begin_at_one(sp, *semaphores):
    for s in semaphores:
        sp.sem_inc(s, 1)


def first_pass_jobs():
    jobs = []
    for qt in range(TILES):
        keys = (qt + 1) * P
        for n, k0 in enumerate(range(0, keys, BANK)):
            width = min(BANK, keys - k0)
            last = k0 + width == keys
            jobs.append((qt, k0, width, qt * P - k0 if last else None, n))
    return jobs


def second_pass_rounds():
    def tiles(c):
        return [(kt, c, max(0, kt * P - c * BANK), kt * P >= c * BANK) for kt in range(4 * c + 4)]

    return list(zip(*[tiles(p) + tiles(S // BANK - 1 - p) for p in range(4)]))


def attention(nc, sem, tag, q_parts, k_parts, v_cols_dram, heads_out, consts, beside=None):
    ident_bf, ident_f, mask_first, mask_second = consts
    jobs = first_pass_jobs()
    rounds = second_pass_rounds()
    J = len(jobs) + 1
    R, T = len(rounds), 4 * len(rounds)
    work = [sum(job[2] for job in jobs[:j + 1]) for j in range(len(jobs))]
    job_end = [sum(w <= work[-1] * min(1.0, (g + 1) / R / 0.88) for w in work) for g in range(R)]
    FS, NS, NE = 3, 3, 8
    COPIES = (max(i for i, tiles in enumerate(rounds) if any(t[1] < 4 for t in tiles)), R - 1)
    LOADED = 7 * DMA

    with ExitStack() as ctx:
        def sb(name, shape, dt):
            return ctx.enter_context(nc.sbuf_tensor(f"{tag}_{name}", shape, dt))

        def ps(name, shape):
            return ctx.enter_context(nc.psum_tensor(f"{tag}_{name}", shape, F32))

        q_rows = sb("q_rows", [P, 3, S], BF16)
        k_rows = sb("k_rows", [P, 3, S], BF16)
        v_cols = sb("v_cols", [P, 3, TILES, VW], F32)
        exps = sb("exps", [P, NE, BANK], F32)
        out_t = sb("out_t", [P, 2, BANK], F32)
        piece_max = sb("piece_max", [P, TILES, S // BANK], F32)
        neg_max = sb("neg_max", [P, TILES], F32)
        shift_hi = sb("shift_hi", [TILES, P], BF16)
        shift_lo = sb("shift_lo", [TILES, P], BF16)
        first_ps = ps("first_ps", [P, FS, BANK])
        second_ps = ps("second_ps", [P, NS, BANK])
        acc_ps = ps("acc_ps", [P, 2, BANK])

        loaded = [sem(f"{tag}_loaded{i}") for i in range(3)]
        constants_set = sem(f"{tag}_constants_set")
        first_ready = sem(f"{tag}_first_ready")
        first_read = sem(f"{tag}_first_read")
        max_ready = sem(f"{tag}_max_ready")
        hi_ready = sem(f"{tag}_hi_ready")
        shift_stored = sem(f"{tag}_shift_stored")
        second_ready = sem(f"{tag}_second_ready")
        exp_ready = sem(f"{tag}_exp_ready")
        pv_done = sem(f"{tag}_pv_done")
        acc_read = sem(f"{tag}_acc_read")
        out_stored = [sem(f"{tag}_out_stored{i}") for i in range(2)]

        block = ctx.enter_context(nc.Block())

        @block.sync
        def _(sp):
            def load(h):
                q, k, n, full = q_rows[:, h.slot, :], k_rows[:, h.slot, :], h.index, loaded[h.slot]
                sp.dma_start(q[0:3 * HD], q_parts[n]).then_inc(full, DMA)
                sp.dma_start(k[0:3 * HD], k_parts[n][0].partition_broadcast(3)).then_inc(full, DMA)
                sp.dma_start(q[3 * HD:5 * HD], q_parts[n][0:2]).then_inc(full, DMA)
                sp.dma_start(k[3 * HD:5 * HD], k_parts[n][1].partition_broadcast(2)).then_inc(full, DMA)
                sp.dma_start(q[5 * HD:6 * HD], q_parts[n][0]).then_inc(full, DMA)
                sp.dma_start(k[5 * HD:6 * HD], k_parts[n][2]).then_inc(full, DMA)
                sp.dma_start(v_cols[:, h.slot], v_cols_dram[n]).then_inc(full, DMA)

            def store_shift(h):
                sp.wait_ge(first_read, h.past(J, J))
                for row, part in ((ROWS, shift_hi), (ROWS + 1, shift_lo)):
                    sp.dma_start(q_rows[row:row + 1, h.slot, :].rearrange("o (t q) -> o t q", t=TILES),
                                 part[:, :]).then_inc(shift_stored, DMA)

            def store_out(h, s):
                sp.wait_ge(acc_read, h.at(2, s + 3))
                for c in range(4):
                    q0, row = (4 * s + c) * BANK, 32 * (3 - c if s else c)
                    sp.dma_start(heads_out[h.index][:, q0:q0 + BANK],
                                 out_t[row:row + HD + 1, s, :]).then_inc(out_stored[s], DMA)

            def step(h, loads, last):
                if loads:
                    sp.wait_ge(pv_done, h.at(T, NE))
                    load(h.next(2))
                store_out(h, 0)
                if not last:
                    store_shift(h.next(1))
                store_out(h, 1)

            sp.sem_inc(acc_read, 2)
            begin_at_one(sp, first_read, shift_stored, *out_stored)
            load(Head(0, 0))
            load(Head(0, 1))
            store_shift(Head(0, 0))
            with sp.Fori(0, 4) as turn:
                for r in range(3):
                    step(Head(turn, r), True, False)
            for r in range(4):
                step(Head(4, r), 12 + r + 2 < H, 12 + r + 1 == H)
            for s in range(2):
                sp.wait_ge(out_stored[s], 1 + H * 4 * DMA)

        @block.gpsimd
        def _(pool):
            pool.memset(piece_max[:, :, :], -3.0e38).then_inc(constants_set, 1)
            pool.wait_ge(constants_set, 1)
            for slot in range(3):
                pool.memset(k_rows[ROWS:ROWS + 2, slot, :], 1.0).then_inc(constants_set, 1)
            pool.wait_ge(constants_set, 4)
            if beside:
                beside(pool)

        @block.tensor
        def _(pe):
            def first_job(h, j):
                qt, k0, width, diagonal, _ = jobs[j]
                pe.wait_ge(first_read, h.past(J, max(0, j - FS + 1)))
                done = pe.matmul(first_ps[:, j % FS, 0:width], q_rows[0:ROWS, h.slot, qt * P:(qt + 1) * P],
                                 k_rows[0:ROWS, h.slot, k0:k0 + width], start=True, stop=diagonal is None)
                if diagonal is not None:
                    done = pe.matmul(first_ps[:, j % FS, diagonal:diagonal + P], ident_bf[:, :], mask_first[:, :],
                                     start=False, stop=True)
                done.then_inc(first_ready, 1)

            def turn_maxima(h):
                pe.wait_ge(max_ready, h.at(1, 1))
                pe.transpose(first_ps[0:TILES, 0, 0:P], neg_max[:, :], ident_f[:, :]).then_inc(first_ready, 1)

            def scores(h, t):
                kt, c, start, masked = rounds[t // 4][t % 4]
                slot, q0 = t % NS, c * BANK
                pe.wait_ge(exp_ready, h.at(T, t + 1))
                done = pe.matmul(second_ps[:, slot, start:BANK], k_rows[0:ROWS + 2, h.slot, kt * P:(kt + 1) * P],
                                 q_rows[0:ROWS + 2, h.slot, q0 + start:q0 + BANK], start=True, stop=not masked)
                if masked:
                    done = pe.matmul(second_ps[:, slot, start:start + P], ident_bf[:, :], mask_second[:, :],
                                     start=False, stop=True)
                done.then_inc(second_ready, 1)

            def times_v(h, g):
                for p, (kt, c, start, _) in enumerate(rounds[g]):
                    if kt == 0 and c in (0, S // BANK - 1):
                        pe.wait_ge(acc_read, h.at(2, 1 + c // 4))
                    pe.wait_ge(exp_ready, h.at(T, NS + 4 * g + p + 1))
                    pe.matmul(acc_ps[32 * p:32 * p + VW, c // 4, start:BANK], v_cols[:, h.slot, kt, :],
                              exps[:, (4 * g + p) % NE, start:BANK], start=kt == 0, stop=kt == 4 * c + 3,
                              tile_position=(0, 32 * p)).then_inc(pv_done, 1)

            def start_second(h):
                pe.wait_ge(shift_stored, h.past(2 * DMA, 2 * DMA))
                for t in range(4):
                    scores(h, t)

            def job_if_due(h, j, due):
                if due:
                    first_job(h, j)
                return j + due

            def step(h, last):
                n, j = h.next(1), len(jobs) + 1 if last else 0
                if not last:
                    pe.wait_ge(loaded[n.slot], n.filled(LOADED))
                for g in range(R):
                    if j == len(jobs):
                        turn_maxima(n)
                        j += 1
                    if g + 1 == R and not last:
                        pe.wait_ge(shift_stored, n.past(2 * DMA, 2 * DMA))
                    m, t0 = (h, 4 * g + 4) if g + 1 < R else (n, 0)
                    for i in range(4):
                        j = job_if_due(n, j, j < job_end[g])
                        if i == 2:
                            times_v(h, g)
                            j = job_if_due(n, j, j < job_end[g])
                        if g + 1 < R or not last:
                            scores(m, t0 + i)
                    while j < job_end[g]:
                        j = job_if_due(n, j, True)

            first = Head(0, 0)
            pe.wait_ge(loaded[0], LOADED)
            for j in range(len(jobs)):
                first_job(first, j)
            turn_maxima(first)
            pe.wait_ge(constants_set, 4)
            start_second(first)
            each_head(pe, step, 5, 1)

        @block.scalar
        def _(act):
            def exponentials(h, g):
                for t, (_, _, start, _) in enumerate(rounds[g], 4 * g):
                    act.wait_ge(second_ready, h.at(T, t + 1))
                    act.wait_ge(pv_done, h.at(T, t + 1))
                    nc.scalar.activation(exps[:, t % NE, start:BANK], second_ps[:, t % NS, start:BANK],
                                         ACT.Exp, scale=HD ** -0.5).then_inc(exp_ready, 1)

            def step(h, last):
                for g in range(R):
                    if g + 1 < R:
                        exponentials(h, g + 1)
                    elif not last:
                        exponentials(h.next(1), 0)
                    if g in COPIES:
                        copy_out(h, g)

            def copy_out(h, g):
                s = COPIES.index(g)
                act.wait_ge(out_stored[s], h.past(4 * DMA, 0))
                act.wait_ge(pv_done, h.at(T, NE + 4 * g + 4))
                nc.scalar.copy(out_t[:, s, :], acc_ps[:, s, :]).then_inc(acc_read, 1)

            act.sem_inc(exp_ready, NS)
            act.sem_inc(pv_done, NE)
            exponentials(Head(0, 0), 0)
            each_head(act, step, 5, 1)

        @block.vector
        def _(dve):
            def step(h, _):
                for j, (qt, _, width, _, piece) in enumerate(jobs):
                    dve.wait_ge(first_ready, h.at(J, j + 1))
                    nc.vector.reduce_max(piece_max[:, qt, piece:piece + 1], first_ps[:, j % FS, 0:width],
                                         AX.X).then_inc(first_read, 1)
                dve.wait_ge(first_read, h.past(J, J - 1))
                nc.vector.tensor_reduce(neg_max[:, :], piece_max[:, :, :], AX.X, ALU.max,
                                        negate=True).then_inc(max_ready, 1)
                dve.wait_ge(first_ready, h.at(J, J))
                dve.wait_ge(shift_stored, h.past(2 * DMA, 0))
                nc.vector.tensor_copy(shift_hi[:, :], first_ps[0:TILES, 0, 0:P]).then_inc(hi_ready, 1)
                dve.wait_ge(hi_ready, h.at(1, 1))
                nc.vector.tensor_tensor(shift_lo[:, :], first_ps[0:TILES, 0, 0:P], shift_hi[:, :],
                                        ALU.subtract).then_inc(first_read, 1)

            dve.wait_ge(constants_set, 1)
            each_head(dve, step, 5, 1)


def set_constants(nc, sem, consts):
    ident_bf, ident_f, mask_first, mask_second = consts
    made = sem("const_made")
    with nc.Block() as block:
        @block.gpsimd
        def _(pool):
            for n, (t, compare, fill, step, channel) in enumerate((
                    (ident_bf, ALU.not_equal, 1.0, -1, 1), (ident_f, ALU.not_equal, 1.0, -1, 1),
                    (mask_first, ALU.is_ge, MASKED, -1, 1), (mask_second, ALU.is_ge, MASKED, 1, -1))):
                pool.memset(t[:, :], 0.0).then_inc(made, 1)
                pool.wait_ge(made, 2 * n + 1)
                pool.affine_select(out=t[:, :], in_=t[:, :], compare_op=compare, fill=fill, base=0,
                                   pattern=[[step, P]], channel_multiplier=channel).then_inc(made, 1)
                pool.wait_ge(made, 2 * n + 2)




class Chunk:

    def __init__(self, turn, parity):
        self.turn, self.r = turn, parity

    def at(self, per_chunk, c):
        return self.turn * (2 * per_chunk) + (self.r * per_chunk + c)

    def past(self, per_chunk, c):
        return self.at(per_chunk, c + 1)

    def next(self):
        return Chunk(self.turn, self.r + 1)

    @property
    def index(self):
        return self.turn * 2 + self.r

    @property
    def parity(self):
        return self.r % 2


def nothing(*_, **__):
    pass


def each_chunk(eng, ahead, work, before=None, ready=nothing):
    def step(n):
        if before:
            before(n.next())
        work(n, lambda: ahead(n.next()))

    if before:
        before(Chunk(0, 0))
    ahead(Chunk(0, 0))
    ready()
    with eng.Fori(0, CHUNKS // 2 - 1) as turn:
        for r in range(2):
            step(Chunk(turn, r))
    step(Chunk(CHUNKS // 2 - 1, 0))
    work(Chunk(CHUNKS // 2 - 1, 1), nothing)


def two_ahead(eng, load, work, load_once=nothing):
    load(Chunk(0, 0))
    load_once()
    load(Chunk(0, 1))
    with eng.Fori(0, CHUNKS // 2 - 1) as turn:
        for r in range(2):
            work(Chunk(turn, r), lambda n=Chunk(turn, r + 2), **what: load(n, **what))
    for r in range(2):
        work(Chunk(CHUNKS // 2 - 1, r), nothing)


class Stage:

    def __init__(self, nc, sem, ctx, tag):
        self.nc, self.ctx, self.tag, self.new_sem = nc, ctx, tag, sem

    def sb(self, name, shape, dt=F32):
        return self.ctx.enter_context(self.nc.sbuf_tensor(f"{self.tag}_{name}", shape, dt))

    def ps(self, name, shape):
        return self.ctx.enter_context(self.nc.psum_tensor(f"{self.tag}_{name}", shape, F32))

    def sem(self, name):
        return self.new_sem(f"{self.tag}_{name}")


def by_chunk(x):
    return x.rearrange("(n t p) d -> n p t d", t=TPC, p=P)


class Normed:

    def __init__(self, st, x, ident):
        self.st, self.nc, self.x, self.ident = st, st.nc, by_chunk(x), ident
        self.raw = st.sb("raw", [P, 2, TPC, D])
        self.normed = st.sb("normed", [P, TPC, D])
        self.stats = st.sb("stats", [P, TPC, 6])
        self.moments = st.sb("moments", [P, TPC, 2])
        self.variance = st.sb("variance", [P, TPC])
        self.inverse = st.sb("inverse", [P, TPC])
        self.power_of = st.sb("power_of", [P, TPC])
        self.xt = st.sb("xt", [P, 2, DK, CHUNK])
        self.turned_ps = st.ps("turned_ps", [P, DK, CHUNK])
        self.x_loaded = [st.sem("x_loaded0"), st.sem("x_loaded1")]
        self.stats_ready = st.sem("stats_ready")
        self.passed = st.sem("passed")
        self.moments_ready = st.sem("moments_ready")
        self.variance_ready = st.sem("variance_ready")
        self.inverse_ready = st.sem("inverse_ready")
        self.normed_ready = st.sem("normed_ready")
        self.turned_ready = st.sem("turned_ready")
        self.xt_ready = st.sem("xt_ready")
        self.from_one = (self.normed_ready, self.turned_ready, self.xt_ready)

    def load(self, sp, n):
        sp.dma_start(self.raw[:, n.parity], self.x[n.index]).then_inc(self.x_loaded[n.parity], DMA)

    def start_power(self, pool):
        pool.memset(self.power_of[:, :], -0.5).then_inc(self.inverse_ready, 1)
        pool.wait_ge(self.inverse_ready, 1)

    def power(self, pool, n):
        pool.wait_ge(self.variance_ready, n.at(1, 1))
        pool.tensor_tensor(self.inverse[:, :], self.variance[:, :], self.power_of[:, :],
                           ALU.pow).then_inc(self.inverse_ready, 1)

    def normalise(self, dve, n):
        self.find_moments(dve, n)
        self.finish_normalise(dve, n)

    def find_moments(self, dve, n):
        raw = self.raw[:, n.parity]
        dve.wait_ge(self.x_loaded[n.parity], n.turn * DMA + (n.r // 2 + 1) * DMA)
        for t in range(TPC):
            self.nc.vector.bn_stats(self.stats[:, t, :], raw[:, t, :]).then_inc(self.stats_ready, 1)
        dve.wait_ge(self.stats_ready, n.at(TPC, TPC))
        dve.sem_inc(self.passed, 1)
        for t in range(TPC):
            self.nc.vector.bn_aggr(self.moments[:, t, :], self.stats[:, t, :]).then_inc(self.moments_ready, 1)
        dve.wait_ge(self.moments_ready, n.at(TPC, TPC))
        self.nc.vector.tensor_scalar(self.variance[:, :], self.moments[:, :, 1], LN_EPS, None,
                                     ALU.add).then_inc(self.variance_ready, 1)

    def finish_normalise(self, dve, n):
        raw = self.raw[:, n.parity]
        dve.wait_ge(self.inverse_ready, n.at(1, 2))
        dve.wait_ge(self.turned_ready, n.past(DK, 0))
        for t in range(TPC):
            self.nc.vector.tensor_scalar(self.normed[:, t, :], raw[:, t, :], self.moments[:, t, 0:1],
                                         self.inverse[:, t:t + 1], ALU.subtract, ALU.mult).then_inc(self.normed_ready, 1)

    def turn(self, pe, n):
        pe.wait_ge(self.normed_ready, n.past(TPC, TPC))
        pe.wait_ge(self.xt_ready, n.past(DK, 0))
        for k in range(DK):
            for t in range(TPC):
                done = pe.transpose(self.turned_ps[:, k, t * P:(t + 1) * P], self.normed[:, t, k * P:(k + 1) * P],
                                    self.ident[:, :])
            done.then_inc(self.turned_ready, 1)

    def copy(self, act, n):
        for k in range(DK):
            act.wait_ge(self.turned_ready, n.past(DK, k + 1))
            self.nc.scalar.copy(self.xt[:, n.parity, k, :], self.turned_ps[:, k, :]).then_inc(self.xt_ready, 1)


def turn_weights(nc, sem, tag, ident, matrices):
    pieces = []
    for src, dst, factor in matrices:
        rows, cols = src.shape
        for r in range(0, rows, P):
            for c in range(0, cols, D):
                pieces.append((src[r:r + P, c:c + D],
                               dst[c:c + D, r:r + P].rearrange("(k p) r -> p k r", p=P), factor))
    with ExitStack() as ctx:
        st = Stage(nc, sem, ctx, tag)
        N = 4
        raw = [st.sb(f"raw{i}", [P, D]) for i in range(N)]
        raw_int = [st.sb(f"raw_int{i}", [P, D], I32) for i in range(N)]
        turned = st.sb("turned", [P, N, DK, P])
        turned_ps = st.ps("turned_ps", [P, N, BANK])
        piece_loaded = [st.sem(f"piece_loaded{i}") for i in range(N)]
        dequantised, turned_ready, copied = st.sem("dequantised"), st.sem("turned_ready"), st.sem("copied")
        stored = [st.sem(f"stored{i}") for i in range(N)]
        quantised = [sum(f is not None for _, _, f in pieces[:i]) for i in range(len(pieces) + 1)]
        block = ctx.enter_context(nc.Block())

        @block.sync
        def _(sp):
            for i, (src, _, factor) in enumerate(pieces):
                if i >= N:
                    sp.wait_ge(turned_ready, i - N + 1)
                sp.dma_start((raw if factor is None else raw_int)[i % N][:, :], src).then_inc(piece_loaded[i % N], DMA)

        @block.vector
        def _(dve):
            for i, (_, _, factor) in enumerate(pieces):
                if factor is not None:
                    dve.wait_ge(piece_loaded[i % N], (i // N + 1) * DMA)
                    if i >= N:
                        dve.wait_ge(turned_ready, i - N + 1)
                    nc.vector.tensor_scalar(raw[i % N][:, :], raw_int[i % N][:, :], factor, None,
                                            ALU.mult).then_inc(dequantised, 1)

        @block.tensor
        def _(pe):
            for i, (_, _, factor) in enumerate(pieces):
                if factor is None:
                    pe.wait_ge(piece_loaded[i % N], (i // N + 1) * DMA)
                else:
                    pe.wait_ge(dequantised, quantised[i + 1])
                if i >= N:
                    pe.wait_ge(copied, i - N + 1)
                for k in range(DK):
                    done = pe.transpose(turned_ps[:, i % N, k * P:(k + 1) * P], raw[i % N][:, k * P:(k + 1) * P],
                                        ident[:, :])
                done.then_inc(turned_ready, 1)

        @block.scalar
        def _(act):
            for i, (_, dst, _) in enumerate(pieces):
                act.wait_ge(turned_ready, i + 1)
                if i >= N:
                    act.wait_ge(stored[i % N], (i // N) * DMA)
                nc.scalar.copy(turned[:, i % N].rearrange("p k r -> p (k r)"),
                               turned_ps[:, i % N, 0:D]).then_inc(copied, 1)
                act.wait_ge(copied, i + 1)
                act.dma_start(dst, turned[:, i % N]).then_inc(stored[i % N], DMA)
            for i in range(N):
                act.wait_ge(stored[i], len(range(i, len(pieces), N)) * DMA)


def swapped_columns(nc, eng, dst, src, done):
    a, b = (t.rearrange("p (g two) -> p g two", two=2) for t in (src, dst))
    for half in range(2):
        eng.tensor_copy(b[:, :, half], a[:, :, 1 - half]).then_inc(done, 1)


def project(nc, sem, tag, x, ident, q_parts, k_parts, v_cols_dram, weights, rotary=None):
    with ExitStack() as ctx:
        st = Stage(nc, sem, ctx, tag)
        front = Normed(st, x, ident)
        wq, wk, wv = (st.sb(n, [P, DK, D]) for n in ("wq", "wk", "wv"))
        partner_w = rotary is not None
        if partner_w:
            wq_partner = st.sb("wq_partner", [P, DK, D])
            wk_partner = st.sb("wk_partner", [P, DK, D])
            cos_sin = st.sb("cos_sin", [P, 2, 2, CHUNK])
        rot_a = st.sb("rot_a", [P, 2, CHUNK])
        rot_b = st.sb("rot_b", [P, 2, CHUNK])
        value = st.sb("value", [P, 2, CHUNK])
        rest = st.sb("rest", [P, 2, CHUNK])
        parts = st.sb("parts", [P, 2, PARTS, CHUNK], BF16)
        v_tiles = st.sb("v_tiles", [P, H, TPC, VW])
        pair_ps = st.ps("pair_ps", [P, 2, 2, BANK])
        v_ps = st.ps("v_ps", [P, 2, BANK])
        w_loaded, w_made = st.sem("w_loaded"), st.sem("w_made")
        v_tiles_set = st.sem("v_tiles_set")
        table_loaded = [st.sem("table_loaded0"), st.sem("table_loaded1")]
        pair_ready, pair_read = st.sem("pair_ready"), st.sem("pair_read")
        v_ready, v_read = st.sem("v_ready"), st.sem("v_read")
        v_stored = st.sem("v_stored")
        passed = [st.sem(f"passed{i}") for i in range(3)]
        cut_step = [st.sem("cut_step0"), st.sem("cut_step1")]
        cut_done = [st.sem("cut_done0"), st.sem("cut_done1")]
        parts_stored = [st.sem("parts_stored0"), st.sem("parts_stored1")]
        UNITS = [(0, 0), (0, 1), (1, 0), (1, 1)]
        W_LOADS, W_MADE = 3 * DMA, 8 if partner_w else 0
        CUT = 4
        block = ctx.enter_context(nc.Block())

        @block.sync
        def _(sp):
            begin_at_one(sp, v_stored, *parts_stored, *cut_done, *front.from_one)

            def load_weights():
                for w, src in zip((wq, wk, wv), weights):
                    sp.dma_start(w[:, :, :], src.rearrange("(k p) n -> p k n", p=P)).then_inc(w_loaded, DMA)

            def load(n, values=True, table=partner_w):
                if values:
                    front.load(sp, n)
                if table:
                    for i in range(2):
                        sp.dma_start(cos_sin[:, n.parity, i, :], rotary[i].rearrange("p (n s) -> n p s", s=CHUNK)[n.index]
                                     ).then_inc(table_loaded[n.parity], DMA)

            def work(n, load_later):
                sp.wait_ge(front.normed_ready, n.past(TPC, TPC))
                load_later(table=False)
                sp.wait_ge(v_read, n.at(2, 4))
                sp.dma_start(v_cols_dram.rearrange("h p (n t) c -> n p h (t c)", t=TPC)[n.index],
                             v_tiles[:, :, :, :].rearrange("p h t c -> p h (t c)")).then_inc(v_stored, DMA)
                for u, (kind, m) in enumerate(UNITS):
                    b = u % 2
                    sp.wait_ge(cut_done[b], n.past(2, u // 2 + 1))
                    sp.sem_inc(passed[2], 1)
                    dst = (q_parts, k_parts)[kind].rearrange("a (m p) (n s) -> n m p a s", p=P, s=CHUNK)[n.index][m]
                    sp.dma_start(dst, parts[:, b]).then_inc(parts_stored[b], DMA)
                if partner_w:
                    sp.wait_ge(pair_read, n.at(4, 6))
                    load_later(values=False)

            two_ahead(sp, load, work, load_weights)
            sp.wait_ge(v_stored, 1 + CHUNKS * DMA)
            for b in range(2):
                sp.wait_ge(parts_stored[b], 1 + CHUNKS * 2 * DMA)

        def cut(eng, n, u):
            b = u % 2
            step = cut_step[b]
            if partner_w:
                eng.wait_ge(pair_read, n.at(4, u + 3))
                eng.tensor_tensor(value[:, b], rot_a[:, b], rot_b[:, b], ALU.add).then_inc(step, 1)
                eng.wait_ge(step, n.at(2 * CUT, CUT * (u // 2) + 1))
            else:
                eng.wait_ge(pair_read, n.at(4, u + 3))
            eng.wait_ge(parts_stored[b], n.past(2 * DMA, u // 2 * DMA))
            base = 1 if partner_w else 0
            eng.sem_inc(passed[b], 1)
            eng.tensor_copy(parts[:, b, 0], value[:, b]).then_inc(step, 1)
            eng.wait_ge(step, n.at(2 * CUT, CUT * (u // 2) + base + 1))
            eng.tensor_tensor(rest[:, b], value[:, b], parts[:, b, 0], ALU.subtract).then_inc(step, 1)
            eng.wait_ge(step, n.at(2 * CUT, CUT * (u // 2) + base + 2))
            eng.sem_inc(passed[b], 1)
            eng.tensor_copy(parts[:, b, 1], rest[:, b]).then_inc(step, 1 if partner_w else 2)
            eng.wait_ge(step, n.at(2 * CUT, CUT * (u // 2) + CUT))
            eng.tensor_tensor(parts[:, b, 2], rest[:, b], parts[:, b, 1], ALU.subtract).then_inc(cut_done[b], 1)

        @block.gpsimd
        def _(pool):
            front.start_power(pool)
            pool.memset(v_tiles[:, :, :, HD:VW], 0.0).then_inc(v_tiles_set, 1)
            pool.wait_ge(v_tiles_set, 1)
            pool.memset(v_tiles[:, :, :, HD:HD + 1], 1.0).then_inc(v_tiles_set, 1)
            pool.wait_ge(v_tiles_set, 2)

            def work(n, ahead_next):
                ahead_next()
                cut(pool, n, 1)

            each_chunk(pool, lambda n: front.power(pool, n), work)

        @block.tensor
        def _(pe):
            def weights_ready():
                pe.wait_ge(w_loaded, W_LOADS)
                if W_MADE:
                    pe.wait_ge(w_made, W_MADE)

            def work(n, ahead_next):
                xt = front.xt[:, n.parity]
                pe.wait_ge(front.xt_ready, n.past(DK, DK))
                for i in range(2):
                    pe.wait_ge(v_read, n.at(2, i + 1))
                    for j in range(2):
                        t = 2 * i + j
                        for k in range(DK):
                            done = pe.matmul(v_ps[:, i, j * D:(j + 1) * D], xt[:, k, t * P:(t + 1) * P], wv[:, k, :],
                                             start=k == 0, stop=k == DK - 1)
                    done.then_inc(v_ready, 1)
                for u in range(4):
                    if u == 3:
                        ahead_next()
                    pair(n, u, xt)

            def pair(n, u, xt):
                kind, m = UNITS[u]
                pe.wait_ge(pair_read, n.at(4, u + 1))
                w = [(wq, wk)[kind]] + ([(wq_partner, wk_partner)[kind]] if partner_w else [])
                for i, wi in enumerate(w):
                    for k in range(DK):
                        done = pe.matmul(pair_ps[:, u % 2, i, :], wi[:, k, m * P:(m + 1) * P], xt[:, k, :],
                                         start=k == 0, stop=k == DK - 1)
                done.then_inc(pair_ready, 1)

            each_chunk(pe, lambda n: front.turn(pe, n), work, ready=weights_ready)

        @block.scalar
        def _(act):
            act.wait_ge(v_tiles_set, 2)
            act.sem_inc(pair_read, 2)
            act.sem_inc(v_read, 2)

            def work(n, ahead_next):
                act.wait_ge(v_stored, n.past(DMA, 0))
                for i in range(2):
                    act.wait_ge(v_ready, n.at(2, i + 1))
                    nc.scalar.copy(v_tiles[:, :, 2 * i:2 * i + 2, 0:HD].rearrange("p h t c -> p t h c"),
                                   v_ps[:, i, :].rearrange("p (t h c) -> p t h c", t=2, h=H)).then_inc(v_read, 1)
                if not partner_w:
                    for u in range(4):
                        b = u % 2
                        if u == 3:
                            ahead_next()
                        act.wait_ge(pair_ready, n.at(4, u + 1))
                        act.wait_ge(cut_done[b], n.past(2, u // 2))
                        nc.scalar.copy(value[:, b], pair_ps[:, b, 0, :]).then_inc(pair_read, 1)
                else:
                    ahead_next()

            each_chunk(act, lambda n: front.copy(act, n), work)

        @block.vector
        def _(dve):
            def make_partners():
                dve.wait_ge(w_loaded, W_LOADS)
                for k in range(DK):
                    swapped_columns(nc, nc.vector, wq_partner[:, k, :], wq[:, k, :], w_made)
                    swapped_columns(nc, nc.vector, wk_partner[:, k, :], wk[:, k, :], w_made)

            def work(n, ahead_next):
                for u, (kind, m) in enumerate(UNITS):
                    b = u % 2
                    if partner_w:
                        dve.wait_ge(pair_ready, n.at(4, u + 1))
                        dve.wait_ge(cut_done[b], n.past(2, u // 2))
                        if u == 0:
                            dve.wait_ge(table_loaded[n.parity], n.turn * 2 * DMA + (n.r // 2 + 1) * 2 * DMA)
                        for i, rot in enumerate((rot_a, rot_b)):
                            table = cos_sin[:, n.parity, i, :]
                            done = nc.vector.tensor_tensor(rot[:, b], pair_ps[:, b, i, :], table, ALU.mult)
                        done.then_inc(pair_read, 1)
                    if u == 1:
                        ahead_next()
                    if u != 1:
                        cut(dve, n, u)

            dve.wait_ge(v_tiles_set, 2)
            each_chunk(dve, lambda n: front.finish_normalise(dve, n), work, before=lambda n: front.find_moments(dve, n),
                       ready=make_partners if partner_w else nothing)


def merge_heads(nc, sem, tag, x, x_out, heads_out, w_out):
    with ExitStack() as ctx:
        st = Stage(nc, sem, ctx, tag)
        w = st.sb("w", [P, DK, D])
        spread = st.sb("spread", [H, DK, P])
        raw = st.sb("raw", [P, 2, TPC, D])
        rows = st.sb("rows", [P, 2, DK, CHUNK])
        sums = st.sb("sums", [H, 2, CHUNK])
        over = st.sb("over", [H, CHUNK])
        scaled = st.sb("scaled", [P, 2, DK, CHUNK])
        y = st.sb("y", [P, 2, TPC, D])
        over_ps = st.ps("over_ps", [P, DK, BANK])
        y_ps = st.ps("y_ps", [P, 2, BANK])
        w_loaded, spread_set = st.sem("w_loaded"), st.sem("spread_set")
        loaded = [st.sem("loaded0"), st.sem("loaded1")]
        over_ready, spread_ready, scaled_ready = st.sem("over_ready"), st.sem("spread_ready"), st.sem("scaled_ready")
        y_ready, y_added = st.sem("y_ready"), st.sem("y_added")
        y_stored = [st.sem("y_stored0"), st.sem("y_stored1")]
        x_loaded = [st.sem("x_loaded0"), st.sem("x_loaded1")]
        LOADS = 3 * DMA
        block = ctx.enter_context(nc.Block())

        @block.sync
        def _(sp):
            begin_at_one(sp, scaled_ready, spread_ready, y_added, *y_stored)

            def load_weights():
                sp.dma_start(w[:, :, :], w_out.rearrange("(k p) n -> p k n", p=P)).then_inc(w_loaded, DMA)

            def load(n, attended=True, residual=True):
                full = loaded[n.parity]
                if attended:
                    cut = heads_out.rearrange("h r (n s) -> n h r s", s=CHUNK)[n.index]
                    for m in range(DK):
                        sp.dma_start(rows[:, n.parity, m, :], cut[m * H // 2:(m + 1) * H // 2, 0:HD, :]).then_inc(full, DMA)
                    sp.dma_start(sums[:, n.parity, :], cut[:, HD, :]).then_inc(full, DMA)
                if residual:
                    sp.dma_start(raw[:, n.parity], by_chunk(x)[n.index]).then_inc(x_loaded[n.parity], DMA)

            def work(n, load_later):
                sp.wait_ge(scaled_ready, n.past(DK, DK))
                load_later(residual=False)
                sp.wait_ge(y_added, n.past(2, 2))
                sp.dma_start(by_chunk(x_out)[n.index], y[:, n.parity]).then_inc(y_stored[n.parity], DMA)
                load_later(attended=False)

            two_ahead(sp, load, work, load_weights)
            for b in range(2):
                sp.wait_ge(y_stored[b], 1 + CHUNKS // 2 * DMA)

        @block.gpsimd
        def _(pool):
            pool.memset(spread[:, :, :], 1.0).then_inc(spread_set, 1)
            pool.wait_ge(spread_set, 1)
            flat = spread[:, :, :].rearrange("h m p -> h (m p)")
            pool.affine_select(out=flat, in_=flat, compare_op=ALU.is_ge, fill=0.0, base=0,
                               pattern=[[1, D]], channel_multiplier=-HD).then_inc(spread_set, 1)
            pool.wait_ge(spread_set, 2)
            pool.affine_select(out=flat, in_=flat, compare_op=ALU.is_ge, fill=0.0, base=HD - 1,
                               pattern=[[-1, D]], channel_multiplier=HD).then_inc(spread_set, 1)
            pool.wait_ge(spread_set, 3)

        @block.tensor
        def _(pe):
            pe.wait_ge(spread_set, 3)

            def ahead(n):
                pe.wait_ge(over_ready, n.at(1, 1))
                pe.wait_ge(scaled_ready, n.past(DK, 0))
                for m in range(DK):
                    pe.matmul(over_ps[:, m, :], spread[:, m, :], over[:, :], start=True,
                              stop=True).then_inc(spread_ready, 1)

            def work(n, ahead_next):
                pe.wait_ge(scaled_ready, n.past(DK, DK))
                pe.wait_ge(y_added, n.past(2, 0))
                for i in range(2):
                    if i == 1:
                        ahead_next()
                    for j in range(2):
                        t = 2 * i + j
                        for m in range(DK):
                            done = pe.matmul(y_ps[:, i, j * D:(j + 1) * D], scaled[:, n.parity, m, t * P:(t + 1) * P],
                                             w[:, m, :], start=m == 0, stop=m == DK - 1)
                    done.then_inc(y_ready, 1)

            each_chunk(pe, ahead, work, ready=lambda: pe.wait_ge(w_loaded, DMA))

        @block.vector
        def _(dve):
            def ahead(n):
                dve.wait_ge(loaded[n.parity], n.turn * LOADS + (n.r // 2 + 1) * LOADS)
                dve.wait_ge(spread_ready, n.past(DK, 0))
                nc.vector.reciprocal(over[:, :], sums[:, n.parity, :]).then_inc(over_ready, 1)
                for m in range(DK):
                    dve.wait_ge(spread_ready, n.past(DK, m + 1))
                    nc.vector.tensor_tensor(scaled[:, n.parity, m, :], over_ps[:, m, :], rows[:, n.parity, m, :],
                                            ALU.mult).then_inc(scaled_ready, 1)

            def work(n, ahead_next):
                ahead_next()
                dve.wait_ge(y_stored[n.parity], 1 + n.turn * DMA + n.r // 2 * DMA)
                dve.wait_ge(x_loaded[n.parity], n.turn * DMA + (n.r // 2 + 1) * DMA)
                for i in range(2):
                    dve.wait_ge(y_ready, n.at(2, i + 1))
                    nc.vector.tensor_tensor(y[:, n.parity, 2 * i:2 * i + 2, :].rearrange("p t d -> p (t d)"), y_ps[:, i, :],
                                            raw[:, n.parity, 2 * i:2 * i + 2, :].rearrange("p t d -> p (t d)"),
                                            ALU.add).then_inc(y_added, 1)

            each_chunk(dve, ahead, work)


def feed_forward(nc, sem, tag, x, x_out, ident, hidden, w_in, w_gate, w_down, in_bias=None, out_biases=()):
    M = hidden // P
    gated = w_gate is not None
    with ExitStack() as ctx:
        st = Stage(nc, sem, ctx, tag)
        front = Normed(st, x, ident)
        wi = st.sb("wi", [P, DK, hidden])
        wg = st.sb("wg", [P, DK, hidden if gated else 1])
        wd = st.sb("wd", [P, M, D])
        bias_in = st.sb("bias_in", [P, M])
        bias_out = st.sb("bias_out", [P, 2, 2 * D])
        act_t = st.sb("act_t", [P, M, CHUNK])
        silu_t = st.sb("silu_t", [P, 2, CHUNK])
        y = st.sb("y", [P, 2, TPC, D])
        G = 2 if gated else 1
        up_ps = st.ps("up_ps", [P, 2, G, BANK])
        y_ps = st.ps("y_ps", [P, 2, BANK])
        w_loaded, bias_added = st.sem("w_loaded"), st.sem("bias_added")
        up_ready, act_ready = st.sem("up_ready"), st.sem("act_ready")
        silu_ready = st.sem("silu_ready")
        y_ready, y_added = st.sem("y_ready"), st.sem("y_added")
        biased = st.sem("biased")
        y_stored = [st.sem("y_stored0"), st.sem("y_stored1")]
        loads = [(wi[:, :, :], w_in.rearrange("(k p) n -> p k n", p=P)), (wd[:, :, :], w_down.rearrange("(k p) n -> p k n", p=P))]
        if gated:
            loads.append((wg[:, :, :], w_gate.rearrange("(k p) n -> p k n", p=P)))
        else:
            loads.append((bias_in[:, :], in_bias.rearrange("(m p) -> p m", p=P)))
        for i, b in enumerate(out_biases):
            loads.append((bias_out[:, i, 0:D], b.partition_broadcast(P)))
            loads.append((bias_out[:, i, D:2 * D], b.partition_broadcast(P)))
        W_LOADS = len(loads) * DMA
        block = ctx.enter_context(nc.Block())

        @block.sync
        def _(sp):
            begin_at_one(sp, y_added, *y_stored, *front.from_one)

            def load_weights():
                with nc.allow_non_contiguous_dma(reason="1024 bias values by partition"):
                    for dst, src in loads:
                        sp.dma_start(dst, src).then_inc(w_loaded, DMA)

            def work(n, load_later):
                sp.wait_ge(y_added, n.past(2, 2))
                sp.dma_start(by_chunk(x_out)[n.index], y[:, n.parity]).then_inc(y_stored[n.parity], DMA)
                load_later()

            two_ahead(sp, lambda n: front.load(sp, n), work, load_weights)
            for b in range(2):
                sp.wait_ge(y_stored[b], 1 + CHUNKS // 2 * DMA)

        @block.gpsimd
        def _(pool):
            front.start_power(pool)

            def add_biases():
                pool.wait_ge(w_loaded, W_LOADS)
                pool.tensor_tensor(bias_out[:, 0, :], bias_out[:, 0, :], bias_out[:, 1, :], ALU.add).then_inc(bias_added, 1)
                pool.wait_ge(bias_added, 1)

            def work(n, ahead_next):
                ahead_next()
                if out_biases:
                    pool.wait_ge(front.normed_ready, n.past(TPC, TPC))
                    flat_x = front.raw[:, n.parity].rearrange("p (i t) d -> p i (t d)", i=2)
                    for i in range(2):
                        pool.tensor_tensor(flat_x[:, i, :], flat_x[:, i, :], bias_out[:, 0, :], ALU.add).then_inc(biased, 1)
                        pool.wait_ge(biased, n.at(2, i + 1))

            each_chunk(pool, lambda n: front.power(pool, n), work, ready=add_biases if out_biases else nothing)

        @block.tensor
        def _(pe):
            def work(n, ahead_next):
                xt = front.xt[:, n.parity]
                pe.wait_ge(front.xt_ready, n.past(DK, DK))
                for m in range(M):
                    pe.wait_ge(act_ready, n.at(M, m + 1))
                    for g, w in enumerate((wg, wi) if gated else (wi,)):
                        for k in range(DK):
                            done = pe.matmul(up_ps[:, m % 2, g, :], w[:, k, m * P:(m + 1) * P], xt[:, k, :],
                                             start=k == 0, stop=k == DK - 1)
                    done.then_inc(up_ready, 1)
                ahead_next()
                pe.wait_ge(y_added, n.past(2, 0))
                for i in range(2):
                    for j in range(2):
                        t = 2 * i + j
                        for m in range(M):
                            if i == 0 and j == 0:
                                pe.wait_ge(act_ready, n.at(M, m + 3))
                            done = pe.matmul(y_ps[:, i, j * D:(j + 1) * D], act_t[:, m, t * P:(t + 1) * P], wd[:, m, :],
                                             start=m == 0, stop=m == M - 1)
                    done.then_inc(y_ready, 1)

            each_chunk(pe, lambda n: front.turn(pe, n), work, ready=lambda: pe.wait_ge(w_loaded, W_LOADS))

        @block.scalar
        def _(act):
            act.sem_inc(act_ready, 2)

            def work(n, ahead_next):
                for m in range(M):
                    act.wait_ge(up_ready, n.at(M, m + 1))
                    if gated:
                        act.wait_ge(act_ready, n.at(M, m + 1))
                        nc.scalar.activation(silu_t[:, m % 2, :], up_ps[:, m % 2, 0, :], ACT.Silu).then_inc(silu_ready, 1)
                    else:
                        nc.scalar.activation(act_t[:, m, :], up_ps[:, m % 2, 0, :], ACT.Gelu,
                                             bias=bias_in[:, m:m + 1]).then_inc(act_ready, 1)
                ahead_next()

            each_chunk(act, lambda n: front.copy(act, n), work, ready=lambda: act.wait_ge(w_loaded, W_LOADS))

        @block.vector
        def _(dve):
            def work(n, ahead_next):
                for m in range(M if gated else 0):
                    if m == M - 2:
                        ahead_next()
                    dve.wait_ge(silu_ready, n.at(M, m + 1))
                    nc.vector.tensor_tensor(act_t[:, m, :], up_ps[:, m % 2, 1, :], silu_t[:, m % 2, :],
                                            ALU.mult).then_inc(act_ready, 1)
                if not gated:
                    ahead_next()
                if out_biases:
                    dve.wait_ge(biased, n.at(2, 2))
                dve.wait_ge(y_stored[n.parity], 1 + n.turn * DMA + n.r // 2 * DMA)
                for i in range(2):
                    dve.wait_ge(y_ready, n.at(2, i + 1))
                    nc.vector.tensor_tensor(y[:, n.parity, 2 * i:2 * i + 2, :].rearrange("p t d -> p (t d)"), y_ps[:, i, :],
                                            front.raw[:, n.parity, 2 * i:2 * i + 2, :].rearrange("p t d -> p (t d)"),
                                            ALU.add).then_inc(y_added, 1)

            each_chunk(dve, lambda n: front.normalise(dve, n), work)


HL, EL = 16, 64
WL = HL * EL
PAIRS = WL // P
Z_EPS = 1e-6


def linear_state(nc, sem, tag, x, ident, w_k, w_v, state_out):
    with ExitStack() as ctx:
        st = Stage(nc, sem, ctx, tag)
        front = Normed(st, x, ident)
        wk, wv = st.sb("wk", [P, DK, WL]), st.sb("wv", [P, DK, WL])
        low = st.sb("low", [P, 2, BANK])
        phi = st.sb("phi", [P, 2, WL])
        phi_sum = st.sb("phi_sum", [P, WL])
        x_kept = st.sb("x_kept", [P, 2, TPC, D])
        ones = st.sb("ones", [P, P])
        product = st.sb("product", [P, PAIRS, D])
        product_t = st.sb("product_t", [P, PAIRS, DK, P])
        wide = st.sb("wide", [P, 2, PAIRS, P])
        k_ps = st.ps("k_ps", [P, 2, BANK])
        product_ps = st.ps("product_ps", [P, 4, 2, D])
        w_loaded, ones_set = st.sem("w_loaded"), st.sem("ones_set")
        x_copied = st.sem("x_copied")
        k_ready, low_ready, exp_ready = st.sem("k_ready"), st.sem("low_ready"), st.sem("exp_ready")
        phi_ready = st.sem("phi_ready")
        phi_added = st.sem("phi_added")
        products = st.sem("products")
        product_copied, turned, turned_copied = st.sem("product_copied"), st.sem("turned"), st.sem("turned_copied")
        sum_ready, state_ready = st.sem("sum_ready"), st.sem("state_ready")
        wide_set, stored = st.sem("wide_set"), st.sem("stored")
        HALVES = WL // BANK
        block = ctx.enter_context(nc.Block())

        @block.sync
        def _(sp):
            begin_at_one(sp, *front.from_one)

            def load_weights():
                sp.dma_start(wk[:, :, :], w_k.rearrange("(k p) n -> p k n", p=P)).then_inc(w_loaded, DMA)
                sp.dma_start(wv[:, :, :], w_v.rearrange("(k p) n -> p k n", p=P)).then_inc(w_loaded, DMA)

            def work(n, load_later):
                sp.wait_ge(front.normed_ready, n.past(TPC, TPC))
                load_later()

            two_ahead(sp, lambda n: front.load(sp, n), work, load_weights)
            sp.wait_ge(wide_set, 1 + 4 * 4)
            sp.dma_start(state_out.rearrange("i p a c -> p i a c"), wide[:, :, :, :]).then_inc(stored, DMA)
            sp.wait_ge(stored, DMA)

        @block.gpsimd
        def _(pool):
            front.start_power(pool)
            pool.memset(ones[:, :], 1.0).then_inc(ones_set, 1)
            pool.wait_ge(ones_set, 1)
            pool.memset(phi_sum[:, :], 0.0).then_inc(phi_added, 2)
            pool.wait_ge(phi_added, 2)
            pool.memset(wide[:, :, :, :], 0.0).then_inc(wide_set, 1)
            pool.wait_ge(wide_set, 1)

            def work(n, ahead_next):
                for t in range(TPC):
                    pool.wait_ge(phi_ready, n.at(TPC * HALVES, HALVES * t + HALVES + 2))
                    pool.tensor_tensor(phi_sum[:, :], phi_sum[:, :], phi[:, t % 2, :], ALU.add).then_inc(phi_added, 1)
                    pool.wait_ge(phi_added, n.at(TPC, t + 3))
                    if t == 0:
                        ahead_next()

            each_chunk(pool, lambda n: front.power(pool, n), work)

        @block.tensor
        def _(pe):
            def work(n, ahead_next):
                xt = front.xt[:, n.parity]
                pe.wait_ge(front.xt_ready, n.past(DK, DK))
                for t in range(TPC):
                    if t == 3:
                        ahead_next()
                    for f in range(HALVES):
                        pe.wait_ge(phi_ready, n.at(TPC * HALVES, HALVES * t + f + 1))
                        for k in range(DK):
                            done = pe.matmul(k_ps[:, f, :], xt[:, k, t * P:(t + 1) * P], wk[:, k, f * BANK:(f + 1) * BANK],
                                             start=k == 0, stop=k == DK - 1)
                        done.then_inc(k_ready, 1)
                        if t:
                            multiply(n, t - 1, f)
                for f in range(HALVES):
                    multiply(n, TPC - 1, f)

            def multiply(n, t, f):
                pe.wait_ge(phi_ready, n.at(TPC * HALVES, HALVES * t + f + 3))
                pe.wait_ge(x_copied, n.at(1, 2))
                for a in range(4 * f, 4 * f + 4):
                    done = pe.matmul(product_ps[:, a // 2, a % 2, :], phi[:, t % 2, a * P:(a + 1) * P],
                                     x_kept[:, n.parity, t, :], start=False, stop=False, skip_group_check=True)
                if f == HALVES - 1:
                    done.then_inc(products, 1)

            def start_sums():
                pe.wait_ge(wide_set, 1)
                pe.wait_ge(ones_set, 1)
                for b in range(4):
                    pe.matmul(product_ps[:, b, :, :].rearrange("p a c -> p (a c)"), ones[:, :],
                              wide[:, 0, 0:4, :].rearrange("p a c -> p (a c)"), start=True, stop=False,
                              skip_group_check=True)
                pe.wait_ge(w_loaded, 2 * DMA)

            each_chunk(pe, lambda n: front.turn(pe, n), work, ready=start_sums)
            for b in range(4):
                done = pe.matmul(product_ps[:, b, :, :].rearrange("p a c -> p (a c)"), ones[:, :],
                                 wide[:, 0, 0:4, :].rearrange("p a c -> p (a c)"), start=False, stop=True,
                                 skip_group_check=True)
            done.then_inc(products, 1)
            pe.wait_ge(phi_added, 2 + CHUNKS * TPC)
            for a in range(PAIRS):
                done = pe.matmul(k_ps[:, a // 4, a % 4 * P:(a % 4 + 1) * P], phi_sum[:, a * P:(a + 1) * P], ones[:, :],
                                 start=True, stop=True)
            done.then_inc(sum_ready, 1)
            for a in range(PAIRS):
                pe.wait_ge(product_copied, a // 2 + 1)
                if a >= 4:
                    pe.wait_ge(turned_copied, a // 2 - 1)
                for k in range(DK):
                    done = pe.transpose(front.turned_ps[:, a // 2 % 2, (2 * (a % 2) + k) * P:(2 * (a % 2) + k + 1) * P],
                                        product[:, a, k * P:(k + 1) * P], ident[:, :])
                if a % 2:
                    done.then_inc(turned, 1)
            pe.wait_ge(product_copied, 4)
            pe.wait_ge(turned_copied, 4)
            for a in range(PAIRS):
                for k in range(DK):
                    done = pe.matmul(product_ps[:, a // 4, :, :].rearrange("p a c -> p (a c)")[:, a % 4 * P:(a % 4 + 1) * P],
                                     wv[:, k, a * P:(a + 1) * P], product_t[:, a, k, :], start=k == 0, stop=k == DK - 1)
                if a % 4 == 3:
                    done.then_inc(state_ready, 1)

        @block.scalar
        def _(act):
            act.sem_inc(products, 2)
            act.sem_inc(x_copied, 1)

            def copy(n):
                front.copy(act, n)
                act.wait_ge(front.normed_ready, n.past(TPC, TPC))
                act.wait_ge(front.turned_ready, n.past(DK, DK))
                nc.scalar.copy(x_kept[:, n.parity], front.normed[:, :, :]).then_inc(x_copied, 1)

            def work(n, ahead_next):
                for t in range(TPC):
                    for f in range(HALVES):
                        act.wait_ge(low_ready, n.at(TPC * HALVES, HALVES * t + f + 1))
                        nc.scalar.activation(low[:, f, :], low[:, f, :], ACT.Exp).then_inc(exp_ready, 1)
                    if t == TPC - 2:
                        ahead_next()

            each_chunk(act, copy, work)
            for b in range(4):
                act.wait_ge(turned, b + 1)
                nc.scalar.copy(product_t[:, 2 * b:2 * b + 2, :, :].rearrange("p a k c -> p (a k c)"),
                               front.turned_ps[:, b % 2, :]).then_inc(turned_copied, 1)

        @block.vector
        def _(dve):
            dve.sem_inc(phi_ready, 2)

            def work(n, ahead_next):
                for t in range(TPC):
                    for f in range(HALVES):
                        dve.wait_ge(k_ready, n.at(TPC * HALVES, HALVES * t + f + 1))
                        nc.vector.tensor_scalar(low[:, f, :], k_ps[:, f, :], 0.0, None, ALU.min).then_inc(low_ready, 1)
                    dve.wait_ge(products, n.at(TPC, t + 1))
                    dve.wait_ge(phi_added, n.at(TPC, t + 1))
                    for f in range(HALVES):
                        dve.wait_ge(exp_ready, n.at(TPC * HALVES, HALVES * t + f + 1))
                        nc.vector.scalar_tensor_tensor(phi[:, t % 2, f * BANK:(f + 1) * BANK], k_ps[:, f, :], 0.0,
                                                       low[:, f, :], ALU.max, ALU.add).then_inc(phi_ready, 1)
                    if t == 1:
                        dve.wait_ge(x_copied, n.at(1, 2))
                        ahead_next()

            each_chunk(dve, lambda n: front.normalise(dve, n), work)
            dve.wait_ge(products, 3 + CHUNKS * TPC)
            for b in range(4):
                nc.vector.tensor_copy(product[:, 2 * b:2 * b + 2, :], product_ps[:, b, :, :]).then_inc(product_copied, 1)
            dve.wait_ge(wide_set, 1)
            for i, ready in ((1, sum_ready), (0, state_ready)):
                for b in range(2):
                    dve.wait_ge(ready, b + 1 if i == 0 else 1)
                    source = product_ps[:, b, :, :].rearrange("p a c -> p (a c)") if i == 0 else k_ps[:, b, :]
                    for h in range(2):
                        block_of = slice(h * EL, (h + 1) * EL)
                        nc.vector.tensor_copy(wide[block_of, i, 4 * b:4 * b + 4, block_of],
                                              source.rearrange("p (a c) -> p a c", a=4)[block_of, :, block_of]
                                              ).then_inc(wide_set, 2)


def linear_output(nc, sem, tag, x, x_out, ident, w_q, state_in, w_out, bias):
    QUADRANT = P // 4
    with ExitStack() as ctx:
        st = Stage(nc, sem, ctx, tag)
        front = Normed(st, x, ident)
        wq = st.sb("wq", [P, DK, WL])
        wo = st.sb("wo", [P, PAIRS, D])
        state = st.sb("state", [P, 2, PAIRS, P])
        state_wo = st.sb("state_wo", [P, PAIRS, D])
        z_columns = st.sb("z_columns", [P, PAIRS, QUADRANT])
        spread = st.sb("spread", [P, PAIRS, P])
        bias_all = st.sb("bias_all", [P, 2 * D])
        low = st.sb("low", [P, 2, CHUNK])
        phi = st.sb("phi", [P, 2, PAIRS, CHUNK])
        z, over = st.sb("z", [P, CHUNK]), st.sb("over", [P, CHUNK])
        y = st.sb("y", [P, 2, TPC, D])
        eps = st.sb("eps", [P, 1])
        q_ps = st.ps("q_ps", [P, 2, BANK])
        spread_ps, z_ps = st.ps("spread_ps", [P, BANK]), st.ps("z_ps", [P, BANK])
        y_ps = st.ps("y_ps", [P, 2, BANK])
        w_loaded, constants_set, z_columns_set = st.sem("w_loaded"), st.sem("constants_set"), st.sem("z_columns_set")
        merged, state_wo_ready = st.sem("merged"), st.sem("state_wo_ready")
        q_ready, low_ready, exp_ready = st.sem("q_ready"), st.sem("low_ready"), st.sem("exp_ready")
        phi_ready = st.sem("phi_ready")
        z_ready, z_copied, over_ready = st.sem("z_ready"), st.sem("z_copied"), st.sem("over_ready")
        spread_ready, divided = st.sem("spread_ready"), st.sem("divided")
        y_ready, y_added, biased = st.sem("y_ready"), st.sem("y_added"), st.sem("biased")
        x_in_y = [st.sem("x_in_y0"), st.sem("x_in_y1")]
        y_stored = [st.sem("y_stored0"), st.sem("y_stored1")]
        state_loaded, wo_loaded = st.sem("state_loaded"), st.sem("wo_loaded")
        W_LOADS = 3 * DMA
        block = ctx.enter_context(nc.Block())

        def each_step(eng, step):
            with eng.Fori(0, CHUNKS // 2 - 1) as turn:
                for r in range(2):
                    step(Chunk(turn, r), True, True)
            step(Chunk(CHUNKS // 2 - 1, 0), True, False)
            step(Chunk(CHUNKS // 2 - 1, 1), False, False)

        @block.sync
        def _(sp):
            begin_at_one(sp, divided, y_added, *front.from_one)

            def load_weights():
                sp.dma_start(state[:, :, :, :], state_in.rearrange("i p a c -> p i a c")).then_inc(state_loaded, DMA)
                sp.dma_start(wo[:, :, :], w_out.rearrange("(k p) n -> p k n", p=P)).then_inc(wo_loaded, DMA)
                sp.dma_start(wq[:, :, :], w_q.rearrange("(k p) n -> p k n", p=P)).then_inc(w_loaded, DMA)
                for i in range(2):
                    sp.dma_start(bias_all[:, i * D:(i + 1) * D], bias.partition_broadcast(P)).then_inc(w_loaded, DMA)

            def load(n, normed=True, residual=True):
                if normed:
                    front.load(sp, n)
                if residual:
                    sp.dma_start(y[:, n.parity], by_chunk(x)[n.index]).then_inc(x_in_y[n.parity], DMA)

            def work(n, load_later):
                sp.wait_ge(front.normed_ready, n.past(TPC, TPC))
                load_later(residual=False)
                sp.wait_ge(y_added, n.past(2, 2))
                sp.dma_start(by_chunk(x_out)[n.index], y[:, n.parity]).then_inc(y_stored[n.parity], DMA)
                sp.wait_ge(y_stored[n.parity], n.turn * DMA + (n.r // 2 + 1) * DMA)
                load_later(normed=False)

            two_ahead(sp, load, work, load_weights)
            for b in range(2):
                sp.wait_ge(y_stored[b], CHUNKS // 2 * DMA)

        @block.gpsimd
        def _(pool):
            front.start_power(pool)
            pool.memset(eps[:, :], Z_EPS).then_inc(constants_set, 1)
            pool.wait_ge(constants_set, 1)
            pool.memset(z_columns[:, :, :], 0.0).then_inc(constants_set, 1)
            pool.wait_ge(constants_set, 2)
            pool.memset(spread[:, :, :], 0.0).then_inc(constants_set, 1)
            pool.wait_ge(constants_set, 3)
            for a in range(PAIRS):
                for half in range(2):
                    cut = spread[:, a, half * EL:(half + 1) * EL]
                    pool.affine_select(out=cut, in_=cut, compare_op=ALU.not_equal, fill=1.0,
                                       base=-(a % 4 * QUADRANT + a // 4 * 2 + half), pattern=[[0, EL]],
                                       channel_multiplier=1).then_inc(constants_set, 1)
            pool.wait_ge(constants_set, 3 + 2 * PAIRS)

            def step(n, _, two_more):
                pool.wait_ge(x_in_y[n.parity], n.turn * DMA + (n.r // 2 + 1) * DMA)
                for i in range(2):
                    flat = y[:, n.parity, 2 * i:2 * i + 2, :].rearrange("p t d -> p (t d)")
                    pool.tensor_tensor(flat, flat, bias_all[:, :], ALU.add).then_inc(biased, 1)
                    pool.wait_ge(biased, n.at(2, i + 1))
                if two_more:
                    front.power(pool, n.next().next())

            for r in range(2):
                front.power(pool, Chunk(0, r))
            pool.wait_ge(w_loaded, W_LOADS)
            each_step(pool, step)

        @block.tensor
        def _(pe):
            def query(n, a):
                pe.wait_ge(phi_ready, n.at(PAIRS, a + 1))
                for k in range(DK):
                    done = pe.matmul(q_ps[:, a % 2, :], wq[:, k, a * P:(a + 1) * P], front.xt[:, n.parity, k, :],
                                     start=k == 0, stop=k == DK - 1)
                done.then_inc(q_ready, 1)

            def z_of(n, q):
                for p in range(4):
                    a = 4 * q + p
                    pe.wait_ge(phi_ready, n.at(PAIRS, a + 3))
                    done = pe.matmul(z_ps[p * QUADRANT:(p + 1) * QUADRANT, :], z_columns[:, a, :], phi[:, n.parity, a, :],
                                     start=q == 0, stop=q == PAIRS // 4 - 1, tile_position=(0, p * QUADRANT))
                if q == PAIRS // 4 - 1:
                    done.then_inc(z_ready, 1)

            def output(n, i):
                for j in range(2):
                    t = 2 * i + j
                    for a in range(PAIRS):
                        done = pe.matmul(y_ps[:, i, j * D:(j + 1) * D], phi[:, n.parity, a, t * P:(t + 1) * P],
                                         state_wo[:, a, :], start=a == 0, stop=a == PAIRS - 1)
                done.then_inc(y_ready, 1)

            def step(n, more, two_more):
                pe.wait_ge(over_ready, n.at(1, 1))
                if more:
                    pe.wait_ge(front.xt_ready, n.next().past(DK, DK))
                for a in range(PAIRS):
                    pe.wait_ge(divided, n.past(PAIRS, a))
                    pe.matmul(spread_ps[:, :], spread[:, a, :], over[:, :], start=True, stop=True).then_inc(spread_ready, 1)
                    if more:
                        query(n.next(), a)
                        if a == PAIRS // 2 + 1:
                            z_of(n.next(), 0)
                pe.wait_ge(divided, n.past(PAIRS, PAIRS))
                pe.wait_ge(y_added, n.past(2, 0))
                output(n, 0)
                if more:
                    z_of(n.next(), 1)
                if two_more:
                    front.turn(pe, n.next().next())
                output(n, 1)

            pe.wait_ge(state_loaded, DMA)
            pe.wait_ge(wo_loaded, DMA)
            for i in range(2):
                if i:
                    pe.wait_ge(state_wo_ready, 2)
                for a in range(4):
                    done = pe.matmul(y_ps[:, a // 2, a % 2 * D:(a % 2 + 1) * D], state[:, 0, 4 * i + a, :], wo[:, 4 * i + a, :],
                                     start=True, stop=True)
                done.then_inc(merged, 1)
            pe.wait_ge(state_wo_ready, 4)
            pe.wait_ge(z_columns_set, 4)
            pe.wait_ge(constants_set, 3 + 2 * PAIRS)
            pe.wait_ge(w_loaded, W_LOADS)
            first = Chunk(0, 0)
            front.turn(pe, first)
            pe.wait_ge(front.xt_ready, first.past(DK, DK))
            for a in range(PAIRS):
                query(first, a)
                if a == PAIRS // 2:
                    z_of(first, 0)
            z_of(first, 1)
            front.turn(pe, first.next())
            each_step(pe, step)

        @block.scalar
        def _(act):
            def exponentials(n):
                for a in range(PAIRS):
                    act.wait_ge(low_ready, n.at(PAIRS, a + 1))
                    nc.scalar.activation(low[:, a % 2, :], low[:, a % 2, :], ACT.Exp).then_inc(exp_ready, 1)
                act.wait_ge(z_ready, n.at(1, 1))
                nc.scalar.activation(z[:, :], z_ps[:, :], ACT.Identity, bias=eps[:, 0:1]).then_inc(z_copied, 1)

            def step(n, more, two_more):
                if more:
                    exponentials(n.next())
                if two_more:
                    front.copy(act, n.next().next())

            act.wait_ge(constants_set, 1)
            front.copy(act, Chunk(0, 0))
            exponentials(Chunk(0, 0))
            front.copy(act, Chunk(0, 1))
            each_step(act, step)

        @block.vector
        def _(dve):
            def low_of(n, a):
                dve.wait_ge(q_ready, n.at(PAIRS, a + 1))
                nc.vector.tensor_scalar(low[:, a % 2, :], q_ps[:, a % 2, :], 0.0, None, ALU.min).then_inc(low_ready, 1)

            def phi_of(n, a):
                dve.wait_ge(exp_ready, n.at(PAIRS, a + 1))
                nc.vector.scalar_tensor_tensor(phi[:, n.parity, a, :], q_ps[:, a % 2, :], 0.0, low[:, a % 2, :],
                                               ALU.max, ALU.add).then_inc(phi_ready, 1)

            def one_over_z(n):
                dve.wait_ge(z_copied, n.at(1, 1))
                nc.vector.reciprocal(over[:, :], z[:, :]).then_inc(over_ready, 1)

            def step(n, more, two_more):
                for a in range(PAIRS):
                    dve.wait_ge(spread_ready, n.at(PAIRS, a + 1))
                    nc.vector.tensor_tensor(phi[:, n.parity, a, :], spread_ps[:, :], phi[:, n.parity, a, :],
                                            ALU.mult).then_inc(divided, 1)
                    if more:
                        if a:
                            phi_of(n.next(), a - 1)
                        low_of(n.next(), a)
                if more:
                    phi_of(n.next(), PAIRS - 1)
                if two_more:
                    front.normalise(dve, n.next().next())
                if more:
                    one_over_z(n.next())
                dve.wait_ge(biased, n.at(2, 2))
                for i in range(2):
                    dve.wait_ge(y_ready, n.at(2, i + 1))
                    flat = y[:, n.parity, 2 * i:2 * i + 2, :].rearrange("p t d -> p (t d)")
                    nc.vector.tensor_tensor(flat, y_ps[:, i, :], flat, ALU.add).then_inc(y_added, 1)

            dve.sem_inc(phi_ready, 2)
            front.normalise(dve, Chunk(0, 0))
            dve.wait_ge(state_loaded, DMA)
            dve.wait_ge(constants_set, 2)
            for q in range(2):
                for half in range(2):
                    rows = slice(half * EL, (half + 1) * EL)
                    nc.vector.tensor_copy(z_columns[rows, 4 * q:4 * q + 4, 2 * q + half:2 * q + half + 1],
                                          state[rows, 1, 4 * q:4 * q + 4, half * EL:half * EL + 1]).then_inc(z_columns_set, 1)
            for i in range(2):
                dve.wait_ge(merged, i + 1)
                for j in range(2):
                    nc.vector.tensor_copy(state_wo[:, 4 * i + 2 * j:4 * i + 2 * j + 2, :].rearrange("p a d -> p (a d)"),
                                          y_ps[:, j, :]).then_inc(state_wo_ready, 1)
            for a in range(PAIRS):
                low_of(Chunk(0, 0), a)
                phi_of(Chunk(0, 0), a)
            front.normalise(dve, Chunk(0, 1))
            one_over_z(Chunk(0, 0))
            each_step(dve, step)


LATENT = 64
SHARE = 9
TURN = 2 * TPC


class Tile:

    def __init__(self, turn, r):
        self.turn, self.r = turn, r

    def at(self, c):
        return self.turn * TURN + (self.r + c)

    def steps(self, per_tile, c):
        return self.turn * (TURN * per_tile) + (self.r * per_tile + c)

    @property
    def slot(self):
        return self.r % 2

    @property
    def chunk(self):
        return Chunk(self.turn, self.r // TPC)


def each_tile(eng, steps, ahead, ready=nothing):
    def body(turn, r, present=lambda r: True, more=True):
        for t, prepare in ahead:
            if more and r % TPC == t:
                prepare(Chunk(turn, r // TPC + 1))
        for lag, step in steps:
            if present(r - lag):
                step(Tile(turn, r - lag))

    for _, prepare in ahead:
        prepare(Chunk(0, 0))
    ready()
    for r in range(TPC):
        body(0, r, present=lambda r: r >= 0)
    with eng.Fori(0, CHUNKS // 2 - 1) as turn:
        for r in range(TPC, TPC + TURN):
            body(turn, r)
    for r in range(TPC, TURN + max(lag for lag, _ in steps)):
        body(CHUNKS // 2 - 1, r, present=lambda r: r < TURN, more=False)


def attention_over_heads(nc, sem, tag, x, x_out, ident, weights, rotary):
    Wq, bq, Wdown, bdown, Wup, bup, Wout, bout = weights
    with ExitStack() as ctx:
        st = Stage(nc, sem, ctx, tag)
        front = Normed(st, x, ident)
        wq, w_down = st.sb("wq", [P, DK, D]), st.sb("w_down", [P, DK, LATENT])
        w_up = st.sb("w_up", [LATENT + 1, 2, D])
        w_out = st.sb("w_out", [P, DK, D])
        b_rows, ones = st.sb("b_rows", [1, 2, D]), st.sb("ones", [1, P])
        b_down = st.sb("b_down", [LATENT, 1])
        cos_sin = st.sb("cos_sin", [P, 2, TILES, HD])
        latent = st.sb("latent", [LATENT + 1, 2, CHUNK])
        rot_a, rot_b = st.sb("rot_a", [P, 2 * D]), st.sb("rot_b", [P, 2 * D])
        qk = st.sb("qk", [P, 2, 2 * D])
        v_t = st.sb("v_t", [P, 4, H, HD])
        score_terms = st.sb("score_terms", [P, 2, H, H, HD])
        scores = st.sb("scores", [P, 2, H, H])
        exps = st.sb("exps", [P, 2, H, H])
        probs = st.sb("probs", [P, 2, H, H])
        out_terms = st.sb("out_terms", [P, 4, H, H, HD])
        row_max, row_sum = st.sb("row_max", [P, H]), st.sb("row_sum", [P, H])
        over = st.sb("over", [P, H])
        attended_t = st.sb("attended_t", [P, 2, DK, P])
        y = st.sb("y", [P, 2, TPC, D])
        qk_ps = st.ps("qk_ps", [P, 2, BANK])
        v_ps, latent_ps = st.ps("v_ps", [P, D]), st.ps("latent_ps", [LATENT, CHUNK])
        back_ps, y_ps = st.ps("back_ps", [P, DK, P]), st.ps("y_ps", [P, D])
        w_loaded, ones_set = st.sem("w_loaded"), st.sem("ones_set")
        latent_ready, latent_read = st.sem("latent_ready"), st.sem("latent_read")
        qk_ready, v_ready, v_copied = st.sem("qk_ready"), st.sem("v_ready"), st.sem("v_copied")
        products_made = st.sem("products_made")
        qk_rotated = st.sem("qk_rotated")
        terms_made, scores_made = st.sem("terms_made"), st.sem("scores_made")
        max_made, shifted, exp_made = st.sem("max_made"), st.sem("shifted"), st.sem("exp_made")
        sum_made, over_made = st.sem("sum_made"), st.sem("over_made")
        probs_made = st.sem("probs_made")
        out_terms_made = [st.sem("out_terms_made0"), st.sem("out_terms_made1")]
        back_ready, back_copied = st.sem("back_ready"), st.sem("back_copied")
        y_ready, y_added = st.sem("y_ready"), st.sem("y_added")
        x_in_y = [st.sem("x_in_y0"), st.sem("x_in_y1")]
        y_stored = [st.sem("y_stored0"), st.sem("y_stored1")]
        loads = [(wq[:, :, :], Wq.rearrange("(k p) n -> p k n", p=P)), (w_out[:, :, :], Wout.rearrange("(k p) n -> p k n", p=P)),
                 (w_down[:, :, :], Wdown.rearrange("(k p) n -> p k n", p=P)),
                 (b_down[:, :], bdown.rearrange("(p o) -> p o", o=1)),
                 (b_rows[:, 0, :], bq.rearrange("(o n) -> o n", o=1)), (b_rows[:, 1, :], bout.rearrange("(o n) -> o n", o=1)),
                 (cos_sin[:, 0], rotary[0]), (cos_sin[:, 1], rotary[1])]
        for i in range(2):
            loads.append((w_up[0:LATENT, i, :].rearrange("p (h c) -> p h c", c=HD),
                          Wup.rearrange("p (h two c) -> two p h c", two=2, c=HD)[i]))
            loads.append((w_up[LATENT:LATENT + 1, i, :].rearrange("p (h c) -> p h c", c=HD),
                          bup.rearrange("(o h two c) -> two o h c", o=1, two=2, c=HD)[i]))
        W_LOADS = len(loads) * DMA
        block = ctx.enter_context(nc.Block())

        @block.sync
        def _(sp):
            begin_at_one(sp, latent_read, *front.from_one)

            def load_weights():
                for dst, src in loads:
                    sp.dma_start(dst, src).then_inc(w_loaded, DMA)

            def load(n, normed=True, residual=True):
                if normed:
                    front.load(sp, n)
                if residual:
                    sp.dma_start(y[:, n.parity], by_chunk(x)[n.index]).then_inc(x_in_y[n.parity], DMA)

            def work(n, load_later):
                sp.wait_ge(front.normed_ready, n.past(TPC, TPC))
                load_later(residual=False)
                sp.wait_ge(y_added, n.at(TPC, TPC + 2))
                sp.dma_start(by_chunk(x_out)[n.index], y[:, n.parity]).then_inc(y_stored[n.parity], DMA)
                sp.wait_ge(y_stored[n.parity], n.turn * DMA + (n.r // 2 + 1) * DMA)
                load_later(normed=False)

            two_ahead(sp, load, work, load_weights)
            for b in range(2):
                sp.wait_ge(y_stored[b], CHUNKS // 2 * DMA)

        def multiply(eng, i, half):
            heads = (slice(0, SHARE), slice(SHARE, H))[half]
            shape = [P, heads.stop - heads.start, H, HD]
            eng.wait_ge(v_copied, i.at(3))
            eng.wait_ge(back_ready, i.at(1))
            p = probs[:, i.slot, :, heads].rearrange("p h (g o) -> p g h o", o=1).broadcast_to(shape)
            v = v_t[:, i.r % 4, heads, :].rearrange("p g (o d) -> p g o d", o=1).broadcast_to(shape)
            eng.tensor_tensor(out_terms[:, i.r % 4, heads], p, v, ALU.mult).then_inc(out_terms_made[half], 1)

        @block.gpsimd
        def _(pool):
            front.start_power(pool)
            pool.memset(ones[:, :], 1.0).then_inc(ones_set, 1)
            pool.wait_ge(ones_set, 1)
            pool.memset(latent[LATENT:LATENT + 1, :, :], 1.0).then_inc(ones_set, 1)
            pool.wait_ge(ones_set, 2)
            pool.sem_inc(terms_made, 2)
            pool.sem_inc(out_terms_made[1], 2)

            def multiply_qk(i):
                pool.wait_ge(qk_rotated, i.at(3))
                pool.wait_ge(scores_made, i.at(1))
                q = qk[:, i.slot, 0:D].rearrange("p (h o d) -> p h o d", o=1, d=HD).broadcast_to([P, H, H, HD])
                k = qk[:, i.slot, D:2 * D].rearrange("p (o g d) -> p o g d", o=1, d=HD).broadcast_to([P, H, H, HD])
                pool.tensor_tensor(score_terms[:, i.slot], q, k, ALU.mult).then_inc(terms_made, 1)
                pool.wait_ge(terms_made, i.at(3))

            def multiply_v(i):
                pool.wait_ge(probs_made, i.at(3))
                multiply(pool, i, 1)
                pool.wait_ge(out_terms_made[1], i.at(3))

            each_tile(pool, [(0, multiply_qk), (2, multiply_v)], [(0, lambda n: front.power(pool, n))])

        @block.tensor
        def _(pe):
            pe.wait_ge(ones_set, 2)
            pe.sem_inc(back_ready, 4)

            def make_latent(n):
                pe.wait_ge(front.xt_ready, n.past(DK, DK))
                pe.wait_ge(latent_read, n.past(1, 0))
                for k in range(DK):
                    done = pe.matmul(latent_ps[:, :], w_down[:, k, :], front.xt[:, n.parity, k, :],
                                     start=k == 0, stop=k == DK - 1)
                done.then_inc(latent_ready, 1)

            def project_tile(i):
                n, tokens = i.chunk, slice(i.r % TPC * P, (i.r % TPC + 1) * P)
                if i.r % TPC == 0:
                    make_latent(n)
                pe.wait_ge(qk_rotated, i.at(1))
                for k in range(DK):
                    pe.matmul(qk_ps[:, i.slot, 0:D], front.xt[:, n.parity, k, tokens], wq[:, k, :], start=k == 0, stop=False)
                pe.matmul(qk_ps[:, i.slot, 0:D], ones[:, :], b_rows[:, 0, :], start=False, stop=True)
                pe.wait_ge(latent_read, n.past(1, 1))
                pe.matmul(qk_ps[:, i.slot, D:2 * D], latent[:, n.parity, tokens], w_up[:, 0, :],
                          start=True, stop=True).then_inc(qk_ready, 1)
                pe.wait_ge(v_copied, i.at(2))
                pe.matmul(v_ps[:, :], latent[:, n.parity, tokens], w_up[:, 1, :],
                          start=True, stop=True).then_inc(v_ready, 1)

            def turn_back(i):
                pe.wait_ge(out_terms_made[0], i.at(1))
                pe.wait_ge(out_terms_made[1], i.at(3))
                pe.wait_ge(back_copied, i.at(2))
                for k in range(DK):
                    for g in range(H):
                        done = pe.matmul(back_ps[:, k, :], out_terms[:, i.r % 4, g, k * H // 2:(k + 1) * H // 2, :]
                                         .rearrange("p h d -> p (h d)"), ident[:, :], start=g == 0, stop=g == H - 1)
                done.then_inc(back_ready, 1)

            def project_out(i):
                pe.wait_ge(back_copied, i.at(3))
                pe.wait_ge(y_added, i.at(2))
                for k in range(DK):
                    pe.matmul(y_ps[:, :], attended_t[:, i.slot, k, :], w_out[:, k, :], start=k == 0, stop=False)
                pe.matmul(y_ps[:, :], ones[:, :], b_rows[:, 1, :], start=False, stop=True).then_inc(y_ready, 1)

            each_tile(pe, [(0, project_tile), (4, project_out), (3, turn_back)], [(3, lambda n: front.turn(pe, n))],
                      lambda: pe.wait_ge(w_loaded, W_LOADS))

        @block.scalar
        def _(act):
            act.sem_inc(v_copied, 2)
            act.sem_inc(back_copied, 2)

            def copy_latent(n):
                act.wait_ge(latent_ready, n.at(1, 1))
                nc.scalar.activation(latent[0:LATENT, n.parity, :], latent_ps[:, :], ACT.Identity,
                                     bias=b_down[:, 0:1]).then_inc(latent_read, 1)

            def copy_v(i):
                if i.r % TPC == 0:
                    copy_latent(i.chunk)
                act.wait_ge(v_ready, i.at(1))
                act.wait_ge(back_ready, i.at(1))
                nc.scalar.copy(v_t[:, i.r % 4, :, :].rearrange("p g d -> p (g d)"), v_ps[:, :]).then_inc(v_copied, 1)

            def exponentials(i):
                act.wait_ge(shifted, i.at(1))
                act.wait_ge(probs_made, i.at(1))
                nc.scalar.activation(exps[:, i.slot, :, :], scores[:, i.slot, :, :], ACT.Exp,
                                     scale=HD ** -0.5).then_inc(exp_made, 1)

            def copy_back(i):
                act.wait_ge(back_ready, i.at(5))
                nc.scalar.copy(attended_t[:, i.slot, :, :], back_ps[:, :, :]).then_inc(back_copied, 1)

            each_tile(act, [(0, copy_v), (1, exponentials), (3, copy_back)], [(3, lambda n: front.copy(act, n))],
                      lambda: act.wait_ge(w_loaded, W_LOADS))

        @block.vector
        def _(dve):
            dve.sem_inc(qk_rotated, 2)
            dve.sem_inc(scores_made, 2)
            dve.sem_inc(probs_made, 2)
            dve.sem_inc(y_added, 2)

            def rotate(i):
                def halves(t):
                    return t.rearrange("p (h two j) -> p h two j", two=2, j=HD // 2)

                dve.wait_ge(qk_ready, i.at(1))
                dve.wait_ge(qk_rotated, i.at(2))
                both = qk_ps[:, i.slot, :]
                tile = bass.ds(i.turn * TURN + i.r, 1)
                nc.vector.tensor_tensor(rot_a[:, :].rearrange("p (h d) -> p h d", d=HD),
                                        both.rearrange("p (h d) -> p h d", d=HD),
                                        cos_sin[:, 0, tile, :].broadcast_to([P, 2 * H, HD]),
                                        ALU.mult).then_inc(products_made, 1)
                for half in range(2):
                    nc.vector.tensor_tensor(halves(rot_b[:, :])[:, :, half, :], halves(both)[:, :, 1 - half, :],
                                            cos_sin[:, 1, tile, half * HD // 2:(half + 1) * HD // 2]
                                            .broadcast_to([P, 2 * H, HD // 2]),
                                            ALU.mult).then_inc(products_made, 1)
                dve.wait_ge(products_made, i.steps(3, 3))
                dve.wait_ge(terms_made, i.at(1))
                nc.vector.tensor_tensor(qk[:, i.slot, :], rot_a[:, :], rot_b[:, :], ALU.add).then_inc(qk_rotated, 1)

            def shift_scores(i):
                dve.wait_ge(terms_made, i.at(3))
                nc.vector.tensor_reduce(scores[:, i.slot, :, :], score_terms[:, i.slot], AX.X, ALU.add).then_inc(scores_made, 1)
                dve.wait_ge(scores_made, i.at(3))
                nc.vector.tensor_reduce(row_max[:, :], scores[:, i.slot, :, :], AX.X, ALU.max).then_inc(max_made, 1)
                dve.wait_ge(max_made, i.at(1))
                nc.vector.tensor_tensor(scores[:, i.slot, :, :], scores[:, i.slot, :, :],
                                        row_max[:, :].rearrange("p (h o) -> p h o", o=1).broadcast_to([P, H, H]),
                                        ALU.subtract).then_inc(shifted, 1)

            def attend(i):
                dve.wait_ge(exp_made, i.at(1))
                nc.vector.tensor_reduce(row_sum[:, :], exps[:, i.slot, :, :], AX.X, ALU.add).then_inc(sum_made, 1)
                dve.wait_ge(sum_made, i.at(1))
                nc.vector.reciprocal(over[:, :], row_sum[:, :]).then_inc(over_made, 1)
                dve.wait_ge(over_made, i.at(1))
                dve.wait_ge(out_terms_made[1], i.at(1))
                nc.vector.tensor_tensor(probs[:, i.slot, :, :], exps[:, i.slot, :, :],
                                        over[:, :].rearrange("p (h o) -> p h o", o=1).broadcast_to([P, H, H]),
                                        ALU.mult).then_inc(probs_made, 1)
                dve.wait_ge(probs_made, i.at(3))
                multiply(dve, i, 0)

            def add_y(i):
                n, t = i.chunk, i.r % TPC
                dve.wait_ge(y_ready, i.at(1))
                if t == 0:
                    dve.wait_ge(x_in_y[n.parity], n.turn * DMA + (n.r // 2 + 1) * DMA)
                nc.vector.tensor_tensor(y[:, n.parity, t, :], y_ps[:, :], y[:, n.parity, t, :],
                                        ALU.add).then_inc(y_added, 1)

            each_tile(dve, [(0, rotate), (4, add_y), (2, attend), (1, shift_scores)],
                      [(0, lambda n: front.find_moments(dve, n)), (2, lambda n: front.finish_normalise(dve, n))],
                      lambda: dve.wait_ge(w_loaded, W_LOADS))


BF_STAGES, PAIRS_BF = 10, 512


def fold_butterflies(nc, sem, ctx, w_exp, b_exp, up_weights, up_bias, w_con_turned, down_weights,
                     dma_sems, w_up_out, bias_out, w_down_out):
    W = 2 * PAIRS_BF
    st = Stage(nc, sem, ctx, "fold")
    rows = [st.sb("rows0", [P, DK, W]), st.sb("rows1", [P, DK, W])]
    line = [st.sb("line0", [1, W]), st.sb("line1", [1, W])]
    product, line_product = st.sb("product", [P, DK, PAIRS_BF]), st.sb("line_product", [1, PAIRS_BF])
    pair_w = [st.sb("pair_w0", [P, PAIRS_BF, 2, 2]), st.sb("pair_w1", [P, PAIRS_BF, 2, 2])]
    last_bias = st.sb("last_bias", [1, W])
    rows_loaded, line_loaded, *pair_loaded, stored = dma_sems
    step = st.sem("step")

    def program(pool):
        done = [0]

        def chained(ins):
            done[0] += 1
            ins.then_inc(step, 1)
            pool.wait_ge(step, done[0])

        def load_pairs(n):
            weights = up_weights[n] if n < BF_STAGES else down_weights[2 * BF_STAGES - 1 - n]
            pool.dma_start(pair_w[n % 2][:, :, :, :].rearrange("p k i j -> p (k i j)"),
                           weights.rearrange("k i j -> (k i j)").partition_broadcast(P)).then_inc(pair_loaded[n % 2], DMA)

        def stage(src, dst, tmp, weights, stride, transposed):
            halves = [t.rearrange("p (n two s) -> p n two s", two=2, s=stride) for t in (src, dst)]
            t = tmp.rearrange("p (n s) -> p n s", s=stride)
            w = weights.rearrange("p (n s) i j -> p n s i j", s=stride)
            for i in range(2):
                for j in range(2):
                    wij = w[:, :, :, j, i] if transposed else w[:, :, :, i, j]
                    out = t if j else halves[1][:, :, i, :]
                    chained(pool.tensor_tensor(out, halves[0][:, :, j, :], wij, ALU.mult))
                chained(pool.tensor_tensor(halves[1][:, :, i, :], halves[1][:, :, i, :], t, ALU.add))

        pool.dma_start(rows[0][:, :, :], w_exp.rearrange("(k p) n -> p k n", p=P)).then_inc(rows_loaded, DMA)
        pool.dma_start(line[0][:, :], b_exp.rearrange("(o n) -> o n", o=1)).then_inc(line_loaded, DMA)
        pool.dma_start(last_bias[:, :], up_bias.rearrange("(o n) -> o n", o=1)).then_inc(line_loaded, DMA)
        load_pairs(0)
        load_pairs(1)
        pool.wait_ge(rows_loaded, DMA)
        pool.wait_ge(line_loaded, 2 * DMA)
        for n in range(2 * BF_STAGES):
            down = n >= BF_STAGES
            stride = 1 << (2 * BF_STAGES - 1 - n if down else n)
            if n == BF_STAGES:
                chained(pool.tensor_tensor(line[0][:, :], line[0][:, :], last_bias[:, :], ALU.add))
                pool.dma_start(w_up_out.rearrange("(k p) n -> p k n", p=P), rows[0][:, :, :]).then_inc(stored, DMA)
                pool.dma_start(bias_out.rearrange("(o n) -> o n", o=1), line[0][:, :]).then_inc(stored, DMA)
                pool.wait_ge(stored, 2 * DMA)
                pool.dma_start(rows[0][:, :, :], w_con_turned.rearrange("(k p) n -> p k n", p=P)).then_inc(rows_loaded, DMA)
                pool.wait_ge(rows_loaded, 2 * DMA)
            pool.wait_ge(pair_loaded[n % 2], (n // 2 + 1) * DMA)
            w = pair_w[n % 2][:, :, :, :]
            for k in range(DK):
                stage(rows[n % 2][:, k, :], rows[1 - n % 2][:, k, :], product[:, k, :], w, stride, down)
            if not down:
                stage(line[n % 2][:, :], line[1 - n % 2][:, :], line_product[:, :], w[0:1], stride, False)
            if n + 2 < 2 * BF_STAGES:
                load_pairs(n + 2)
        pool.dma_start(w_down_out.rearrange("(k p) n -> p k n", p=P), rows[0][:, :, :]).then_inc(stored, DMA)
        pool.wait_ge(stored, 3 * DMA)

    return program


HID0, HID1 = 1024, 768


def run_stage(nc, stage, *args, **kwargs):
    with ExitStack() as ctx:
        used = []

        def sem(name):
            used.append(ctx.enter_context(nc.semaphore(name)))
            return used[-1]

        stage(nc, sem, *args, **kwargs)
        with nc.Block() as block:
            @block.gpsimd
            def _(pool):
                for s in used:
                    pool.sem_clear(s)


def first_attention(nc, sem, ins, by_head, v_cols, heads_out, consts, w_con_t, folded):
    with ExitStack() as ctx:
        beside = fold_butterflies(nc, sem, ctx, ins["L0_ffn_W_exp"], ins["L0_ffn_b_exp"],
                                  ins["L0_ffn_up_weights"], ins["L0_ffn_up_bias"], w_con_t,
                                  ins["L0_ffn_down_weights"], *folded)
        attention(nc, sem, "a0", *by_head, v_cols, heads_out, consts, beside)


def program(nc, ins, out):
    with ExitStack() as ctx:
        def dram(name, shape, dt=F32):
            return nc.dram_tensor(name, shape, dt, kind="Internal").ap()

        ident_bf = ctx.enter_context(nc.sbuf_tensor("ident_bf", [P, P], BF16))
        ident = ctx.enter_context(nc.sbuf_tensor("ident", [P, P], F32))
        mask_first = ctx.enter_context(nc.sbuf_tensor("mask_first", [P, P], BF16))
        mask_second = ctx.enter_context(nc.sbuf_tensor("mask_second", [P, P], BF16))
        consts = (ident_bf, ident, mask_first, mask_second)

        wqkv_t, wo0_t = dram("wqkv_t", [D, 3 * D]), dram("wo0_t", [D, D])
        w1_t = {n: dram(f"w1_{n}_t", [D, D]) for n in "QKVO"}
        w_con_t, w_up0, bias0 = dram("w_con_t", [D, HID0]), dram("w_up0", [D, HID0]), dram("bias0", [HID0])
        w_down0_t, w_down0 = dram("w_down0_t", [D, HID0]), dram("w_down0", [HID0, D])
        w_gate1, w_up1, w_down1 = dram("w_gate1", [D, HID1]), dram("w_up1", [D, HID1]), dram("w_down1", [HID1, D])
        xs = [dram(f"x{i}", [S, D]) for i in range(7)]
        q_parts, k_parts = (dram(n, [PARTS, D, S], BF16) for n in ("q_parts", "k_parts"))
        v_cols = dram("v_cols", [H, P, TILES, VW])
        heads_out = dram("heads_out", [H, HD + 1, S])
        state = dram("state", [2, P, PAIRS, P])
        by_head = [t.rearrange("a (h d) s -> h a d s", d=HD) for t in (q_parts, k_parts)]

        fold_sems = [ctx.enter_context(nc.semaphore(f"fold_{n}"))
                     for n in ("rows_loaded", "line_loaded", "pair_loaded0", "pair_loaded1", "stored")]
        scale = 1.0 / 127.0
        run_stage(nc, set_constants, consts)
        run_stage(nc, turn_weights, "turn", ident, [
            (ins["L0_attn_a_W_qkv"], wqkv_t, None), (ins["L0_attn_a_W_o"], wo0_t, None),
            (ins["L0_ffn_W_con"], w_con_t, None)]
            + [(ins[f"L0_attn_b_W_{n}"], w1_t[n], None) for n in "QKVO"]
            + [(ins["L1_ffn_w_gate"], w_gate1, scale), (ins["L1_ffn_w_up"], w_up1, scale),
               (ins["L1_ffn_w_down"], w_down1, scale)])

        x0 = ins["L0_attn_a_x"].rearrange("b s d -> (b s) d")
        run_stage(nc, project, "p0", x0, ident, q_parts, k_parts, v_cols,
                [wqkv_t[:, i * D:(i + 1) * D] for i in range(3)], rotary=(ins["cos0"], ins["sin0"]))
        run_stage(nc, first_attention, ins, by_head, v_cols, heads_out, consts, w_con_t, (fold_sems, w_up0, bias0, w_down0_t))
        run_stage(nc, turn_weights, "turn2", ident, [(w_down0_t, w_down0, None)])
        run_stage(nc, merge_heads, "m0", x0, xs[0], heads_out, wo0_t)
        ffn0 = dict(hidden=HID0, w_in=w_up0, w_gate=None, w_down=w_down0, in_bias=bias0,
                    out_biases=(ins["L0_ffn_b_con"], ins["L0_ffn_down_bias"]))
        run_stage(nc, feed_forward, "f0", xs[0], xs[1], ident, **ffn0)

        run_stage(nc, project, "p1", xs[1], ident, q_parts, k_parts, v_cols, [w1_t[n] for n in "QKV"])
        run_stage(nc, attention, "a1", *by_head, v_cols, heads_out, consts)
        run_stage(nc, merge_heads, "m1", xs[1], xs[2], heads_out, w1_t["O"])
        run_stage(nc, feed_forward, "f1", xs[2], xs[3], ident, **ffn0)

        run_stage(nc, linear_state, "s2", xs[3], ident, ins["L1_attn_a_Wk"], ins["L1_attn_a_Wv"], state)
        run_stage(nc, linear_output, "o2", xs[3], xs[4], ident, ins["L1_attn_a_Wq"], state, ins["L1_attn_a_Wo"],
                      ins["L1_attn_a_bo"])
        ffn1 = dict(hidden=HID1, w_in=w_up1, w_gate=w_gate1, w_down=w_down1)
        run_stage(nc, feed_forward, "f2", xs[4], xs[5], ident, **ffn1)

        run_stage(nc, attention_over_heads, "a3", xs[5], xs[6], ident,
                  [ins[f"L1_attn_b_{n}"] for n in ("Wq", "bq", "Wdown", "bdown", "Wup", "bup", "Wout", "bout")],
                  (ins["cos1"], ins["sin1"]))
        run_stage(nc, feed_forward, "f3", xs[6], out.rearrange("b s d -> (b s) d"), ident, **ffn1)




def rotary_tables():
    import numpy as np

    theta = np.float32(10000.0) ** (np.arange(0, HD, 2, dtype=np.float32) / np.float32(HD))
    tokens = np.arange(S, dtype=np.float32)
    near = (tokens[:, None] / theta[None, :]).astype(np.float64)
    far = (tokens[:, None] * (np.float32(1.0) / theta)[None, :]).astype(np.float64)
    feature = np.arange(HD)
    sign_near, sign_far = np.where(feature % 2 == 0, -1.0, 1.0), np.where(feature < HD // 2, -1.0, 1.0)
    near, far = near[:, feature // 2], far[:, feature % (HD // 2)]

    def by_feature(t):
        return np.ascontiguousarray(np.tile(t, (1, P // HD)).T.astype(np.float32))

    def by_token(t):
        return np.ascontiguousarray(t.reshape(TILES, P, HD).transpose(1, 0, 2).astype(np.float32))

    return {"cos0": by_feature(np.cos(near)), "sin0": by_feature(np.sin(near) * sign_near),
            "cos1": by_token(np.cos(far)), "sin1": by_token(np.sin(far) * sign_far)}


_INS = [
    "L0_attn_a_x", "L0_attn_a_W_qkv", "L0_attn_a_W_o", "L0_attn_b_W_Q", "L0_attn_b_W_K", "L0_attn_b_W_V",
    "L0_attn_b_W_O", "L0_ffn_W_exp", "L0_ffn_b_exp", "L0_ffn_up_weights", "L0_ffn_up_bias", "L0_ffn_down_weights",
    "L0_ffn_W_con", "L0_ffn_b_con", "L0_ffn_down_bias", "L1_attn_a_Wq", "L1_attn_a_Wk", "L1_attn_a_Wv",
    "L1_attn_a_Wo", "L1_attn_a_bo", "L1_attn_b_Wq", "L1_attn_b_bq", "L1_attn_b_Wdown", "L1_attn_b_bdown",
    "L1_attn_b_Wup", "L1_attn_b_bup", "L1_attn_b_Wout", "L1_attn_b_bout", "L1_ffn_w_gate", "L1_ffn_w_up",
    "L1_ffn_w_down",
]


def kernel(**inputs):
    import concourse.bacc as bacc
    import numpy as np
    from concourse.bass_utils import run_bass_kernel_spmd

    nc = bacc.Bacc("TRN2", target_bir_lowering=False, num_devices=1)
    arrays, ins = {}, {}

    def give(name, a):
        arrays[f"in_{name}_dram"] = a
        ins[name] = nc.dram_tensor(f"in_{name}_dram", a.shape, mybir.dt.from_np(a.dtype), kind="ExternalInput").ap()

    for name in _INS:
        give(name, np.ascontiguousarray(inputs[name]))
    for name, table in rotary_tables().items():
        give(name, table)
    out = nc.dram_tensor("out_0_dram", (1, S, D), F32, kind="ExternalOutput").ap()
    program(nc, ins, out)
    r = run_bass_kernel_spmd(nc, [arrays], core_ids=[0])
    return r.results[0]["out_0_dram"]
```
